# Optimizing a Trainium2 kernel written in Bass

```python
import numpy as np
import jax
import jax.numpy as jnp

def _softmax(x, axis=-1):
    return jax.nn.softmax(x, axis=axis)

def _gelu(x):
    return jax.nn.gelu(x, approximate=True)

def _silu(x):
    return jax.nn.silu(x)

def _sigmoid(x):
    return jax.nn.sigmoid(x)

def _layernorm(x, axis=-1, eps=1e-05):
    m = jnp.mean(x, axis=axis, keepdims=True)
    v = jnp.var(x, axis=axis, keepdims=True)
    return (x - m) / jnp.sqrt(v + eps)

def _scatter_add(tgt, idx, src, axis=0):
    return tgt.at[idx].add(src)

def _segment_sum(src, seg, n):
    return jax.ops.segment_sum(src, seg, n)
kernel_name = 'mk_seq_preln_d2_jaxref_r8_71c4a5'

def setup_inputs(seed: int=0):
    np.random.seed(seed)
    _w = jnp.asarray

    def _L0_attn_setup():
        import jax, jax.numpy as jnp
        import numpy as np
        B_, L, D_MODEL = (2, 512, 256)
        H, P, N, G, K = (32, 64, 128, 1, 4)
        EPS = 1e-05
        INTER = H * P
        CONV_DIM = INTER + 2 * G * N
        PROJ = INTER + CONV_DIM + H

        def _silu(x):
            return x * jax.nn.sigmoid(x)

        def _mamba2_mixer(hidden_states, W_in, conv_w, conv_b, dt_bias, A_log, D_param, norm_w, W_out):
            b, l, _ = hidden_states.shape
            proj = jnp.einsum('bld,pd->blp', hidden_states, W_in)
            gate = proj[..., :INTER]
            hBC = proj[..., INTER:INTER + CONV_DIM]
            dt = proj[..., INTER + CONV_DIM:]
            xc = jnp.transpose(hBC, (0, 2, 1))
            conv = jax.lax.conv_general_dilated(xc, conv_w[:, None, :], window_strides=(1,), padding=[(K - 1, 0)], dimension_numbers=('NCH', 'OIH', 'NCH'), feature_group_count=CONV_DIM)
            hBC = _silu(jnp.transpose(conv + conv_b[None, :, None], (0, 2, 1)))
            xs = hBC[..., :INTER].reshape(b, l, H, P)
            Bm = hBC[..., INTER:INTER + G * N].reshape(b, l, G, N)
            Cm = hBC[..., INTER + G * N:].reshape(b, l, G, N)
            Bh = jnp.repeat(Bm, H // G, axis=2)
            Ch = jnp.repeat(Cm, H // G, axis=2)
            dt = jax.nn.softplus(dt + dt_bias)
            A = -jnp.exp(A_log)
            dA = jnp.exp(dt * A)

            def step(h, inp):
                dA_t, dt_t, x_t, B_t, C_t = inp
                u = (dt_t[:, :, None] * x_t)[..., None] * B_t[:, :, None, :]
                h = dA_t[:, :, None, None] * h + u
                y = jnp.einsum('bhpn,bhn->bhp', h, C_t)
                return (h, y)
            tm = lambda a: jnp.moveaxis(a, 1, 0)
            h0 = jnp.zeros((b, H, P, N), hidden_states.dtype)
            _, ys = jax.lax.scan(step, h0, (tm(dA), tm(dt), tm(xs), tm(Bh), tm(Ch)))
            y = jnp.moveaxis(ys, 0, 1) + D_param[None, None, :, None] * xs
            y = y.reshape(b, l, INTER)
            g = y * _silu(gate)
            g = g * jax.lax.rsqrt(jnp.mean(g * g, axis=-1, keepdims=True) + EPS) * norm_w
            return jnp.einsum('bli,di->bld', g, W_out)
        key = jax.random.key(seed)
        ks = jax.random.split(key, 5)
        hidden_states = jax.random.normal(ks[0], (B_, L, D_MODEL), jnp.float32)
        W_in = jax.random.normal(ks[1], (PROJ, D_MODEL), jnp.float32) * 0.02
        conv_w = jax.random.normal(ks[2], (CONV_DIM, K), jnp.float32) * 0.1
        conv_b = jnp.zeros((CONV_DIM,), jnp.float32)
        dt_bias = jnp.ones((H,), jnp.float32)
        A_log = jnp.log(jnp.arange(1, H + 1, dtype=jnp.float32))
        D_param = jnp.ones((H,), jnp.float32)
        norm_w = jnp.ones((INTER,), jnp.float32)
        W_out = jax.random.normal(ks[3], (D_MODEL, INTER), jnp.float32) * 0.02
        return dict(hidden_states=hidden_states, W_in=W_in, conv_w=conv_w, conv_b=conv_b, dt_bias=dt_bias, A_log=A_log, D_param=D_param, norm_w=norm_w, W_out=W_out)
    _L0_attn_in = _L0_attn_setup()

    def _L0_ffn_setup():
        import jax, jax.numpy as jnp
        import numpy as np
        EPS = 1e-08

        def _quantize(w):
            gamma = jnp.mean(jnp.abs(w))
            return jnp.clip(jnp.round(w / (gamma + EPS)), -1.0, 1.0)

        def _bitlinear(x, w):
            return jnp.matmul(x, _quantize(w).T)
        key = jax.random.key(seed)
        k1, k2, k3, k4 = jax.random.split(key, 4)
        d, h = (256, 704)
        x = jax.random.normal(k1, (4, 256, d), dtype=jnp.float32)
        w1 = jax.random.normal(k2, (h, d), dtype=jnp.float32)
        w2 = jax.random.normal(k3, (h, d), dtype=jnp.float32)
        w3 = jax.random.normal(k4, (d, h), dtype=jnp.float32)
        return {'x': x, 'w1': w1, 'w2': w2, 'w3': w3}
    _L0_ffn_in = _L0_ffn_setup()

    def _L1_attn_setup():
        import jax, jax.numpy as jnp
        import numpy as np
        import math
        N_EMBD = 256
        N_HEADS = 16
        HEAD_DIM = N_EMBD // N_HEADS
        CTX = 256

        def alibi_bias(seq_len: int, n_heads: int) -> jnp.ndarray:
            i = jnp.arange(seq_len)[:, None]
            j = jnp.arange(seq_len)[None, :]
            pos = jnp.where(j <= i, (j - i).astype(jnp.float32), 0.0)
            slopes = 2.0 ** (-8.0 / jnp.arange(1, n_heads + 1, dtype=jnp.float32))
            return slopes[:, None, None] * pos[None, :, :]

        def causal_mask(seq_len: int) -> jnp.ndarray:
            i = jnp.arange(seq_len)[:, None]
            j = jnp.arange(seq_len)[None, :]
            return jnp.where(j > i, -jnp.inf, 0.0).astype(jnp.float32)
        key = jax.random.key(seed)
        k_x, k_qkv, k_o = jax.random.split(key, 3)
        scale = 1.0 / math.sqrt(N_EMBD)
        x = jax.random.normal(k_x, (2, CTX, N_EMBD), dtype=jnp.float32)
        W_qkv = jax.random.normal(k_qkv, (N_EMBD, 3 * N_EMBD), dtype=jnp.float32) * scale
        W_o = jax.random.normal(k_o, (N_EMBD, N_EMBD), dtype=jnp.float32) * scale
        return {'x': x, 'W_qkv': W_qkv, 'W_o': W_o}
    _L1_attn_in = _L1_attn_setup()

    def _L1_ffn_setup():
        import jax, jax.numpy as jnp
        import numpy as np
        E = 64
        K = 6
        NG = 8
        TKG = 4
        SCALE = 2.5
        CAP = 64

        def _router(x, gate_w, e_bias):
            logits = x.astype(jnp.float32) @ gate_w.T
            scores = jax.nn.sigmoid(logits)
            sc = scores + e_bias[None, :]
            T = x.shape[0]
            gs = sc.reshape(T, NG, E // NG)
            grp_score = jax.lax.top_k(gs, 2)[0].sum(-1)
            _, gidx = jax.lax.top_k(grp_score, TKG)
            gmask = jax.nn.one_hot(gidx, NG, dtype=sc.dtype).sum(1)
            emask = jnp.repeat(gmask, E // NG, axis=1)
            masked = jnp.where(emask > 0, sc, -jnp.inf)
            _, idx = jax.lax.top_k(masked, K)
            w = jnp.take_along_axis(scores, idx, axis=1)
            w = w / (w.sum(-1, keepdims=True) + 1e-20) * SCALE
            return (idx, w)

        def _relu2(h):
            return jnp.square(jax.nn.relu(h))

        def _moe(x, idx, w, w1, w2):
            T, D = x.shape
            e_flat = idx.reshape(-1)
            tok = jnp.repeat(jnp.arange(T), K)
            oh = jax.nn.one_hot(e_flat, E, dtype=jnp.float32)
            pos = jnp.cumsum(oh, axis=0) - oh
            pos = (pos * oh).sum(-1).astype(jnp.int32)
            keep = pos < CAP
            slot = jnp.where(keep, pos, CAP)
            xd = jnp.zeros((E, CAP + 1, D), x.dtype).at[e_flat, slot].set(x[tok])
            h = _relu2(jnp.einsum('ecd,eid->eci', xd, w1))
            yd = jnp.einsum('eci,edi->ecd', h, w2)
            gate = w.reshape(-1)[:, None] * keep[:, None].astype(x.dtype)
            y_assign = yd[e_flat, slot] * gate
            return jnp.zeros((T, D), x.dtype).at[tok].add(y_assign)
        key = jax.random.key(seed)
        ks = jax.random.split(key, 6)
        D, I, SH, T = (256, 128, 512, 256)
        x = jax.random.normal(ks[0], (1, T, D), jnp.float32)
        gate_w = jax.random.normal(ks[1], (E, D), jnp.float32) * D ** (-0.5)
        e_bias = jnp.zeros((E,), jnp.float32)
        w1 = jax.random.normal(ks[2], (E, I, D), jnp.float32) * D ** (-0.5)
        w2 = jax.random.normal(ks[3], (E, D, I), jnp.float32) * I ** (-0.5)
        su = jax.random.normal(ks[4], (SH, D), jnp.float32) * D ** (-0.5)
        sd = jax.random.normal(ks[5], (D, SH), jnp.float32) * SH ** (-0.5)
        return {'hidden_states': x, 'gate_w': gate_w, 'e_bias': e_bias, 'w1': w1, 'w2': w2, 'shared_up_w': su, 'shared_down_w': sd}
    _L1_ffn_in = _L1_ffn_setup()
    _d = {'L0_attn_hidden_states': _L0_attn_in['hidden_states'], 'L0_attn_W_in': _L0_attn_in['W_in'], 'L0_attn_conv_w': _L0_attn_in['conv_w'], 'L0_attn_conv_b': _L0_attn_in['conv_b'], 'L0_attn_dt_bias': _L0_attn_in['dt_bias'], 'L0_attn_A_log': _L0_attn_in['A_log'], 'L0_attn_D_param': _L0_attn_in['D_param'], 'L0_attn_norm_w': _L0_attn_in['norm_w'], 'L0_attn_W_out': _L0_attn_in['W_out'], 'L0_ffn_w1': _L0_ffn_in['w1'], 'L0_ffn_w2': _L0_ffn_in['w2'], 'L0_ffn_w3': _L0_ffn_in['w3'], 'L1_attn_W_qkv': _L1_attn_in['W_qkv'], 'L1_attn_W_o': _L1_attn_in['W_o'], 'L1_ffn_gate_w': _L1_ffn_in['gate_w'], 'L1_ffn_e_bias': _L1_ffn_in['e_bias'], 'L1_ffn_w1': _L1_ffn_in['w1'], 'L1_ffn_w2': _L1_ffn_in['w2'], 'L1_ffn_shared_up_w': _L1_ffn_in['shared_up_w'], 'L1_ffn_shared_down_w': _L1_ffn_in['shared_down_w']}
    _x0 = _d['L0_attn_hidden_states']
    _d['L0_attn_hidden_states'] = jax.random.normal(jax.random.fold_in(jax.random.key(seed), 1), (4, 512, 256), dtype=_x0.dtype)
    del _x0
    return _d

def reference(L0_attn_hidden_states, L0_attn_W_in, L0_attn_conv_w, L0_attn_conv_b, L0_attn_dt_bias, L0_attn_A_log, L0_attn_D_param, L0_attn_norm_w, L0_attn_W_out, L0_ffn_w1, L0_ffn_w2, L0_ffn_w3, L1_attn_W_qkv, L1_attn_W_o, L1_ffn_gate_w, L1_ffn_e_bias, L1_ffn_w1, L1_ffn_w2, L1_ffn_shared_up_w, L1_ffn_shared_down_w):

    def _L0_attn_ref(hidden_states, W_in, conv_w, conv_b, dt_bias, A_log, D_param, norm_w, W_out):
        import jax, jax.numpy as jnp
        import numpy as np
        B_, L, D_MODEL = (2, 512, 256)
        H, P, N, G, K = (32, 64, 128, 1, 4)
        EPS = 1e-05
        INTER = H * P
        CONV_DIM = INTER + 2 * G * N
        PROJ = INTER + CONV_DIM + H

        def _silu(x):
            return x * jax.nn.sigmoid(x)

        def _mamba2_mixer(hidden_states, W_in, conv_w, conv_b, dt_bias, A_log, D_param, norm_w, W_out):
            b, l, _ = hidden_states.shape
            proj = jnp.einsum('bld,pd->blp', hidden_states, W_in)
            gate = proj[..., :INTER]
            hBC = proj[..., INTER:INTER + CONV_DIM]
            dt = proj[..., INTER + CONV_DIM:]
            xc = jnp.transpose(hBC, (0, 2, 1))
            conv = jax.lax.conv_general_dilated(xc, conv_w[:, None, :], window_strides=(1,), padding=[(K - 1, 0)], dimension_numbers=('NCH', 'OIH', 'NCH'), feature_group_count=CONV_DIM)
            hBC = _silu(jnp.transpose(conv + conv_b[None, :, None], (0, 2, 1)))
            xs = hBC[..., :INTER].reshape(b, l, H, P)
            Bm = hBC[..., INTER:INTER + G * N].reshape(b, l, G, N)
            Cm = hBC[..., INTER + G * N:].reshape(b, l, G, N)
            Bh = jnp.repeat(Bm, H // G, axis=2)
            Ch = jnp.repeat(Cm, H // G, axis=2)
            dt = jax.nn.softplus(dt + dt_bias)
            A = -jnp.exp(A_log)
            dA = jnp.exp(dt * A)

            def step(h, inp):
                dA_t, dt_t, x_t, B_t, C_t = inp
                u = (dt_t[:, :, None] * x_t)[..., None] * B_t[:, :, None, :]
                h = dA_t[:, :, None, None] * h + u
                y = jnp.einsum('bhpn,bhn->bhp', h, C_t)
                return (h, y)
            tm = lambda a: jnp.moveaxis(a, 1, 0)
            h0 = jnp.zeros((b, H, P, N), hidden_states.dtype)
            _, ys = jax.lax.scan(step, h0, (tm(dA), tm(dt), tm(xs), tm(Bh), tm(Ch)))
            y = jnp.moveaxis(ys, 0, 1) + D_param[None, None, :, None] * xs
            y = y.reshape(b, l, INTER)
            g = y * _silu(gate)
            g = g * jax.lax.rsqrt(jnp.mean(g * g, axis=-1, keepdims=True) + EPS) * norm_w
            return jnp.einsum('bli,di->bld', g, W_out)
        return _mamba2_mixer(hidden_states, W_in, conv_w, conv_b, dt_bias, A_log, D_param, norm_w, W_out)

    def _L0_ffn_ref(x, w1, w2, w3):
        import jax, jax.numpy as jnp
        import numpy as np
        EPS = 1e-08

        def _quantize(w):
            gamma = jnp.mean(jnp.abs(w))
            return jnp.clip(jnp.round(w / (gamma + EPS)), -1.0, 1.0)

        def _bitlinear(x, w):
            return jnp.matmul(x, _quantize(w).T)
        x1 = _bitlinear(x, w1)
        x2 = _bitlinear(x, w2)
        hidden = jax.nn.sigmoid(x1) * x2
        return _bitlinear(hidden, w3)

    def _L1_attn_ref(x, W_qkv, W_o):
        import jax, jax.numpy as jnp
        import numpy as np
        import math
        N_EMBD = 256
        N_HEADS = 16
        HEAD_DIM = N_EMBD // N_HEADS
        CTX = 256

        def alibi_bias(seq_len: int, n_heads: int) -> jnp.ndarray:
            i = jnp.arange(seq_len)[:, None]
            j = jnp.arange(seq_len)[None, :]
            pos = jnp.where(j <= i, (j - i).astype(jnp.float32), 0.0)
            slopes = 2.0 ** (-8.0 / jnp.arange(1, n_heads + 1, dtype=jnp.float32))
            return slopes[:, None, None] * pos[None, :, :]

        def causal_mask(seq_len: int) -> jnp.ndarray:
            i = jnp.arange(seq_len)[:, None]
            j = jnp.arange(seq_len)[None, :]
            return jnp.where(j > i, -jnp.inf, 0.0).astype(jnp.float32)
        bsz, seq_len, n_embd = x.shape
        qkv = jnp.einsum('bsd,de->bse', x, W_qkv)
        q, k, v = jnp.split(qkv, 3, axis=-1)

        def to_heads(t):
            return t.reshape(bsz, seq_len, N_HEADS, HEAD_DIM).transpose(0, 2, 1, 3)
        q, k, v = (to_heads(q), to_heads(k), to_heads(v))
        attn = jnp.einsum('bhqd,bhkd->bhqk', q, k) / math.sqrt(HEAD_DIM)
        attn = attn + alibi_bias(seq_len, N_HEADS)[None] + causal_mask(seq_len)[None, None]
        attn = jax.nn.softmax(attn, axis=-1)
        y = jnp.einsum('bhqk,bhkd->bhqd', attn, v)
        y = y.transpose(0, 2, 1, 3).reshape(bsz, seq_len, n_embd)
        return jnp.einsum('bsd,de->bse', y, W_o)

    def _L1_ffn_ref(hidden_states, gate_w, e_bias, w1, w2, shared_up_w, shared_down_w):
        import jax, jax.numpy as jnp
        import numpy as np
        E = 64
        K = 6
        NG = 8
        TKG = 4
        SCALE = 2.5
        CAP = 64

        def _router(x, gate_w, e_bias):
            logits = x.astype(jnp.float32) @ gate_w.T
            scores = jax.nn.sigmoid(logits)
            sc = scores + e_bias[None, :]
            T = x.shape[0]
            gs = sc.reshape(T, NG, E // NG)
            grp_score = jax.lax.top_k(gs, 2)[0].sum(-1)
            _, gidx = jax.lax.top_k(grp_score, TKG)
            gmask = jax.nn.one_hot(gidx, NG, dtype=sc.dtype).sum(1)
            emask = jnp.repeat(gmask, E // NG, axis=1)
            masked = jnp.where(emask > 0, sc, -jnp.inf)
            _, idx = jax.lax.top_k(masked, K)
            w = jnp.take_along_axis(scores, idx, axis=1)
            w = w / (w.sum(-1, keepdims=True) + 1e-20) * SCALE
            return (idx, w)

        def _relu2(h):
            return jnp.square(jax.nn.relu(h))

        def _moe(x, idx, w, w1, w2):
            T, D = x.shape
            e_flat = idx.reshape(-1)
            tok = jnp.repeat(jnp.arange(T), K)
            oh = jax.nn.one_hot(e_flat, E, dtype=jnp.float32)
            pos = jnp.cumsum(oh, axis=0) - oh
            pos = (pos * oh).sum(-1).astype(jnp.int32)
            keep = pos < CAP
            slot = jnp.where(keep, pos, CAP)
            xd = jnp.zeros((E, CAP + 1, D), x.dtype).at[e_flat, slot].set(x[tok])
            h = _relu2(jnp.einsum('ecd,eid->eci', xd, w1))
            yd = jnp.einsum('eci,edi->ecd', h, w2)
            gate = w.reshape(-1)[:, None] * keep[:, None].astype(x.dtype)
            y_assign = yd[e_flat, slot] * gate
            return jnp.zeros((T, D), x.dtype).at[tok].add(y_assign)
        orig = hidden_states.shape
        x = hidden_states.reshape(-1, orig[-1])
        idx, wts = _router(x, gate_w, e_bias)
        shared = _relu2(x @ shared_up_w.T) @ shared_down_w.T
        routed = _moe(x, idx, wts.astype(x.dtype), w1, w2)
        return (shared + routed).reshape(orig)
    x = L0_attn_hidden_states
    x = x + _L0_attn_ref(_layernorm(x, axis=-1), L0_attn_W_in, L0_attn_conv_w, L0_attn_conv_b, L0_attn_dt_bias, L0_attn_A_log, L0_attn_D_param, L0_attn_norm_w, L0_attn_W_out)
    x = x + _L0_ffn_ref(_layernorm(x, axis=-1), L0_ffn_w1, L0_ffn_w2, L0_ffn_w3)
    x = x + _L1_attn_ref(_layernorm(x, axis=-1), L1_attn_W_qkv, L1_attn_W_o)
    x = x + _L1_ffn_ref(_layernorm(x, axis=-1), L1_ffn_gate_w, L1_ffn_e_bias, L1_ffn_w1, L1_ffn_w2, L1_ffn_shared_up_w, L1_ffn_shared_down_w)
    return x

_drawn_inputs = setup_inputs


def setup_inputs(seed=0):
    import zlib

    import numpy as np

    out = dict(_drawn_inputs(seed))
    spreads = {'L0_attn_conv_b': (0.0, 0.1),
     'L0_attn_dt_bias': (1.0, 0.6),
     'L0_attn_D_param': (1.0, 0.2),
     'L0_attn_norm_w': (1.0, 0.2),
     'L1_ffn_e_bias': (0.0, 0.8)}
    factors = {'L0_attn_A_log': 8.0,
     'L1_attn_W_qkv': 8.0,
     'L1_attn_W_o': 8.0,
     'L1_ffn_gate_w': 8.0,
     'L1_ffn_w1': 8.0,
     'L1_ffn_w2': 8.0,
     'L1_ffn_shared_up_w': 8.0,
     'L1_ffn_shared_down_w': 8.0}
    for name, (base, spread) in spreads.items():
        noise = np.random.default_rng([zlib.crc32(name.encode()), seed]).standard_normal(out[name].shape)
        drawn = base * np.exp(spread * noise) if base else spread * noise
        out[name] = jnp.asarray(drawn.astype(out[name].dtype))
    for name, factor in factors.items():
        out[name] = (out[name] * factor).astype(out[name].dtype)
    return out
```

```python
from contextlib import ExitStack

import numpy as np
import concourse.bass as bass
from concourse import mybir

ALU = mybir.AluOpType
ACT = mybir.ActivationFunctionType
AX = mybir.AxisListType
F32 = mybir.dt.float32
F16 = mybir.dt.float16
BF16 = mybir.dt.bfloat16
U32 = mybir.dt.uint32

P = 128
B, L, D = 4, 512, 256
T = L // P
KD = D // P
NTOK = B * L
H, HP, N = 32, 64, 128
INTER = H * HP
TAPS = 4
XS, BC, CC, DTC = INTER, 2 * INTER, 2 * INTER + N, 2 * INTER + 2 * N
PROJ = DTC + H
CT = (INTER + 2 * N) // P
G = 4
GH = H // G
GF = INTER // G
GK = GF // P
UNITS = T * G
FF = 704
FT = (FF + P - 1) // P
AH, AD = 16, 16
AG = AH // 4
AU = T * AH
E, TOPK, NG, TKG, CAP = 64, 6, 8, 4, 64
EG = E // NG
SCALE = 2.5
SH = 512
ST = SH // P
XW = D + E
PAIRS = E // 2
EPS = 1e-5
BIG = 1e30


class Signal:

    def __init__(self, sem, step, per_trip, start):
        self.sem, self.step, self.per_trip, self.start = sem, step, per_trip, start
        self.count = self.most = 0

    def inc(self, instruction):
        self.count += 1
        self.most = max(self.most, self.count)
        instruction.then_inc(self.sem, self.step)

    def new_trip(self):
        self.count = 0

    def free_at_first(self, engine):
        for _ in range(self.start):
            engine.drain().then_inc(self.sem, self.step)

    def upto(self, k, b=None):
        value = (self.start + k) * self.step
        return value if b is None else b * (self.per_trip * self.step) + value


def build(nc, a, per_trip):
    with ExitStack() as ctx:
        signals = {}

        def sb(name, shape, dt=F32):
            return ctx.enter_context(nc.sbuf_tensor(name, shape, dt))

        def signal(name, step=1, start=0):
            s = Signal(ctx.enter_context(nc.semaphore(name)), step, per_trip.get(name, 0), start)
            signals[name] = s
            return s

        pb = [ctx.enter_context(nc.psum_tensor(f"bank{i}", [P, 512], F32)) for i in range(8)]

        xg = nc.dram_tensor("xg", (NTOK + 1, XW), F32).ap()
        ytab = nc.dram_tensor("ytab", (E * CAP + 1, D), F32).ap()
        base = nc.dram_tensor("base", (NTOK, D), F32).ap()

        win = sb("win", [P, KD, PROJ])
        wout = sb("wout", [P, INTER // P, D])
        convw = sb("convw", [P, CT, TAPS])
        convb = sb("convb", [P, CT])
        dtb = sb("dtb", [P, H])
        expA = sb("expA", [P, H])
        dpar = sb("dpar", [P, H])
        normw = sb("normw", [P, INTER // P])
        w1q = sb("w1q", [P, KD, FT * P], F16)
        w2q = sb("w2q", [P, KD, FT * P], F16)
        w3q = sb("w3q", [P, FT, D], F16)
        gw = sb("gw", [P, KD, E])
        ebias = sb("ebias", [P, E])
        ident = sb("ident", [P, P])
        upto_ = sb("upto_", [P, P])
        after = sb("after", [P, P])
        before = sb("before", [P, P])
        ones = sb("ones", [P, P])
        identb = sb("identb", [P, P], BF16)
        maskb = sb("maskb", [P, P], BF16)
        iota8 = sb("iota8", [P, NG])
        iota64 = sb("iota64", [P, E])
        slot0 = sb("slot0", [P, E])
        eps = sb("eps", [P, 1])
        cum = sb("cum", [P, T + 1, E])

        xb = sb("xb", [P, T, D])
        xn = sb("xn", [P, T, D])
        xnT = sb("xnT", [P, KD, L])
        stats = sb("stats", [P, T, 6])
        mv = sb("mv", [P, T, 2])
        std = sb("std", [P, T])
        rstd = sb("rstd", [P, T])

        pool_a = sb("pool_a", [P, T * INTER])
        pool_b = sb("pool_b", [P, T * INTER])
        pool_c = sb("pool_c", [P, 8192])
        xtok = pool_a[:, :].rearrange("p (t f) -> p t f", t=T)
        sz = pool_b[:, :].rearrange("p (t f) -> p t f", t=T)

        def carve(buf, at, n, dt=F32):
            ap = buf[:, at:at + n]
            return ap if dt == F32 else ap.bitcast(dt)

        conv = [carve(pool_c, i * 512, 512) for i in range(2)]
        xsf = [carve(pool_c, 1024 + i * 512, 512) for i in range(2)]
        rA = [carve(pool_c, i * 1024, 1024).rearrange("p (h i) -> p h i", h=GH) for i in range(2)]
        Lx = [carve(pool_c, 2048 + i * 1024, 1024).rearrange("p (h i) -> p h i", h=GH) for i in range(2)]
        xdt = [carve(pool_c, 4096 + i * 512, 512) for i in range(2)]
        xde = [carve(pool_c, 5120 + i * 512, 512) for i in range(2)]
        xD = [carve(pool_c, 6144 + i * 512, 512) for i in range(2)]
        sx = [carve(pool_c, 7168 + i * 512, 512) for i in range(2)]
        BT = sb("BT", [P, L])
        CTm = sb("CTm", [P, L])
        btok = sb("btok", [P, T, N])
        v_dt = sb("v_dt", [P, T, H])
        u_dt = sb("u_dt", [P, T, H])
        l_dt = sb("l_dt", [P, T, H])
        dt_ = sb("dt_", [P, T, H])
        a_ = sb("a_", [P, T, H])
        dec = sb("dec", [P, 3, T * H])
        cbm = sb("cbm", [P, P])
        S = sb("S", [P, INTER])
        yb, yo = xn[:, 0:2, :].rearrange("p t n -> p (t n)"), xn[:, 2:4, :].rearrange("p t n -> p (t n)")
        gb = [xnT[:, i, :] for i in range(2)]
        gTs = [sb(f"gTs{i}", [P, GK, P]) for i in range(2)]
        ssq = sb("ssq", [P, T, G])
        ms = sb("ms", [P, T])
        pob = sb("pob", [P, T, D])
        junk = sb("junk", [P, 512], BF16)

        h_hi = carve(pool_c, 0, 512, F16).rearrange("p (k n) -> p k n", k=KD)
        h_lo = carve(pool_c, 512, 512, F16).rearrange("p (k n) -> p k n", k=KD)
        sg = [carve(pool_c, 1024 + i * 512, 512) for i in range(2)]
        hid = [carve(pool_c, 2048 + i * 512, 512) for i in range(2)]
        hh = carve(pool_c, 3072, FT * 256, F16).rearrange("p (f n) -> p f n", f=FT)
        hl = carve(pool_c, 3072 + FT * 256, FT * 256, F16).rearrange("p (f n) -> p f n", f=FT)

        qT = carve(pool_a, 0, AG * L).rearrange("p (g n) -> p g n", g=AG)
        kT = carve(pool_a, 2048, AG * L).rearrange("p (g n) -> p g n", g=AG)
        vt = carve(pool_a, 4096, T * D).rearrange("p (t n) -> p t n", t=T)
        qadd = carve(pool_a, 5120, AG * L).rearrange("p (g n) -> p g n", g=AG)
        kadd = carve(pool_a, 7168, L)
        pr = [carve(pool_b, i * 512, 512) for i in range(3)]
        pT = [carve(pool_b, 1536 + i * 512, 512) for i in range(2)]
        yat = carve(pool_b, 2560, T * D).rearrange("p (t n) -> p t n", t=T)
        yT = carve(pool_b, 3584, KD * L).rearrange("p (k n) -> p k n", k=KD)
        wq = carve(pool_c, 6144, KD * AG * P).rearrange("p (k n) -> p k n", k=KD)
        wk = carve(pool_c, 7168, KD * AG * P).rearrange("p (k n) -> p k n", k=KD)
        wv = carve(pool_b, 4608, KD * D).rearrange("p (k n) -> p k n", k=KD)
        wo = carve(pool_b, 5120, KD * D).rearrange("p (k n) -> p k n", k=KD)
        nmax = sb("nmax", [P, AU])
        psums = sb("psums", [P, AU])
        rsums = sb("rsums", [P, AU])

        sc = carve(pool_c, 0, 256).rearrange("p (t e) -> p t e", t=T)
        sbi = carve(pool_c, 256, 256).rearrange("p (t e) -> p t e", t=T)
        m8 = carve(pool_c, 512, 256).rearrange("p (t g m) -> p t g m", t=T, g=NG)
        grp = carve(pool_c, 768, 32).rearrange("p (t g) -> p t g", t=T)
        gm8 = carve(pool_c, 800, 32).rearrange("p (t g) -> p t g", t=T)
        gi = carve(pool_c, 832, 32, U32).rearrange("p (t g) -> p t g", t=T)
        gif = carve(pool_c, 864, 32).rearrange("p (t g) -> p t g", t=T)
        goh = carve(pool_c, 896, 128).rearrange("p (t g k) -> p t g k", t=T, g=NG)
        gmask = carve(pool_c, 1024, 32)
        em8 = carve(pool_c, 1056, 32).rearrange("p (t g) -> p t g", t=T)
        ei = carve(pool_c, 1088, 32, U32).rearrange("p (t g) -> p t g", t=T)
        eif = carve(pool_c, 1120, 32).rearrange("p (t g) -> p t g", t=T)
        wsum = carve(pool_c, 1152, 4)
        wrec = carve(pool_c, 1156, 4)
        s8 = carve(pool_c, 1160, 32).rearrange("p (t g) -> p t g", t=T)
        masked = carve(pool_c, 1280, 256)
        sel = carve(pool_c, 1536, 256).rearrange("p (t e) -> p t e", t=T)
        wsel = carve(pool_c, 1792, 256).rearrange("p (t e) -> p t e", t=T)
        kept = carve(pool_c, 2048, 256)
        sid = carve(pool_c, 2304, 256)
        eoh = carve(pool_c, 2560, T * E * TOPK).rearrange("p (t e k) -> p t e k", t=T, e=E)
        sr = [carve(pool_b, i * 512, 512) for i in range(2)]
        su = carve(pool_b, 6144, KD * SH).rearrange("p (k n) -> p k n", k=KD)
        sd = carve(pool_b, 7168, ST * D).rearrange("p (k n) -> p k n", k=ST)
        hs = carve(pool_b, 1024, ST * L).rearrange("p (f n) -> p f n", f=ST)
        slots = sb("slots", [P, NTOK // P, 8], U32)
        selT = sb("selT", [E, NTOK], BF16)

        tokval = pool_c[0:E, 6144:8192]
        ranked = pool_c[0:E, 4096:6144]
        top = sb("top", [E, CAP])
        tokf = sb("tokf", [E, 2, CAP])
        gidx = sb("gidx", [P, PAIRS], U32)
        WB = 4
        w1m = [carve(pool_a, i * 512, 512).rearrange("p (e k i) -> p e k i", e=2, k=KD) for i in range(WB)]
        w2m = [carve(pool_a, 2048 + i * 512, 512).rearrange("p (e n) -> p e n", e=2) for i in range(WB)]
        xd = [carve(pool_b, i * XW, XW) for i in range(WB)]
        xdT = [carve(pool_b, 1536 + i * 256, 256).rearrange("p (k s) -> p k s", k=KD) for i in range(2)]
        hr = [carve(pool_b, 2048 + i * P, P) for i in range(2)]
        hq = [carve(pool_b, 2304 + i * P, P) for i in range(2)]
        ys = [carve(pool_b, 2560 + i * D, D) for i in range(4)]
        yg = [carve(pool_c, i * TOPK * D, TOPK * D).rearrange("p (k n) -> p k n", k=TOPK) for i in range(4)]
        bt = [carve(pool_b, 4096 + i * D, D) for i in range(4)]
        fin = [carve(pool_b, 5120 + i * D, D) for i in range(4)]
        scol = [sb(f"scol{i}", [P, 8], U32) for i in range(4)]
        gcol = [sb(f"gcol{i}", [P, 1], U32) for i in range(WB)]
        zrow = gTs[0][0:1, :, :].rearrange("p k n -> p (k n)")[:, 0:XW]

        w_in_loaded = signal("w_in_loaded", 16)
        w_rest_loaded = signal("w_rest_loaded", 16)
        w_ffn_loaded = signal("w_ffn_loaded", 16)
        zeros_stored = signal("zeros_stored", 16)
        pro_act = signal("pro_act")
        pro_pe = signal("pro_pe")
        pro_dve = signal("pro_dve")
        pro_pool = signal("pro_pool")
        x_loaded = signal("x_loaded", 16)
        late_loaded = signal("late_loaded", 16)
        tokval_loaded = signal("tokval_loaded", 16)
        row_free = signal("row_free", start=1)
        stored = signal("stored", 16)
        stage = {n: signal(f"stage_{n}") for n in ("pe", "act", "dve", "pool")}
        dstep = signal("dstep")
        settled = signal("settled")
        pstep = signal("pstep")
        ln_stats, ln_std, ln_xn, ln_T, ln_Ta, ln_Td = (signal(n) for n in ("ln_stats", "ln_std", "ln_xn", "ln_T", "ln_Ta", "ln_Td"))
        dt_mm, dt_abs, dt_log, a_ready, dec_mm, dec_ready = (signal(n) for n in ("dt_mm", "dt_abs", "dt_log", "a_ready", "dec_mm", "dec_ready"))
        proj_mm, tap3, conv_done, silu_done, gate_mm, gate_done, xT_mm, xtok_done = (
            signal(n) for n in ("proj_mm", "tap3", "conv_done", "silu_done", "gate_mm", "gate_done", "xT_mm", "xtok_done"))
        rA_ready, seg_mm, L_ready, M_ready, cb_mm, cbm_ready = (signal(n) for n in ("rA_ready", "seg_mm", "L_ready", "M_ready", "cb_mm", "cbm_ready"))
        xdt_ready, xde_ready, xD_ready, sx_ready = (signal(n) for n in ("xdt_ready", "xde_ready", "xD_ready", "sx_ready"))
        yd_mm, yo_mm, ds_mm, yd_read, yo_read, S_ready = (signal(n) for n in ("yd_mm", "yo_mm", "ds_mm", "yd_read", "yo_read", "S_ready"))
        g_ready, g_sq, gT_mm, gTs_ready, out_mm, po_read = (signal(n) for n in ("g_ready", "g_sq", "gT_mm", "gTs_ready", "out_mm", "po_read"))
        ms_ready, rms_std = signal("ms_ready"), signal("rms_std")
        up_mm, sig_done, hid_done, hh_done, hl_done, down_mm = (signal(n) for n in ("up_mm", "sig_done", "hid_done", "hh_done", "hl_done", "down_mm"))
        q_mm, k_mm, v_mm, q_done, k_done, v_done = (signal(n) for n in ("q_mm", "k_mm", "v_mm", "q_done", "k_done", "v_done"))
        s_mm, max_done, exp_done, pT_mm, pT_act, pT_dve, pv_mm, o_done = (
            signal(n) for n in ("s_mm", "max_done", "exp_done", "pT_mm", "pT_act", "pT_dve", "pv_mm", "o_done"))
        yT_mm, yT_act, yT_dve, wo_mm = (signal(n) for n in ("yT_mm", "yT_act", "yT_dve", "wo_mm"))
        lg_mm, sc_ready, su_mm, sr_ready, hs_ready, sd_mm = (signal(n) for n in ("lg_mm", "sc_ready", "su_mm", "sr_ready", "hs_ready", "sd_mm"))
        sel_ready, w_ready, pos_mm, selT_mm, selT_done, out_ready, cum_ready = (
            signal(n) for n in ("sel_ready", "w_ready", "pos_mm", "selT_mm", "selT_done", "out_ready", "cum_ready"))
        post_dve, post_pe, idx_ready = signal("post_dve"), signal("post_pe"), signal("idx_ready")
        wm_loaded = [signal(f"wm_loaded{i}", 16) for i in range(WB)]
        xd_loaded = [signal(f"xd_loaded{i}", 16) for i in range(WB)]
        xdT_mm, xdT_ready, h_mm, hr_ready, hq_ready = (
            signal(n) for n in ("xdT_mm", "xdT_ready", "h_mm", "hr_ready", "hq_ready"))
        y_mm, ys_ready = signal("y_mm", start=WB), signal("ys_ready", start=WB)
        y_stored = [signal(f"y_stored{i}", 16) for i in range(4)]
        yg_loaded = [signal(f"yg_loaded{i}", 16) for i in range(4)]
        bt_loaded = [signal(f"bt_loaded{i}", 16) for i in range(4)]
        fin_ready = signal("fin_ready", start=4)
        dfin, pcol, xcol = signal("dfin"), signal("pcol"), signal("xcol")
        fin_stored = [signal(f"fin_stored{i}", 16) for i in range(4)]

        block = ctx.enter_context(nc.Block())
        n_stage = {n: 0 for n in stage}

        def settle(eng):
            eng.sem_inc(settled.sem, 1)

        def stage_end(name, eng, b):
            n_stage[name] += 1
            settle(eng)
            stage[name].inc(eng.drain())
            for other in stage:
                if other != name:
                    eng.wait_ge(stage[other].sem, stage[other].upto(n_stage[name], b))

        rest_loads = [(wout, a["wout"]), (convw, a["convw"]), (convb, a["convb"]), (dtb, a["dtb"]), (expA, a["alog"]),
                      (dpar, a["dpar"]), (normw, a["normw"]), (ident, a["ident"]), (upto_, a["upto"]), (after, a["after"]),
                      (before, a["before"]), (ones, a["ones"]), 
                      (gw, a["gw"]), (ebias, a["ebias"]),
                      (iota8, a["iota8"]), (iota64, a["iota64"]), (slot0, a["slot0"]), (eps, a["eps"])]
        row_loads = [(wq, a["wq"]), (wk, a["wk"]), (wv, a["wv"]), (wo, a["wo"]), (qadd, a["qadd"]), (kadd, a["kadd"]), (su, a["su"]), (sd, a["sd"])]
        wf = [carve(pool_c, 2048, KD * FT * P), carve(pool_c, 2048 + 1536, KD * FT * P), carve(pool_c, 2048 + 3072, FT * D)]
        wt = [w.rearrange("p k n -> p (k n)") for w in (w1q[:, :, :], w2q[:, :, :], w3q[:, :, :])]
        maskf = carve(pool_c, 2048 + 4608, P)
        low = S[:, 0:KD * FT * P]
        absum, thr, nthr = S[:, 2040:2043], S[:, 2030:2033], S[:, 2034:2037]
        ffn_loads = [(wf[0], a["w1"]), (wf[1], a["w2"]), (wf[2], a["w3"]), (maskf, a["mask"])]

        @block.sync
        def _(sp):
            w_in_loaded.inc(sp.dma_start(win[:, :, :], a["win"]))
            for dst, src in rest_loads:
                w_rest_loaded.inc(sp.dma_start(dst[tuple(slice(None) for _ in dst.shape)], src))
            with sp.Fori(0, B) as b:
                sp.wait_ge(row_free.sem, row_free.upto(0, b))
                x_loaded.inc(sp.dma_start(xb[:, :, :], a["x"].rearrange("b (t p) d -> b p t d", p=P)[bass.ds(b, 1)]
                                          .rearrange("b p t d -> p (b t) d")))
                for s in stage.values():
                    sp.wait_ge(s.sem, s.upto(2, b))
                for dst, src in row_loads:
                    late_loaded.inc(sp.dma_start(dst, src))
                sp.wait_ge(ln_xn.sem, ln_xn.upto(4, b))
                rows = xg[0:NTOK, :].rearrange("(b t p) w -> b p t w", p=P, t=T)[bass.ds(b, 1)]
                stored.inc(sp.dma_start(rows[:, :, :, 0:D].rearrange("b p t w -> p (b t) w"), xn[:, :, :]))
                sp.wait_ge(w_ready.sem, w_ready.upto(1, b))
                stored.inc(sp.dma_start(rows[:, :, :, D:XW].rearrange("b p t w -> p (b t) w"), wsel))
                sp.wait_ge(out_ready.sem, out_ready.upto(1, b))
                stored.inc(sp.dma_start(base.rearrange("(b t p) w -> b p t w", p=P, t=T)[bass.ds(b, 1)]
                                        .rearrange("b p t w -> p (b t) w"), xb[:, :, :]))
            sp.wait_ge(row_free.sem, row_free.upto(B))
            tokval_loaded.inc(sp.dma_start(tokval, a["tokval"]))
            w1v = a["w1m"].rearrange("(h q) p k i -> q p h (k i)", h=2)
            w2v = a["w2m"].rearrange("(h q) i n -> q i h n", h=2)
            with sp.Fori(0, PAIRS // WB) as r:
                for i in range(WB):
                    sp.wait_ge(y_mm.sem, y_mm.upto(i + 1 - WB, r))
                    n = r * WB + i
                    wm_loaded[i].inc(sp.dma_start(w1m[i].rearrange("p e k i -> p e (k i)"),
                                                  w1v[bass.ds(n, 1)].rearrange("q p h w -> p (q h) w")))
                    wm_loaded[i].inc(sp.dma_start(w2m[i], w2v[bass.ds(n, 1)].rearrange("q i h n -> i (q h) n")))
            outv = a["out"].rearrange("b (t p) d -> (b t) p d", p=P)
            with sp.Fori(0, NTOK // P // 4) as r:
                for i in range(4):
                    sp.wait_ge(fin_ready.sem, fin_ready.upto(i + 1, r))
                    fin_stored[i].inc(sp.dma_start(outv[bass.ds(r * 4 + i, 1)].rearrange("n p d -> (n p) d"), fin[i]))
            for i in range(4):
                sp.wait_ge(fin_stored[i].sem, 16 * (NTOK // P // 4))

        @block.scalar
        def _(act):
            sa = nc.scalar
            for dst, src in ffn_loads:
                w_ffn_loaded.inc(act.dma_start(dst, src))
            act.wait_ge(w_rest_loaded.sem, 16 * len(rest_loads))
            pro_act.inc(sa.activation(expA[:, :], expA[:, :], ACT.Exp))
            act.wait_ge(w_ffn_loaded.sem, 16 * len(ffn_loads))
            for i in range(3):
                last = sa.activation(pool_b[:, i * 1536:(i + 1) * 1536], wf[i], ACT.Abs, accum_out=absum[:, i:i + 1])
            pro_act.inc(last)

            with act.Fori(0, B) as b:
                def at(s, k):
                    act.wait_ge(s.sem, s.upto(k, b))

                def norm_std(n):
                    at(ln_stats, n + 1)
                    ln_std.inc(sa.activation(std[:, :], mv[:, :, 1], ACT.Sqrt, bias=eps[:, 0:1]))

                def norm_T(n):
                    at(ln_T, 2 * n + 1)
                    ln_Ta.inc(sa.activation(xnT[:, 0, :], pb[0][:, :], ACT.Copy))

                norm_std(0)
                norm_T(0)
                at(dt_abs, 1)
                dt_log.inc(sa.activation(l_dt[:, :, :], u_dt[:, :, :], ACT.Exp, scale=-1.0))
                at(dt_log, 1)
                dt_log.inc(sa.activation(l_dt[:, :, :], l_dt[:, :, :], ACT.Ln, bias=1.0))
                for j in range(CT + 2):
                    if j < CT:
                        ci = (CT - 2 + j) if j < 2 else j - 2
                        at(proj_mm, j + 1)
                        if j >= 2:
                            at(silu_done, j - 1)
                        tap3.inc(sa.activation(conv[j % 2], pb[j % 2][:, :], ACT.Identity,
                                               scale=convw[:, ci, 3:4], bias=convb[:, ci:ci + 1]))
                    if 1 <= j <= CT:
                        i = j - 1
                        at(conv_done, i + 1)
                        if i >= 4:
                            at(xT_mm, i - 2)
                        dst = (BT[:, :], CTm[:, :])[i] if i < 2 else xsf[i % 2]
                        silu_done.inc(sa.activation(dst, conv[i % 2], ACT.Silu))
                    if 2 <= j < CT:
                        m = j - 2
                        at(gate_mm, m + 1)
                        gate_done.inc(sa.activation(sz[:, m // G, (m % G) * GF:(m % G + 1) * GF], pb[2 + m % 2][:, :], ACT.Silu))
                    if j == 2:
                        at(xT_mm, 1)
                        xtok_done.inc(sa.activation(btok[:, :, :], pb[4][:, :].rearrange("p (t n) -> p t n", t=T), ACT.Copy))
                    if j >= 4:
                        m = j - 4
                        at(xT_mm, m + 2)
                        xtok_done.inc(sa.activation(xtok[:, :, m * P:(m + 1) * P],
                                                    pb[4 + (m + 1) % 2][:, :].rearrange("p (t n) -> p t n", t=T), ACT.Copy))
                at(dec_mm, 1)
                dec_ready.inc(sa.activation(dec[:, :, :].rearrange("p s n -> p (s n)"), pb[6][:, 0:3 * T * H], ACT.Exp))
                stage_end("act", act, b)

                def decay_terms(u):
                    c, g = u // G, u % G
                    if u >= 2:
                        at(seg_mm, 2 * (u - 1))
                    for h in range(GH):
                        hh_ = g * GH + h
                        last = sa.activation(rA[u % 2][:, h, :], upto_[:, :], ACT.Copy, scale=a_[:, c, hh_:hh_ + 1])
                    rA_ready.inc(last)

                decay_terms(0)
                decay_terms(1)
                for u in range(UNITS + 1):
                    if u < UNITS:
                        if u >= 2:
                            at(yd_mm, u - 1)
                        for half in range(2):
                            at(seg_mm, 2 * u + half + 1)
                            L_ready.inc(sa.activation(Lx[u % 2][:, half * 4:half * 4 + 4, :],
                                                      pb[half][:, :].rearrange("p (h i) -> p h i", h=4), ACT.Exp))
                    if u + 2 < UNITS:
                        decay_terms(u + 2)
                    if u >= 1:
                        w = u - 1
                        at(g_ready, w + 1)
                        if w >= 1:
                            at(g_sq, w)
                        g_sq.inc(sa.activation(junk[:, :], gb[w % 2][:, :], ACT.Square, accum_out=ssq[:, w // G, w % G:w % G + 1]))
                        at(gT_mm, w + 1)
                        if w >= 2:
                            at(out_mm, w - 1)
                        gTs_ready.inc(sa.activation(gTs[w % 2][:, :, :].rearrange("p k n -> p (k n)"), pb[5][:, :], ACT.Copy))
                stage_end("act", act, b)

                at(ms_ready, 1)
                rms_std.inc(sa.activation(std[:, :], ms[:, :], ACT.Sqrt, scale=1.0 / INTER, bias=eps[:, 0:1]))
                norm_std(1)
                at(ln_T, 4)
                for k in range(KD):
                    last = sa.activation(h_hi[:, k, :], pb[k][:, :], ACT.Copy)
                ln_Ta.inc(last)
                for f in range(FT):
                    at(up_mm, 2 * f + 1)
                    if f >= 2:
                        at(hid_done, f - 1)
                    sig_done.inc(sa.activation(sg[f % 2], pb[2 + f % 2][:, :], ACT.Sigmoid))
                    at(hid_done, f + 1)
                    hh_done.inc(sa.activation(hh[:, f, :], hid[f % 2], ACT.Copy))
                stage_end("act", act, b)

                norm_std(2)
                norm_T(2)
                for q in range(2):
                    at(v_mm, 2 * q + 2)
                    v_done.inc(sa.activation(vt[:, 2 * q:2 * q + 2, :], pb[6 + q][:, :].rearrange("p (t n) -> p t n", t=2), ACT.Copy))
                stage_end("act", act, b)

                for n in range(AU + 1):
                    if n < AU:
                        cols = (n // AH + 1) * P
                        at(max_done, n + 1)
                        if n >= 3:
                            at(pT_mm, n - 2)
                        exp_done.inc(sa.activation(pr[n % 3][:, 0:cols], pb[(0, 1, 6)[n % 3]][:, 0:cols], ACT.Exp,
                                                   bias=nmax[:, n:n + 1], accum_out=psums[:, n:n + 1]))
                    w = n - 1
                    if w >= 0 and w % 2 == 1:
                        cols = (w // AH + 1) * P
                        at(pT_mm, w + 1)
                        if w >= 2:
                            at(pv_mm, w - 1)
                        pT_act.inc(sa.activation(pT[w % 2][:, 0:cols], pb[2 + w % 2][:, 0:cols], ACT.Copy))
                at(yT_mm, 1)
                yT_act.inc(sa.activation(yT[:, 0, :], pb[2][:, :], ACT.Copy))
                stage_end("act", act, b)

                norm_std(3)
                norm_T(3)
                at(lg_mm, 1)
                sc_ready.inc(sa.activation(sc.rearrange("p t e -> p (t e)"), pb[2][:, 0:T * E], ACT.Sigmoid))
                for f in range(ST):
                    at(su_mm, f + 1)
                    if f >= 2:
                        at(hs_ready, f - 1)
                    sr_ready.inc(sa.activation(sr[f % 2], pb[4 + f % 2][:, :], ACT.Relu))
                stage_end("act", act, b)

            y_stores = ytab[1:E * CAP + 1, :].rearrange("(h q s) n -> h q s n", h=2, s=CAP)
            ys_ready.free_at_first(act)

            def pairs(r, first):
                for i in range(WB):
                    act.wait_ge(h_mm.sem, h_mm.upto(i + 1, r))
                    if i >= 2 or not first:
                        act.wait_ge(hq_ready.sem, hq_ready.upto(i - 1, r))
                    hr_ready.inc(sa.activation(hr[i % 2], pb[2 + i % 2][:, 0:P], ACT.Relu))
                    act.wait_ge(y_mm.sem, y_mm.upto(i + 1, r))
                    if not first:
                        act.wait_ge(y_stored[i].sem, r * 32)
                    n = r * WB + i
                    for h in range(2):
                        gate = xd[i][h * CAP:(h + 1) * CAP, bass.ds(D + h * PAIRS + n, 1)]
                        last = sa.activation(ys[i][h * CAP:(h + 1) * CAP, :], pb[4 + i % 2][h * CAP:(h + 1) * CAP, 0:D],
                                             ACT.Copy, scale=gate)
                    ys_ready.inc(last)
                    act.wait_ge(ys_ready.sem, ys_ready.upto(i + 1, r))
                    for h in range(2):
                        y_stored[i].inc(act.dma_start(y_stores[h][bass.ds(n, 1)].rearrange("q s n -> (q s) n"),
                                                      ys[i][h * CAP:(h + 1) * CAP, :]))
            pairs(0, True)
            for s in signals.values():
                s.new_trip()
            with act.Fori(1, PAIRS // WB) as r:
                pairs(r, False)
            bview = base.rearrange("(n p) d -> n p d", p=P)
            act.wait_ge(stored.sem, 16 * 3 * B)
            with act.Fori(0, NTOK // P // 4) as r:
                for i in range(4):
                    act.wait_ge(fin_ready.sem, fin_ready.upto(i + 1 - 4, r))
                    bt_loaded[i].inc(act.dma_start(bt[i], bview[bass.ds(r * 4 + i, 1)].rearrange("n p d -> (n p) d")))

        @block.tensor
        def _(pe):
            mm = nc.tensor.matmul

            def transpose(out, in_, size=P):
                return nc.tensor.transpose(out, in_, ident[0:size, 0:size])

            pe.wait_ge(w_rest_loaded.sem, 16 * len(rest_loads))
            pe.wait_ge(pro_act.sem, 2)
            pro_pe.inc(mm(pb[7][:, 0:3], ones[:, :], absum, start=True, stop=True))
            pe.wait_ge(w_in_loaded.sem, 16)
            pe.wait_ge(pro_dve.sem, 1)

            with pe.Fori(0, B) as b:
                def at(s, k):
                    pe.wait_ge(s.sem, s.upto(k, b))

                def norm_T(n):
                    at(ln_xn, n + 1)
                    for k in range(KD):
                        for t in range(T):
                            last = transpose(pb[k][:, t * P:(t + 1) * P], xn[:, t, k * P:(k + 1) * P])
                        ln_T.inc(last)
                    at(ln_Ta, n + 1)
                    at(ln_Td, n + 1)

                norm_T(0)
                for t in range(T):
                    for k in range(KD):
                        last = mm(pb[7][:, t * H:(t + 1) * H], xnT[:, k, t * P:(t + 1) * P], win[:, k, DTC:DTC + H],
                                  start=(k == 0), stop=(k == KD - 1))
                dt_mm.inc(last)
                for j in range(CT + 1):
                    if j < CT:
                        if j >= 2:
                            at(conv_done, j - 1)
                        col = (BC, CC)[j] if j < 2 else XS + (j - 2) * P
                        for k in range(KD):
                            last = mm(pb[j % 2][:, :], win[:, k, col:col + P], xnT[:, k, :], start=(k == 0), stop=(k == KD - 1))
                        proj_mm.inc(last)
                    if 2 <= j < CT:
                        m = j - 2
                        if m >= 2:
                            at(gate_done, m - 1)
                        c, g = m // G, m % G
                        for k in range(KD):
                            last = mm(pb[2 + m % 2][:, :], xnT[:, k, c * P:(c + 1) * P], win[:, k, g * GF:(g + 1) * GF],
                                      start=(k == 0), stop=(k == KD - 1))
                        gate_mm.inc(last)
                    i = j - 1
                    if i == 0 or i >= 2:
                        q = 0 if i == 0 else i - 1
                        at(silu_done, i + 1)
                        if q >= 2:
                            at(xtok_done, q - 1)
                        src = BT[:, :] if i == 0 else xsf[i % 2]
                        for t in range(T):
                            last = transpose(pb[4 + q % 2][:, t * P:(t + 1) * P], src[:, t * P:(t + 1) * P])
                        xT_mm.inc(last)
                    if j == 3:
                        at(a_ready, 1)
                        for s, m in enumerate((upto_, after, ones)):
                            last = mm(pb[6][:, s * T * H:(s + 1) * T * H], m[:, :], a_[:, :, :].rearrange("p t h -> p (t h)"),
                                      start=True, stop=True)
                        dec_mm.inc(last)
                stage_end("pe", pe, b)

                def segment_sums(u):
                    at(rA_ready, u + 1)
                    for half in range(2):
                        if u >= 1:
                            at(L_ready, 2 * (u - 1) + half + 1)
                        seg_mm.inc(mm(pb[half][:, :], after[:, :], rA[u % 2][:, half * 4:half * 4 + 4, :].rearrange("p h i -> p (h i)"),
                                      start=True, stop=True))

                def products_bc(c):
                    if c >= 1:
                        at(cbm_ready, c)
                    cb_mm.inc(mm(pb[7][:, 0:P], BT[:, c * P:(c + 1) * P], CTm[:, c * P:(c + 1) * P], start=True, stop=True))

                def out_part(w):
                    c, g = w // G, w % G
                    at(gTs_ready, w + 1)
                    if g == 0 and c >= 1:
                        at(po_read, c)
                    for k in range(GK):
                        last = mm(pb[6][:, 0:D], gTs[w % 2][:, k, :], wout[:, g * GK + k, :],
                                  start=(g == 0 and k == 0), stop=(g == G - 1 and k == GK - 1))
                    out_mm.inc(last)

                products_bc(0)
                segment_sums(0)
                for u in range(UNITS + 2):
                    c, g = u // G, u % G
                    if u < UNITS:
                        if g == 3 and c + 1 < T:
                            products_bc(c + 1)
                        if u + 1 < UNITS:
                            segment_sums(u + 1)
                        if c > 0:
                            at(S_ready, u - G + 1)
                            if u > G:
                                at(yo_read, u - G)
                            yo_mm.inc(mm(pb[3][:, :], CTm[:, c * P:(c + 1) * P], S[:, g * GF:(g + 1) * GF], start=True, stop=True))
                        at(M_ready, u + 1)
                        at(xdt_ready, u + 1)
                        if u >= 1:
                            at(yd_read, u)
                        for h in range(GH):
                            last = mm(pb[2][:, h * HP:(h + 1) * HP], Lx[u % 2][:, h, :], xdt[u % 2][:, h * HP:(h + 1) * HP],
                                      start=True, stop=True)
                        yd_mm.inc(last)
                        if c < T - 1:
                            at(xde_ready, u + 1)
                            if u >= 1:
                                at(S_ready, u)
                            ds_mm.inc(mm(pb[4][:, :], btok[:, c, :], xde[u % 2], start=True, stop=True))
                    if 1 <= u <= UNITS:
                        w = u - 1
                        at(g_ready, w + 1)
                        if w >= 1:
                            at(gTs_ready, w)
                        for k in range(GK):
                            last = transpose(pb[5][:, k * P:(k + 1) * P], gb[w % 2][:, k * P:(k + 1) * P])
                        gT_mm.inc(last)
                    if u >= 2:
                        out_part(u - 2)
                stage_end("pe", pe, b)

                norm_T(1)
                for f in range(FT):
                    for side, w in enumerate((w1q, w2q)):
                        if f >= 2:
                            at(hid_done, f - 1)
                        for k in range(KD):
                            for part in (h_hi, h_lo):
                                last = mm(pb[2 + 2 * side + f % 2][:, :], w[:, k, f * P:(f + 1) * P], part[:, k, :],
                                          start=(k == 0 and part is h_hi), stop=(k == KD - 1 and part is h_lo))
                        up_mm.inc(last)
                at(hh_done, FT)
                at(hl_done, FT)
                for t in range(T):
                    for f in range(FT):
                        for part in (hh, hl):
                            last = mm(pb[6 + t // 2][:, (t % 2) * D:(t % 2 + 1) * D], part[:, f, t * P:(t + 1) * P], w3q[:, f, :],
                                      start=(f == 0 and part is hh), stop=(f == FT - 1 and part is hl))
                    down_mm.inc(last)
                stage_end("pe", pe, b)

                norm_T(2)
                at(late_loaded, len(row_loads))
                for g in range(AG):
                    for side, (w, m_, d_) in enumerate(((wq, q_mm, q_done), (wk, k_mm, k_done))):
                        if g >= 2:
                            at(d_, g - 1)
                        for k in range(KD):
                            last = mm(pb[2 + 2 * side + g % 2][:, :], w[:, k, g * P:(g + 1) * P], xnT[:, k, :],
                                      start=(k == 0), stop=(k == KD - 1))
                        m_.inc(last)
                for t in range(T):
                    for k in range(KD):
                        last = mm(pb[6 + t // 2][:, (t % 2) * D:(t % 2 + 1) * D], xnT[:, k, t * P:(t + 1) * P], wv[:, k, :],
                                  start=(k == 0), stop=(k == KD - 1))
                    v_mm.inc(last)
                stage_end("pe", pe, b)

                def scores(n):
                    t, h = n // AH, n % AH
                    g, s = h // 4, 32 * (h % 4)
                    bank = pb[(0, 1, 6)[n % 3]]
                    if n >= 3:
                        at(exp_done, n - 2)
                    mm(bank[:, 0:(t + 1) * P], qT[s:s + 32, g, t * P:(t + 1) * P], kT[s:s + 32, g, 0:(t + 1) * P], start=True, stop=False)
                    s_mm.inc(mm(bank[:, t * P:(t + 1) * P], identb[:, :], maskb[:, :], start=False, stop=True))

                def weighted_values(n):
                    t, h = n // AH, n % AH
                    if n % 2 == 1:
                        at(pT_act, (n + 1) // 2)
                    else:
                        at(pT_dve, n // 2 + 1)
                    if h == 0 and t >= 2:
                        at(o_done, t - 1)
                    for kb in range(t + 1):
                        last = mm(pb[4 + t % 2][:, h * AD:(h + 1) * AD], pT[n % 2][:, kb * P:(kb + 1) * P],
                                  vt[:, kb, h * AD:(h + 1) * AD], start=(kb == 0), stop=(kb == t))
                    pv_mm.inc(last)

                scores(0)
                scores(1)
                for n in range(AU + 1):
                    if n + 2 < AU:
                        scores(n + 2)
                    if n < AU:
                        at(exp_done, n + 1)
                        if n >= 2:
                            w = n - 2
                            if w % 2 == 1:
                                at(pT_act, (w + 1) // 2)
                            else:
                                at(pT_dve, w // 2 + 1)
                        for kb in range(n // AH + 1):
                            last = transpose(pb[2 + n % 2][:, kb * P:(kb + 1) * P], pr[n % 3][:, kb * P:(kb + 1) * P])
                        pT_mm.inc(last)
                    if n >= 1:
                        weighted_values(n - 1)
                at(o_done, T)
                for k in range(KD):
                    for t in range(T):
                        last = transpose(pb[2 + k][:, t * P:(t + 1) * P], yat[:, t, k * P:(k + 1) * P])
                    yT_mm.inc(last)
                at(yT_act, 1)
                at(yT_dve, 1)
                for t in range(T):
                    for k in range(KD):
                        last = mm(pb[t // 2][:, (t % 2) * D:(t % 2 + 1) * D], yT[:, k, t * P:(t + 1) * P], wo[:, k, :],
                                  start=(k == 0), stop=(k == KD - 1))
                wo_mm.inc(last)
                stage_end("pe", pe, b)

                norm_T(3)
                for t in range(T):
                    for k in range(KD):
                        last = mm(pb[2][:, t * E:(t + 1) * E], xnT[:, k, t * P:(t + 1) * P], gw[:, k, :],
                                  start=(k == 0), stop=(k == KD - 1))
                lg_mm.inc(last)
                at(late_loaded, len(row_loads))
                for f in range(ST):
                    if f >= 2:
                        at(sr_ready, f - 1)
                    for k in range(KD):
                        last = mm(pb[4 + f % 2][:, :], su[:, k, f * P:(f + 1) * P], xnT[:, k, :], start=(k == 0), stop=(k == KD - 1))
                    su_mm.inc(last)
                at(hs_ready, ST)
                for t in range(T):
                    for f in range(ST):
                        last = mm(pb[6 + t // 2][:, (t % 2) * D:(t % 2 + 1) * D], hs[:, f, t * P:(t + 1) * P], sd[:, f, :],
                                  start=(f == 0), stop=(f == ST - 1))
                sd_mm.inc(last)
                at(cum_ready, 1)
                for t in range(T):
                    mm(pb[3][:, t * E:(t + 1) * E], before[:, :], sel[:, t, :], start=True, stop=False)
                    last = mm(pb[3][:, t * E:(t + 1) * E], ones[:, :], cum[:, t, :], start=False, stop=True)
                pos_mm.inc(last)
                for t in range(T):
                    last = transpose(pb[2][0:E, t * P:(t + 1) * P], sel[:, t, :])
                selT_mm.inc(last)
                stage_end("pe", pe, b)

            pe.wait_ge(post_dve.sem, post_dve.upto(2 + 2 * (CAP // 8)))
            post_pe.inc(transpose(pb[6][:, 0:E], tokf[:, :, :].rearrange("e h s -> e (h s)"), E))
            y_mm.free_at_first(pe)

            def pairs(r, first):
                for i in range(WB):
                    pe.wait_ge(xd_loaded[i].sem, xd_loaded[i].upto(1, r))
                    if i >= 2 or not first:
                        pe.wait_ge(xdT_ready.sem, xdT_ready.upto(i - 1, r))
                    for k in range(KD):
                        last = transpose(pb[i % 2][:, k * P:(k + 1) * P], xd[i][:, k * P:(k + 1) * P])
                    xdT_mm.inc(last)
                    pe.wait_ge(wm_loaded[i].sem, wm_loaded[i].upto(2, r))
                    pe.wait_ge(xdT_ready.sem, xdT_ready.upto(i + 1, r))
                    if i >= 2 or not first:
                        pe.wait_ge(hr_ready.sem, hr_ready.upto(i - 1, r))
                    for e in range(2):
                        for k in range(KD):
                            last = mm(pb[2 + i % 2][:, e * CAP:(e + 1) * CAP], w1m[i][:, e, k, :], xdT[i % 2][:, k, e * CAP:(e + 1) * CAP],
                                      start=(k == 0), stop=(k == KD - 1))
                    h_mm.inc(last)
                    pe.wait_ge(hq_ready.sem, hq_ready.upto(i + 1, r))
                    if i >= 2 or not first:
                        pe.wait_ge(ys_ready.sem, ys_ready.upto(i - 1, r))
                    for e in range(2):
                        last = mm(pb[4 + i % 2][e * CAP:(e + 1) * CAP, 0:D], hq[i % 2][:, e * CAP:(e + 1) * CAP], w2m[i][:, e, :],
                                  start=True, stop=True)
                    y_mm.inc(last)
            for s in signals.values():
                s.new_trip()
            pairs(0, True)
            for s in signals.values():
                s.new_trip()
            with pe.Fori(1, PAIRS // WB) as r:
                pairs(r, False)

        @block.vector
        def _(dve):
            v = nc.vector
            dve.wait_ge(w_ffn_loaded.sem, 16 * len(ffn_loads))
            dve.wait_ge(w_rest_loaded.sem, 16 * len(rest_loads))
            v.memset(cum[:, 0, :], 0.0)
            v.memset(zrow, 0.0)
            v.tensor_copy(identb[:, :], ident[:, :])
            v.tensor_copy(maskb[:, :], maskf)
            dve.wait_ge(pro_pe.sem, 1)
            pro_dve.inc(v.tensor_scalar(thr, pb[7][:, 0:3], 1.0 / (FF * D), 1e-8, ALU.mult, ALU.add))
            dve.wait_ge(pro_dve.sem, 1)
            pro_dve.inc(v.tensor_scalar(nthr, thr, -0.5, None, ALU.mult))
            dve.wait_ge(pro_dve.sem, 2)
            pro_dve.inc(v.tensor_scalar(thr, thr, 0.5, None, ALU.mult))
            row_free.free_at_first(dve)

            with dve.Fori(0, B) as b:
                def at(s, k):
                    dve.wait_ge(s.sem, s.upto(k, b))

                def link(ins):
                    dstep.inc(ins)
                    at(dstep, dstep.count)

                def norm_stats(n):
                    for t in range(T):
                        last = v.bn_stats(stats[:, t, :], xb[:, t, :])
                    link(last)
                    settle(dve)
                    for t in range(T):
                        last = v.bn_aggr(mv[:, t, :], stats[:, t, :])
                    ln_stats.inc(last)
                    at(ln_std, n + 1)
                    link(v.reciprocal(rstd[:, :], std[:, :]))
                    for t in range(T):
                        last = v.tensor_scalar(xn[:, t, :], xb[:, t, :], mv[:, t, 0:1], rstd[:, t:t + 1], ALU.subtract, ALU.mult)
                    ln_xn.inc(last)

                def norm_T(n):
                    at(ln_T, 2 * n + 2)
                    ln_Td.inc(v.tensor_copy(xnT[:, 1, :], pb[1][:, :]))

                def heads(x, c, n=GH, width=HP):
                    return x.unsqueeze(2).to_broadcast([P, n, width])

                at(x_loaded, 1)
                norm_stats(0)
                norm_T(0)
                at(dt_mm, 1)
                link(v.tensor_tensor(v_dt[:, :, :], pb[7][:, 0:T * H].rearrange("p (t h) -> p t h", t=T),
                                     dtb[:, :].unsqueeze(1).to_broadcast([P, T, H]), ALU.add))
                dt_abs.inc(v.scalar_tensor_tensor(out=u_dt[:, :, :], in0=v_dt[:, :, :], scalar=-1.0, in1=v_dt[:, :, :],
                                                  op0=ALU.mult, op1=ALU.max))
                at(dt_log, 2)
                link(v.scalar_tensor_tensor(out=dt_[:, :, :], in0=v_dt[:, :, :], scalar=0.0, in1=l_dt[:, :, :], op0=ALU.max, op1=ALU.add))
                a_ready.inc(v.scalar_tensor_tensor(out=a_[:, :, :], in0=dt_[:, :, :], scalar=-1.0,
                                                   in1=expA[:, :].unsqueeze(1).to_broadcast([P, T, H]), op0=ALU.mult, op1=ALU.mult))
                for j in range(CT):
                    ci = (CT - 2 + j) if j < 2 else j - 2
                    at(tap3, j + 1)
                    cv, bank = conv[j % 2], pb[j % 2]
                    for s in (1, 2, 3):
                        ins = v.scalar_tensor_tensor(out=cv[:, s:L], in0=bank[:, 0:L - s], scalar=convw[:, ci, TAPS - 1 - s:TAPS - s],
                                                     in1=cv[:, s:L], op0=ALU.mult, op1=ALU.add)
                        if s < 3:
                            link(ins)
                        else:
                            conv_done.inc(ins)
                stage_end("dve", dve, b)

                def decay_products(u):
                    c, g = u // G, u % G
                    if g == 0:
                        at(cb_mm, c + 1)
                        if u >= 1:
                            at(M_ready, u)
                        cbm_ready.inc(v.tensor_tensor(cbm[:, :], pb[7][:, 0:P], upto_[:, :], ALU.mult))
                        at(cbm_ready, c + 1)
                    at(L_ready, 2 * u + 2)
                    M_ready.inc(v.tensor_tensor(Lx[u % 2], Lx[u % 2], cbm[:, :].unsqueeze(1).to_broadcast([P, GH, P]), ALU.mult))

                decay_products(0)
                for u in range(UNITS + 3):
                    c, g = u // G, u % G
                    if u + 1 < UNITS:
                        decay_products(u + 1)
                    if u < UNITS:
                        hs_ = slice(c * H + g * GH, c * H + (g + 1) * GH)
                        at(yd_mm, u + 1)
                        at(xD_ready, u + 1)
                        if u >= 1:
                            at(g_ready, u)
                        yd_read.inc(v.tensor_tensor(yb, pb[2][:, :], xD[u % 2], ALU.add))
                        if c > 0:
                            at(yo_mm, u - G + 1)
                            yo_read.inc(v.tensor_tensor(yo[:, :].rearrange("p (h w) -> p h w", h=GH), pb[3][:, :].rearrange("p (h w) -> p h w", h=GH),
                                                        heads(dec[:, 0, hs_], c), ALU.mult))
                        if c < T - 1:
                            at(ds_mm, u + 1)
                            if c == 0:
                                S_ready.inc(v.tensor_copy(S[:, g * GF:(g + 1) * GF], pb[4][:, :]))
                            else:
                                at(sx_ready, u - G + 1)
                                S_ready.inc(v.tensor_tensor(S[:, g * GF:(g + 1) * GF], pb[4][:, :], sx[u % 2], ALU.add))
                        at(yd_read, u + 1)
                        if c > 0:
                            at(yo_read, u - G + 1)
                            link(v.tensor_tensor(yb[:, :], yb[:, :], yo[:, :], ALU.add))
                        if u >= 2:
                            at(gT_mm, u - 1)
                            at(g_sq, u - 1)
                        g_ready.inc(v.tensor_tensor(gb[u % 2][:, :], yb[:, :], sz[:, c, g * GF:(g + 1) * GF], ALU.mult))
                    w = u - 2
                    if w >= 0 and w % G == G - 1:
                        at(out_mm, w + 1)
                        po_read.inc(v.tensor_copy(pob[:, w // G, :], pb[6][:, 0:D]))
                stage_end("dve", dve, b)

                ms_ready.inc(v.tensor_reduce(ms[:, :], ssq[:, :, :], AX.X, ALU.add))
                at(rms_std, 1)
                link(v.reciprocal(rstd[:, :], std[:, :]))
                for t in range(T):
                    last = v.scalar_tensor_tensor(out=xb[:, t, :], in0=pob[:, t, :], scalar=rstd[:, t:t + 1], in1=xb[:, t, :],
                                                  op0=ALU.mult, op1=ALU.add)
                link(last)
                norm_stats(1)
                at(ln_Ta, 2)
                for k in range(KD):
                    last = v.tensor_tensor(h_lo[:, k, :], pb[k][:, :], h_hi[:, k, :], ALU.subtract)
                ln_Td.inc(last)
                for f in range(FT):
                    at(up_mm, 2 * f + 2)
                    at(sig_done, f + 1)
                    if f >= 2:
                        at(hh_done, f - 1)
                        at(hl_done, f - 1)
                    hid_done.inc(v.tensor_tensor(hid[f % 2], pb[4 + f % 2][:, :], sg[f % 2], ALU.mult))
                    at(hh_done, f + 1)
                    hl_done.inc(v.tensor_tensor(hl[:, f, :], hid[f % 2], hh[:, f, :], ALU.subtract))
                for q in range(2):
                    at(down_mm, 2 * q + 2)
                    last = v.tensor_tensor(xb[:, 2 * q:2 * q + 2, :], pb[6 + q][:, :].rearrange("p (t n) -> p t n", t=2),
                                           xb[:, 2 * q:2 * q + 2, :], ALU.add)
                link(last)
                stage_end("dve", dve, b)

                norm_stats(2)
                norm_T(2)
                at(late_loaded, len(row_loads))
                for g in range(AG):
                    at(q_mm, g + 1)
                    q_done.inc(v.scalar_tensor_tensor(out=qT[:, g, :], in0=pb[2 + g % 2][:, :], scalar=AD ** -0.5, in1=qadd[:, g, :],
                                                      op0=ALU.mult, op1=ALU.add))
                    at(k_mm, g + 1)
                    k_done.inc(v.tensor_tensor(kT[:, g, :], pb[4 + g % 2][:, :], kadd[:, :], ALU.add))
                stage_end("dve", dve, b)

                def values_norm(t):
                    at(pv_mm, (t + 1) * AH)
                    link(v.reciprocal(rsums[:, t * AH:(t + 1) * AH], psums[:, t * AH:(t + 1) * AH]))
                    o_done.inc(v.tensor_tensor(yat[:, t, :].rearrange("p (h w) -> p h w", h=AH),
                                               pb[4 + t % 2][:, 0:D].rearrange("p (h w) -> p h w", h=AH),
                                               heads(rsums[:, t * AH:(t + 1) * AH], t, AH, AD), ALU.mult))

                for n in range(AU + 1):
                    if n < AU:
                        cols = (n // AH + 1) * P
                        at(s_mm, n + 1)
                        max_done.inc(v.tensor_reduce(nmax[:, n:n + 1], pb[(0, 1, 6)[n % 3]][:, 0:cols], AX.X, ALU.max, negate=True))
                    w = n - 1
                    if w >= 0 and w % 2 == 0:
                        cols = (w // AH + 1) * P
                        at(pT_mm, w + 1)
                        if w >= 2:
                            at(pv_mm, w - 1)
                        pT_dve.inc(v.tensor_copy(pT[w % 2][:, 0:cols], pb[2 + w % 2][:, 0:cols]))
                    if n >= AH + 2 and (n - 2) % AH == 0:
                        values_norm((n - 2) // AH - 1)
                values_norm(T - 1)
                at(yT_mm, 2)
                yT_dve.inc(v.tensor_copy(yT[:, 1, :], pb[3][:, :]))
                at(wo_mm, 1)
                for q in range(2):
                    last = v.tensor_tensor(xb[:, 2 * q:2 * q + 2, :], pb[q][:, :].rearrange("p (t n) -> p t n", t=2),
                                           xb[:, 2 * q:2 * q + 2, :], ALU.add)
                link(last)
                stage_end("dve", dve, b)

                norm_stats(3)
                norm_T(3)
                at(sc_ready, 1)
                link(v.tensor_tensor(sbi, sc, ebias[:, :].unsqueeze(1).to_broadcast([P, T, E]), ALU.add))
                settle(dve)
                for t in range(T):
                    for g in range(NG):
                        last = v.max(m8[:, t, g, :], sbi[:, t, g * EG:(g + 1) * EG])
                link(last)
                link(v.tensor_tensor(grp, m8[:, :, :, 0], m8[:, :, :, 1], ALU.add))
                settle(dve)
                for t in range(T):
                    last = v.max(gm8[:, t, :], grp[:, t, :])
                link(last)
                settle(dve)
                for t in range(T):
                    last = v.max_index(gi[:, t, :], gm8[:, t, :], grp[:, t, :])
                link(last)
                link(v.tensor_copy(gif, gi))
                link(v.tensor_tensor(goh, iota8[:, :].unsqueeze(1).unsqueeze(3).to_broadcast([P, T, NG, TKG]),
                                     gif[:, :, 0:TKG].unsqueeze(2).to_broadcast([P, T, NG, TKG]), ALU.is_equal))
                link(v.tensor_reduce(gmask.rearrange("p (t g) -> p t g", t=T), goh, AX.X, ALU.add))
                link(v.tensor_scalar(gmask, gmask, BIG, -BIG, ALU.mult, ALU.add))
                link(v.tensor_tensor(masked.rearrange("p (n e) -> p n e", e=EG), sbi.rearrange("p t (g e) -> p (t g) e", e=EG),
                                     gmask.unsqueeze(2).to_broadcast([P, T * NG, EG]), ALU.add))
                mk = masked.rearrange("p (t e) -> p t e", t=T)
                settle(dve)
                for t in range(T):
                    last = v.max(em8[:, t, :], mk[:, t, :])
                link(last)
                settle(dve)
                for t in range(T):
                    last = v.max_index(ei[:, t, :], em8[:, t, :], mk[:, t, :])
                link(last)
                link(v.tensor_copy(eif, ei))
                link(v.tensor_tensor(eoh, iota64[:, :].unsqueeze(1).unsqueeze(3).to_broadcast([P, T, E, TOPK]),
                                     eif[:, :, 0:TOPK].unsqueeze(2).to_broadcast([P, T, E, TOPK]), ALU.is_equal))
                sel_ready.inc(v.tensor_reduce(sel, eoh, AX.X, ALU.add))
                at(sel_ready, 1)
                for t in range(T):
                    ins = v.tensor_tensor(cum[:, t + 1, :], cum[:, t, :], sel[:, t, :], ALU.add)
                    if t < T - 1:
                        link(ins)
                    else:
                        cum_ready.inc(ins)
                link(v.tensor_tensor(wsel, sc, sel, ALU.mult))
                link(v.tensor_reduce(wsum, wsel, AX.X, ALU.add))
                link(v.tensor_scalar(wsum, wsum, 1e-20, None, ALU.add))
                link(v.reciprocal(wrec, wsum))
                for t in range(T):
                    last = v.tensor_scalar(wsel[:, t, :], wsel[:, t, :], wrec[:, t:t + 1], SCALE, ALU.mult, ALU.mult)
                w_ready.inc(last)
                at(pos_mm, 1)
                ppos = pb[3][:, 0:T * E]
                link(v.scalar_tensor_tensor(out=kept, in0=ppos, scalar=float(CAP), in1=sel.rearrange("p t e -> p (t e)"),
                                            op0=ALU.is_lt, op1=ALU.mult))
                link(v.tensor_tensor(sid.rearrange("p (t e) -> p t e", t=T), ppos.rearrange("p (t e) -> p t e", t=T),
                                     slot0[:, :].unsqueeze(1).to_broadcast([P, T, E]), ALU.add))
                link(v.tensor_tensor(sid, sid, kept, ALU.mult))
                settle(dve)
                for t in range(T):
                    last = v.max(s8[:, t, :], sid[:, t * E:(t + 1) * E])
                link(last)
                link(v.tensor_copy(slots[:, bass.ds(b * T, T), :], s8))
                at(selT_mm, 1)
                link(v.tensor_copy(selT[:, bass.ds(b * L, L)], pb[2][0:E, :]))
                v.tensor_copy(cum[:, 0, :], cum[:, T, :])
                at(sd_mm, 1)
                for q in range(2):
                    last = v.tensor_tensor(xb[:, 2 * q:2 * q + 2, :], pb[6 + q][:, :].rearrange("p (t n) -> p t n", t=2),
                                           xb[:, 2 * q:2 * q + 2, :], ALU.add)
                out_ready.inc(last)
                dve.wait_ge(stored.sem, stored.upto(3, b))
                stage_end("dve", dve, b)
                settle(dve)
                row_free.inc(dve.drain())

            def link(ins):
                post_dve.inc(ins)
                dve.wait_ge(post_dve.sem, post_dve.upto(post_dve.count))

            dve.wait_ge(tokval_loaded.sem, 16)
            link(v.tensor_tensor(ranked, selT[:, :], tokval, ALU.mult))
            for r in range(CAP // 8):
                link(v.max(top[:, r * 8:(r + 1) * 8], ranked))
                link(v.match_replace(ranked, top[:, r * 8:(r + 1) * 8], ranked, 0.0))
            link(v.tensor_scalar(tokf[:, :, :], top[:, :].unsqueeze(1).to_broadcast([E, 2, CAP]), -1.0, float(NTOK), ALU.mult, ALU.add))
            dve.wait_ge(post_pe.sem, 1)
            v.tensor_copy(gidx[0:CAP, :], pb[6][0:CAP, 0:PAIRS])
            idx_ready.inc(v.tensor_copy(gidx[CAP:2 * CAP, :], pb[6][CAP:2 * CAP, PAIRS:2 * PAIRS]))
            fin_ready.free_at_first(dve)

            def pairs(r, first):
                for i in range(WB):
                    dve.wait_ge(xdT_mm.sem, xdT_mm.upto(i + 1, r))
                    if i >= 2 or not first:
                        dve.wait_ge(h_mm.sem, h_mm.upto(i - 1, r))
                    xdT_ready.inc(v.tensor_copy(xdT[i % 2].rearrange("p k s -> p (k s)"), pb[i % 2][:, 0:KD * P]))
                    dve.wait_ge(hr_ready.sem, hr_ready.upto(i + 1, r))
                    if i >= 2 or not first:
                        dve.wait_ge(y_mm.sem, y_mm.upto(i - 1, r))
                    hq_ready.inc(v.tensor_tensor(hq[i % 2], hr[i % 2], hr[i % 2], ALU.mult))
            for s in signals.values():
                s.new_trip()
            pairs(0, True)
            for s in signals.values():
                s.new_trip()
            with dve.Fori(1, PAIRS // WB) as r:
                pairs(r, False)

            def finish(r, first):
                for i in range(4):
                    dve.wait_ge(yg_loaded[i].sem, yg_loaded[i].upto(TOPK, r))
                    if not first:
                        dve.wait_ge(fin_stored[i].sem, r * 16)
                    dfin.inc(v.tensor_reduce(fin[i], yg[i].rearrange("p k n -> p n k"), AX.X, ALU.add))
                    dve.wait_ge(dfin.sem, dfin.upto(i + 1, r))
                    dve.wait_ge(bt_loaded[i].sem, bt_loaded[i].upto(1, r))
                    fin_ready.inc(v.tensor_tensor(fin[i], fin[i], bt[i], ALU.add))
            for s in signals.values():
                s.new_trip()
            finish(0, True)
            for s in signals.values():
                s.new_trip()
            with dve.Fori(1, NTOK // P // 4) as r:
                finish(r, False)

        @block.gpsimd
        def _(pool):
            p = nc.gpsimd
            pool.wait_ge(pro_dve.sem, 3)
            zeros_stored.inc(pool.dma_start(xg[NTOK:NTOK + 1, :], zrow))
            zeros_stored.inc(pool.dma_start(ytab[0:1, :], zrow[:, 0:D]))
            k = 0
            for i in range(3):
                p.tensor_scalar(low, wf[i], nthr[:, i:i + 1], None, ALU.is_lt)
                pro_pool.inc(p.tensor_scalar(wf[i], wf[i], thr[:, i:i + 1], None, ALU.is_gt))
                k += 1
                pool.wait_ge(pro_pool.sem, k)
                pro_pool.inc(p.tensor_tensor(wt[i], wf[i], low, ALU.subtract))
                k += 1
                pool.wait_ge(pro_pool.sem, k)
            for kk in range(INTER // P):
                p.tensor_scalar(wout[:, kk, :], wout[:, kk, :], normw[:, kk:kk + 1], None, ALU.mult)

            pool.wait_ge(zeros_stored.sem, 32)

            with pool.Fori(0, B) as b:
                def at(s, k):
                    pool.wait_ge(s.sem, s.upto(k, b))

                def heads(x):
                    return x.unsqueeze(2).to_broadcast([P, GH, HP])

                def by_head(x):
                    return x.rearrange("p (h w) -> p h w", h=GH)

                stage_end("pool", pool, b)
                for u in range(UNITS):
                    c, g = u // G, u % G
                    hs_ = slice(g * GH, (g + 1) * GH)
                    dh = slice(c * H + g * GH, c * H + (g + 1) * GH)
                    xs = by_head(xtok[:, c, g * GF:(g + 1) * GF])
                    if u >= 2:
                        at(yd_mm, u - 1)
                        at(xde_ready, min(u - 1, (T - 1) * G))
                    xdt_ready.inc(p.tensor_tensor(by_head(xdt[u % 2]), xs, heads(dt_[:, c, hs_]), ALU.mult))
                    if c < T - 1:
                        at(xdt_ready, u + 1)
                        if u >= 2:
                            at(ds_mm, u - 1)
                        xde_ready.inc(p.tensor_tensor(by_head(xde[u % 2]), by_head(xdt[u % 2]), heads(dec[:, 1, dh]), ALU.mult))
                    if u >= 2:
                        at(yd_read, u - 1)
                    xD_ready.inc(p.tensor_tensor(by_head(xD[u % 2]), xs, heads(dpar[:, hs_]), ALU.mult))
                    if 0 < c < T - 1:
                        at(S_ready, max(u - 4, u - 2) + 1)
                        sx_ready.inc(p.tensor_tensor(by_head(sx[u % 2]), by_head(S[:, g * GF:(g + 1) * GF]), heads(dec[:, 2, dh]), ALU.mult))
                stage_end("pool", pool, b)
                stage_end("pool", pool, b)
                stage_end("pool", pool, b)
                stage_end("pool", pool, b)
                for f in range(ST):
                    at(sr_ready, f + 1)
                    hs_ready.inc(p.tensor_tensor(hs[:, f, :], sr[f % 2], sr[f % 2], ALU.mult))
                stage_end("pool", pool, b)

            pool.wait_ge(stored.sem, 16 * 3 * B)
            pool.wait_ge(idx_ready.sem, 1)
            with pool.Fori(0, PAIRS // WB) as r:
                for i in range(WB):
                    pool.wait_ge(ys_ready.sem, ys_ready.upto(i + 1 - WB, r))
                    pcol.inc(p.tensor_copy(gcol[i][:, :], gidx[:, bass.ds(r * WB + i, 1)]))
                    pool.wait_ge(pcol.sem, pcol.upto(i + 1, r))
                    settle(pool)
                    xd_loaded[i].inc(p.indirect_dma_start(xd[i], None, xg, bass.IndirectOffsetOnAxis(ap=gcol[i][:, :], axis=0)))
            for i in range(4):
                pool.wait_ge(y_stored[i].sem, 32 * (PAIRS // WB))
            with pool.Fori(0, NTOK // P // 4) as r:
                for i in range(4):
                    pool.wait_ge(fin_ready.sem, fin_ready.upto(i + 1 - 4, r))
                    xcol.inc(p.tensor_copy(scol[i][:, :], slots[:, bass.ds(r * 4 + i, 1), :].rearrange("p t k -> p (t k)")))
                    pool.wait_ge(xcol.sem, xcol.upto(i + 1, r))
                    settle(pool)
                    for k in range(TOPK):
                        yg_loaded[i].inc(p.indirect_dma_start(yg[i][:, k, :], None, ytab,
                                                              bass.IndirectOffsetOnAxis(ap=scol[i][:, k:k + 1], axis=0)))
        return {n: s.most for n, s in signals.items()}


def constants():
    r = np.arange(P)
    upto = (r[:, None] <= r[None, :]).astype(np.float32)
    q, k = np.arange(L, dtype=np.float32), np.arange(L, dtype=np.float32)
    slopes = (2.0 ** (-8.0 / np.arange(1, AH + 1, dtype=np.float32))).astype(np.float32)
    qadd, kadd = np.zeros((P, AG, L), np.float32), np.zeros((P, L), np.float32)
    for h in range(AH):
        g, s = h // 4, 32 * (h % 4)
        qadd[s + AD, g] = -slopes[h] * q
        qadd[s + AD + 1, g] = slopes[h]
    for s in range(0, P, 32):
        kadd[s + AD], kadd[s + AD + 1] = 1.0, k
    rep = lambda v: np.ascontiguousarray(np.broadcast_to(np.asarray(v, np.float32), (P, len(v))))
    return dict(ident=np.eye(P, dtype=np.float32), upto=upto, after=np.ascontiguousarray(1 - upto),
                before=(upto - np.eye(P, dtype=np.float32)), ones=np.ones((P, P), np.float32),
                mask=np.where(r[None, :] > r[:, None], -BIG, 0.0).astype(np.float32), qadd=qadd, kadd=kadd,
                iota8=rep(np.arange(NG)), iota64=rep(np.arange(E)), slot0=rep(1 + CAP * np.arange(E)),
                eps=np.full((P, 1), EPS, np.float32),
                tokval=np.ascontiguousarray(np.broadcast_to(NTOK - np.arange(NTOK, dtype=np.float32), (E, NTOK))))


def layouts(i):
    def tiles(w):
        return np.ascontiguousarray(w.reshape(-1, P, w.shape[1]).transpose(1, 0, 2))

    def strips(w):
        out = np.zeros((D, AH, 32), np.float32)
        out[:, :, :AD] = w.reshape(D, AH, AD)
        return tiles(out.reshape(D, AH * 32))

    def padded(w, rows, cols):
        out = np.zeros((rows, cols), np.float32)
        out[:w.shape[0], :w.shape[1]] = w
        return out

    def rep(v):
        return np.ascontiguousarray(np.broadcast_to(v, (P, len(v))))

    flat = lambda w: np.ascontiguousarray(w.reshape(P, -1))
    wqkv = i["L1_attn_W_qkv"]
    return dict(
        x=np.ascontiguousarray(i["L0_attn_hidden_states"]), win=tiles(i["L0_attn_W_in"].T),
        convw=np.ascontiguousarray(i["L0_attn_conv_w"].reshape(CT, P, TAPS).transpose(1, 0, 2)),
        convb=np.ascontiguousarray(i["L0_attn_conv_b"].reshape(CT, P).T),
        dtb=rep(i["L0_attn_dt_bias"]), alog=rep(i["L0_attn_A_log"]), dpar=rep(i["L0_attn_D_param"]),
        normw=np.ascontiguousarray(i["L0_attn_norm_w"].reshape(-1, P).T), wout=tiles(i["L0_attn_W_out"].T),
        w1=flat(tiles(padded(i["L0_ffn_w1"].T, D, FT * P))), w2=flat(tiles(padded(i["L0_ffn_w2"].T, D, FT * P))),
        w3=flat(tiles(padded(i["L0_ffn_w3"].T, FT * P, D))),
        wq=strips(wqkv[:, 0:D]), wk=strips(wqkv[:, D:2 * D]), wv=tiles(wqkv[:, 2 * D:]), wo=tiles(i["L1_attn_W_o"]),
        gw=tiles(i["L1_ffn_gate_w"].T), ebias=rep(i["L1_ffn_e_bias"]),
        su=tiles(i["L1_ffn_shared_up_w"].T), sd=tiles(i["L1_ffn_shared_down_w"].T),
        w1m=np.ascontiguousarray(i["L1_ffn_w1"].reshape(E, P, KD, P).transpose(0, 3, 2, 1)),
        w2m=np.ascontiguousarray(i["L1_ffn_w2"].transpose(0, 2, 1)))


def kernel(**inputs):
    from concourse import bacc
    from concourse.bass_utils import run_bass_kernel_spmd

    arrays = {**layouts({k: np.asarray(v) for k, v in inputs.items()}), **constants()}

    def program(per_trip):
        nc = bacc.Bacc("TRN2", target_bir_lowering=False, num_devices=1)
        aps = {n: nc.dram_tensor(f"in_{n}", x.shape, F32, kind="ExternalInput").ap() for n, x in arrays.items()}
        aps["out"] = nc.dram_tensor("out", (B, L, D), F32, kind="ExternalOutput").ap()
        return nc, build(nc, aps, per_trip)

    _, counts = program({})
    nc, again = program(counts)
    assert counts == again
    r = run_bass_kernel_spmd(nc, [{f"in_{n}": x for n, x in arrays.items()}], core_ids=[0])
    return r.results[0]["out"]
```

```python
from contextlib import ExitStack

import numpy as np
import concourse.bass as bass
from concourse import mybir

ALU = mybir.AluOpType
ACT = mybir.ActivationFunctionType
AX = mybir.AxisListType
F32 = mybir.dt.float32
F16 = mybir.dt.float16
BF16 = mybir.dt.bfloat16
U32 = mybir.dt.uint32

P = 128
B, L, D = 4, 512, 256
T = L // P
KD = D // P
NTOK = B * L
H, HP, N = 32, 64, 128
INTER = H * HP
TAPS = 4
XS, BC, CC, DTC = INTER, 2 * INTER, 2 * INTER + N, 2 * INTER + 2 * N
PROJ = DTC + H
CT = (INTER + 2 * N) // P
G = 4
GH = H // G
GF = INTER // G
GK = GF // P
UNITS = T * G
FF = 704
FT = (FF + P - 1) // P
AH, AD = 16, 16
MROWS, BROWS = 3, 12
QPARTS, KPARTS = (0, 0, 1, 1, 0, 2), (0, 1, 0, 1, 2, 0)
ROWS = BROWS + len(QPARTS) * AD
AV = 2 * AD
AQ = 4
AGROUPS = [(t, q) for half in range(2) for t in range(T) for q in range(half * 2, half * 2 + 2)]
AUNITS = [(g, t, q * AQ + h, T // (t + 1) or 1) for g, (t, q) in enumerate(AGROUPS)
          for h in range(0, AQ, T // (t + 1) or 1)]
E, TOPK, NG, TKG, CAP = 64, 6, 8, 4, 64
EG = E // NG
SCALE = 2.5
SH = 512
ST = SH // P
XW = D + E + 1
PAIRS = E // 2
SUMS = 4
CONSTS = dict(ident=P, upto=P, after=P, before=P, ones=P, iota8=NG, iota64=E, slot0=E, noslot=T * 8, sum0=2,
              tokid=NTOK // P, empty=1, eps=1)
PARAMS = dict(convw=CT * TAPS, convb=CT, dtb=H, alog=H, dpar=H, normw=INTER // P, gw=KD * E, ebias=E)
EPS = 1e-5
BIG = 1e30


class Signal:

    def __init__(self, sem, step, per_trip, start):
        self.sem, self.step, self.per_trip, self.start = sem, step, per_trip, start
        self.count = self.most = 0

    def inc(self, instruction):
        self.count += 1
        self.most = max(self.most, self.count)
        instruction.then_inc(self.sem, self.step)

    def new_trip(self):
        self.count = 0

    def free_at_first(self, engine):
        for _ in range(self.start):
            engine.drain().then_inc(self.sem, self.step)

    def upto(self, k, b=None):
        value = (self.start + k) * self.step
        return value if b is None else b * (self.per_trip * self.step) + value


def build(nc, a, per_trip):
    with ExitStack() as ctx:
        signals = {}

        def sb(name, shape, dt=F32):
            return ctx.enter_context(nc.sbuf_tensor(name, shape, dt))

        def signal(name, step=1, start=0):
            s = Signal(ctx.enter_context(nc.semaphore(name)), step, per_trip.get(name, 0), start)
            signals[name] = s
            return s

        pb = [ctx.enter_context(nc.psum_tensor(f"bank{i}", [P, 512], F32)) for i in range(8)]

        xslot = nc.dram_tensor("xslot", (1 + E * CAP + T * TOPK * P, XW), F32).ap()
        acc = nc.dram_tensor("acc", (SUMS * (NTOK + CAP), D), F32).ap()

        win = sb("win", [P, KD, PROJ])
        wout = sb("wout", [P, INTER // P, D])
        small = {}
        for group, fields in (("consts", CONSTS), ("params", PARAMS)):
            whole = small[group] = sb(group, [P, sum(fields.values())])
            first = 0
            for name, width in fields.items():
                small[name] = whole[:, first:first + width]
                first += width
        convw = small["convw"].rearrange("p (c t) -> p c t", c=CT)
        convb, dtb, expA, dpar, normw = (small[n] for n in ("convb", "dtb", "alog", "dpar", "normw"))
        gw = small["gw"].rearrange("p (k e) -> p k e", k=KD)
        ebias, ident, ones, iota8, iota64 = (small[n] for n in ("ebias", "ident", "ones", "iota8", "iota64"))
        upto_ = small["upto"]
        after = small["after"]
        before = small["before"]
        slot0 = small["slot0"]
        noslot = small["noslot"]
        sum0 = small["sum0"]
        tokid, eps = small["tokid"], small["eps"]
        w1q = sb("w1q", [P, KD, FT * P], F16)
        w2q = sb("w2q", [P, KD, FT * P], F16)
        w3q = sb("w3q", [P, FT, D], F16)
        identb = sb("identb", [P, P], BF16)
        maskb = sb("maskb", [P, P], BF16)
        maskTb = sb("maskTb", [P, P], BF16)
        cum = sb("cum", [P, T + 1, E])

        xrow = sb("xrow", [P, T, XW])
        xb = sb("xb", [P, T, D])
        xn = sb("xn", [P, T, D])
        xnT = sb("xnT", [P, KD, L])
        stats = sb("stats", [P, T, 6])
        mv = sb("mv", [P, T, 2])
        vare = sb("vare", [P, T])
        power = sb("power", [P, T])
        rms = sb("rms", [P, T])
        warm_out = sb("warm_out", [1, 16])
        rstd = sb("rstd", [P, T])

        pool_a = sb("pool_a", [P, T * INTER])
        pool_b = sb("pool_b", [P, T * INTER])
        pool_c = sb("pool_c", [P, 8192])
        xtok = pool_a[:, :].rearrange("p (t f) -> p t f", t=T)
        sz = pool_b[:, :].rearrange("p (t f) -> p t f", t=T)

        def carve(buf, at, n, dt=F32):
            ap = buf[:, at:at + n]
            return ap if dt == F32 else ap.bitcast(dt)

        conv = [carve(pool_c, i * 512, 512) for i in range(2)]
        xsf = [carve(pool_c, 1024 + i * 512, 512) for i in range(2)]
        rA = [carve(pool_c, 2048 + i * 1024, 1024).rearrange("p (h i) -> p h i", h=GH) for i in range(2)]
        Lx = [carve(pool_c, i * 1024, 1024).rearrange("p (h i) -> p h i", h=GH) for i in range(2)]
        xdt = [carve(pool_c, 4096 + i * 512, 512) for i in range(2)]
        xde = [carve(pool_c, 5120 + i * 512, 512) for i in range(2)]
        xD = [carve(pool_c, 6144 + i * 512, 512) for i in range(2)]
        sx = [carve(pool_c, 7168 + i * 512, 512) for i in range(2)]
        BT = sb("BT", [P, L])
        CTm = sb("CTm", [P, L])
        btok = sb("btok", [P, T, N])
        v_dt = sb("v_dt", [P, T, H])
        u_dt = sb("u_dt", [P, T, H])
        l_dt = sb("l_dt", [P, T, H])
        dt_ = sb("dt_", [P, T, H])
        a_ = sb("a_", [P, T, H])
        dec = sb("dec", [P, 3, T * H])
        cbm = sb("cbm", [P, P])
        S = sb("S", [P, INTER])
        yb, yo = xn[:, 0:2, :].rearrange("p t n -> p (t n)"), xn[:, 2:4, :].rearrange("p t n -> p (t n)")
        gb = [xnT[:, i, :] for i in range(2)]
        gTs = [sb(f"gTs{i}", [P, GK, P]) for i in range(2)]
        ssq = sb("ssq", [P, T, G])
        ms = sb("ms", [P, T])
        pob = sb("pob", [P, T, D])
        junk = sb("junk", [P, 512], BF16)

        h_hi = carve(pool_c, 0, 512, F16).rearrange("p (k n) -> p k n", k=KD)
        h_lo = carve(pool_c, 512, 512, F16).rearrange("p (k n) -> p k n", k=KD)
        sg = [carve(pool_c, 1024 + i * 512, 512) for i in range(2)]
        hid = [carve(pool_c, 2048 + i * 512, 512) for i in range(2)]
        hh = carve(pool_c, 3072, FT * 256, F16).rearrange("p (f n) -> p f n", f=FT)
        hl = carve(pool_c, 3072 + FT * 256, FT * 256, F16).rearrange("p (f n) -> p f n", f=FT)

        qks = carve(pool_a, 0, AH * L, BF16).rearrange("p (h s n) -> p h s n", s=2, h=AH)
        qs, ks = qks[:, :, 0], qks[:, :, 1]
        parts = [carve(pool_b, i * 1536, 1536, BF16).rearrange("p (s n) -> p s n", s=6) for i in range(2)]
        rest = [carve(pool_b, 3072 + i * L, L) for i in range(2)]
        vt = carve(pool_b, 4096, T * AH * AV).rearrange("p (t h n) -> p t h n", t=T, h=AH)
        pT = [carve(pool_c, i * 512, 512) for i in range(3)]
        oT = [carve(pool_c, 3584 + i * P, P) for i in range(2)]
        yat = carve(pool_c, 1536, T * D).rearrange("p (t n) -> p t n", t=T)
        yT = carve(pool_c, 2560, KD * L).rearrange("p (k n) -> p k n", k=KD)
        wq = carve(pool_c, 6144, KD * D).rearrange("p (k n) -> p k n", k=KD)
        wk = carve(pool_c, 6656, KD * D).rearrange("p (k n) -> p k n", k=KD)
        wv = carve(pool_c, 7168, KD * D).rearrange("p (k n) -> p k n", k=KD)
        wo = carve(pool_c, 7680, KD * D).rearrange("p (k n) -> p k n", k=KD)
        nmax = sb("nmax", [P, T * AH])
        mrest = sb("mrest", [P, AQ])
        mparts = [sb(f"mparts{i}", [P, AQ, MROWS], BF16) for i in range(2)]
        rsums = sb("rsums", [P, AQ])

        sc = carve(pool_c, 0, 256).rearrange("p (t e) -> p t e", t=T)
        sbi = carve(pool_c, 256, 256).rearrange("p (t e) -> p t e", t=T)
        m8 = carve(pool_c, 512, 256).rearrange("p (t g m) -> p t g m", t=T, g=NG)
        grp = carve(pool_c, 768, 32).rearrange("p (t g) -> p t g", t=T)
        gm8 = carve(pool_c, 800, 32).rearrange("p (t g) -> p t g", t=T)
        gi = carve(pool_c, 832, 32, U32).rearrange("p (t g) -> p t g", t=T)
        gif = carve(pool_c, 864, 32).rearrange("p (t g) -> p t g", t=T)
        goh = carve(pool_c, 896, 128).rearrange("p (t g k) -> p t g k", t=T, g=NG)
        gmask = carve(pool_c, 1024, 32)
        em8 = carve(pool_c, 1056, 32).rearrange("p (t g) -> p t g", t=T)
        ei = carve(pool_c, 1088, 32, U32).rearrange("p (t g) -> p t g", t=T)
        eif = carve(pool_c, 1120, 32).rearrange("p (t g) -> p t g", t=T)
        wsum = carve(pool_c, 1152, 4)
        wrec = carve(pool_c, 1156, 4)
        s8 = carve(pool_c, 1160, 32).rearrange("p (t g) -> p t g", t=T)
        masked = carve(pool_c, 1280, 256)
        sel = carve(pool_c, 1536, 256).rearrange("p (t e) -> p t e", t=T)
        wsel = xrow[:, :, D:D + E]
        kept = carve(pool_c, 2048, 256)
        sid = carve(pool_c, 2304, 256)
        eoh = carve(pool_c, 2560, T * E * TOPK).rearrange("p (t e k) -> p t e k", t=T, e=E)
        sr = [carve(pool_b, i * 512, 512) for i in range(2)]
        su = carve(pool_b, 6144, KD * SH).rearrange("p (k n) -> p k n", k=KD)
        sd = carve(pool_b, 7168, ST * D).rearrange("p (k n) -> p k n", k=ST)
        xnext = carve(pool_b, 5120, T * D).rearrange("p (t n) -> p t n", t=T)
        hs = carve(pool_b, 1024, ST * L).rearrange("p (f n) -> p f n", f=ST)
        nos = carve(pool_c, 5760, 32)
        slots = sb("slots", [P, T, 8], U32)

        WB = 8
        w1m = [carve(pool_a, i * 512, 512).rearrange("p (e k i) -> p e k i", e=2, k=KD) for i in range(WB)]
        w2m = [carve(pool_a, 4096 + i * 512, 512).rearrange("p (e n) -> p e n", e=2) for i in range(WB)]
        xd = [carve(pool_b, i * XW, XW) for i in range(WB)]
        xdT = [carve(pool_b, 2592 + i * 256, 256).rearrange("p (k s) -> p k s", k=KD) for i in range(2)]
        hr = [carve(pool_b, 3104 + i * P, P) for i in range(2)]
        hq = [carve(pool_b, 3360 + i * P, P) for i in range(2)]
        ys = [carve(pool_b, 3616 + i * D, D) for i in range(WB)]
        target = [sb(f"target{i}", [P, 1], U32) for i in range(WB)]
        part_sum = [[carve((pool_c, pool_a)[i // 2], (i % 2 * SUMS + s) * T * D, T * D) for s in range(SUMS)] for i in range(B)]

        w_in_loaded = [signal(f"w_in_loaded{i}", 16) for i in range(2)]
        w_small_loaded = signal("w_small_loaded", 16)
        w_out_loaded = signal("w_out_loaded", 16)
        w_ffn_loaded = signal("w_ffn_loaded", 16)
        empty_stored = signal("empty_stored", 16)
        pro_act = signal("pro_act")
        pro_pe = signal("pro_pe")
        pro_dve = signal("pro_dve")
        pro_pool = signal("pro_pool")
        x_loaded = signal("x_loaded", 16)
        late_loaded = signal("late_loaded", 16)
        xnext_loaded = signal("xnext_loaded", 16, start=1)
        rows_done = signal("rows_done")
        stored = signal("stored", 16)
        stage = {n: signal(f"stage_{n}") for n in ("pe", "act", "dve", "pool")}
        dstep = signal("dstep", start=T)
        settled = signal("settled")
        pstep = signal("pstep", start=T)
        ln_stats, ln_rstd, ln_xn = (signal(n, start=T) for n in ("ln_stats", "ln_rstd", "ln_xn"))
        ln_T, ln_done = signal("ln_T", start=2), signal("ln_done", start=2)
        h_lo_done = signal("h_lo_done")
        dt_mm, dt_abs, dt_log, a_ready, dec_mm, dec_ready = (signal(n) for n in ("dt_mm", "dt_abs", "dt_log", "a_ready", "dec_mm", "dec_ready"))
        proj_mm, tap3, conv_done, silu_done, gate_mm, gate_done, xT_mm, xtok_done = (
            signal(n) for n in ("proj_mm", "tap3", "conv_done", "silu_done", "gate_mm", "gate_done", "xT_mm", "xtok_done"))
        rA_ready, seg_mm, L_ready, M_ready, cb_mm, cbm_ready = (signal(n) for n in ("rA_ready", "seg_mm", "L_ready", "M_ready", "cb_mm", "cbm_ready"))
        xdt_ready, xde_ready, xD_ready, sx_ready = (signal(n) for n in ("xdt_ready", "xde_ready", "xD_ready", "sx_ready"))
        yd_mm, yo_mm, ds_mm, yd_read, yo_read, S_ready = (signal(n) for n in ("yd_mm", "yo_mm", "ds_mm", "yd_read", "yo_read", "S_ready"))
        g_ready, g_sq, gT_mm, gTs_ready, out_mm, po_read = (signal(n) for n in ("g_ready", "g_sq", "gT_mm", "gTs_ready", "out_mm", "po_read"))
        ms_ready, rms_rstd = signal("ms_ready"), signal("rms_rstd")
        up_mm, sig_done, hid_done, hh_done, hl_done, down_mm = (signal(n) for n in ("up_mm", "sig_done", "hid_done", "hh_done", "hl_done", "down_mm"))
        qk_mm, part1, part2, part3, qk_rest, v_mm, v_done, v_ones = (
            signal(n) for n in ("qk_mm", "part1", "part2", "part3", "qk_rest", "v_mm", "v_done", "v_ones"))
        stacked = [signal(f"stacked{i}", 16) for i in range(2)]
        s_mm, max_done, mp_done, mT_mm, mrow_done, sT_mm, exp_done, pv_mm, oT_done, o_mm, o_done = (
            signal(n) for n in ("s_mm", "max_done", "mp_done", "mT_mm", "mrow_done", "sT_mm", "exp_done", "pv_mm", "oT_done", "o_mm", "o_done"))
        yT_mm, yT_done, wo_mm = (signal(n) for n in ("yT_mm", "yT_done", "wo_mm"))
        lg_mm, sc_ready, su_mm, sr_ready, hs_ready, sd_mm = (signal(n) for n in ("lg_mm", "sc_ready", "su_mm", "sr_ready", "hs_ready", "sd_mm"))
        sel_ready, w_ready, pos_mm, slots_ready, out_ready, cum_ready = (
            signal(n) for n in ("sel_ready", "w_ready", "pos_mm", "slots_ready", "out_ready", "cum_ready"))
        scattered = signal("scattered", 16)
        wm_loaded = [signal(f"wm_loaded{i}", 16) for i in range(WB)]
        xd_loaded = [signal(f"xd_loaded{i}", 16) for i in range(WB)]
        xdT_mm, xdT_ready, h_mm, hr_ready, hq_ready, y_mm, ys_ready, target_ready = (
            signal(n) for n in ("xdT_mm", "xdT_ready", "h_mm", "hr_ready", "hq_ready", "y_mm", "ys_ready", "target_ready"))
        added = [signal(f"added{i}", 16) for i in range(2)]
        sums_loaded = [signal(f"sums_loaded{i}", 16) for i in range(B)]
        pair_sum, pair_sum_dve, final_sum = signal("pair_sum"), signal("pair_sum_dve"), signal("final_sum")
        out_stored = signal("out_stored", 16)

        block = ctx.enter_context(nc.Block())
        n_stage = {n: 0 for n in stage}

        def settle(eng):
            eng.sem_inc(settled.sem, 1)

        def stage_end(name, eng, b):
            n_stage[name] += 1
            settle(eng)
            stage[name].inc(eng.drain())
            for other in stage:
                if other != name:
                    eng.wait_ge(stage[other].sem, stage[other].upto(n_stage[name], b))

        attention_steps, ready = [], 0
        of_group = [[n for n, u in enumerate(AUNITS) if u[0] == g] for g in range(len(AGROUPS))]
        for g in range(len(AGROUPS) + 2):
            ahead = of_group[g] if g < len(AGROUPS) else []
            behind = of_group[g - 2] if g >= 2 else []
            turns = max(len(ahead), len(behind))
            for i in range(turns):
                if i < len(ahead):
                    attention_steps.append(("max", ahead[i]))
                if i == min(1, turns - 1) and 1 <= g <= len(AGROUPS):
                    attention_steps.append(("rows", g - 1))
                if i < len(behind):
                    attention_steps.append(("exp", behind[i]))
                    if behind[i] >= 2:
                        attention_steps.append(("values", behind[i] - 2))
        attention_steps += [("values", len(AUNITS) - 2), ("values", len(AUNITS) - 1)]
        for g in range(len(AGROUPS)):
            i = attention_steps.index(("values", of_group[g][-1]))
            attention_steps.insert(min(i + 3, len(attention_steps)), ("turn", g))
        i = attention_steps.index(("rows", len(AGROUPS) - 1))
        attention_steps.insert(i + 3, ("turn outputs", 0))
        attention_steps.insert(i + 6, ("project", 0))
        attention_steps += [("turn outputs", 1), ("project", 1)]
        of_pair_done = [max(g for g, (t, _) in enumerate(AGROUPS) if t // 2 == p) + 1 for p in range(2)]

        down_bank = (0, 6, 7, 1)
        NEXT = 4

        def tile_count(n, t):
            return T * (n - 1) + t + 1

        def pair_count(n, p):
            return 2 * (n - 1) + p + 1

        def norm_out(n):
            return {1: pob, 3: xrow}.get(n, xn)

        def norm_in(n):
            return xnext if n in (0, NEXT) else xb

        def rounds(eng, body):
            body(0, True, False)
            with eng.Fori(1, PAIRS // WB - 1) as r:
                body(r, False, False)
            body(PAIRS // WB - 1, False, True)

        def earliest(r, i):
            return i < 2 and isinstance(r, int) and r == 0

        def load_sums(eng, g, half):
            for j in range(2):
                eng.wait_ge(added[j].sem, 16 * PAIRS // 2)
            for q in range(2 * half, 2 * half + 2):
                r0 = q * (NTOK + CAP) + g * L
                sums_loaded[g].inc(eng.dma_start(part_sum[g][q].rearrange("p (t d) -> p t d", t=T),
                                                     acc[r0:r0 + L, :].rearrange("(t p) d -> p t d", p=P)))

        row_loads = [(wq, a["wq"]), (wk, a["wk"]), (wv, a["wv"]), (wo, a["wo"]), (pool_a[0:BROWS, :], a["rows"]),
                     (su, a["su"]), (sd, a["sd"])]
        wf = [carve(pool_c, 2048, KD * FT * P), carve(pool_c, 2048 + 1536, KD * FT * P), carve(pool_c, 2048 + 3072, FT * D)]
        masks = carve(pool_c, 2048 + 4608, 2 * P)
        wt = [w.rearrange("p k n -> p (k n)") for w in (w1q[:, :, :], w2q[:, :, :], w3q[:, :, :])]
        low = S[:, 0:KD * FT * P]
        absum, thr, nthr = S[:, 2040:2043], S[:, 2030:2033], S[:, 2034:2037]
        ffn_loads = [(wf[0], a["w1"]), (wf[1], a["w2"]), (wf[2], a["w3"]), (masks, a["masks"])]

        @block.sync
        def _(sp):
            def rows_of(x, b):
                return x.rearrange("b (t p) d -> b p t d", p=P)[bass.ds(b, 1)].rearrange("b p t d -> p (b t) d")

            xnext_loaded.inc(sp.dma_start(xnext, rows_of(a["x"], 0)))
            for name in ("consts", "params"):
                w_small_loaded.inc(sp.dma_start(small[name][:, :], a[name]))
            for dst, src in ffn_loads:
                w_ffn_loaded.inc(sp.dma_start(dst, src))
            for lo, hi in ((INTER, PROJ), (0, INTER)):
                w_in_loaded[lo == 0].inc(sp.dma_start(win[:, :, lo:hi], a["win"][:, :, lo:hi]))
            w_out_loaded.inc(sp.dma_start(wout[:, :, :], a["wout"]))
            def row(b, following):
                sp.wait_ge(stored.sem, b * 16)
                x_loaded.inc(sp.dma_start(xb[:, :, :], rows_of(a["x"], b)))
                sp.wait_ge(ln_xn.sem, ln_xn.upto(tile_count(1, T - 1), b))
                for dst, src in row_loads:
                    late_loaded.inc(sp.dma_start(dst, src))
                for half in range(2):
                    sp.wait_ge(part3.sem, part3.upto(2 * half + 2, b))
                    for i, (qp, kp) in enumerate(zip(QPARTS, KPARTS)):
                        r0, kp = BROWS + i * AD, kp + 3
                        stacked[half].inc(sp.dma_start(qks[r0:r0 + AD, half * 8:half * 8 + 8],
                                                       parts[half][:, qp:kp + 1:kp - qp, :]))
                sp.wait_ge(wo_mm.sem, wo_mm.upto(2, b))
                xnext_loaded.inc(sp.dma_start(xnext, rows_of(a["x"], following)))

            for s in signals.values():
                s.new_trip()
            with sp.Fori(0, B - 1) as b:
                row(b, b + 1)
            for s in signals.values():
                s.new_trip()
            row(B - 1, 0)
            w1v = a["w1m"].rearrange("(h q) p k i -> q p h (k i)", h=2)
            w2v = a["w2m"].rearrange("(h q) i n -> q i h n", h=2)
            xv = xslot[1:1 + E * CAP, :].rearrange("(h q s) w -> q h s w", h=2, s=CAP)

            def fetch(r, first, last):
                for i in range(WB):
                    n = r * WB + i
                    if not first:
                        sp.wait_ge(y_mm.sem, n - WB + 1)
                    wm_loaded[i].inc(sp.dma_start(w1m[i].rearrange("p e k i -> p e (k i)"),
                                                  w1v[bass.ds(n, 1)].rearrange("q p h w -> p (q h) w")))
                    wm_loaded[i].inc(sp.dma_start(w2m[i], w2v[bass.ds(n, 1)].rearrange("q i h n -> i (q h) n")))
                    if not first:
                        sp.wait_ge(ys_ready.sem, n - WB + 1)
                        sp.wait_ge(target_ready.sem, n - WB + 1)
                        xd_loaded[i].inc(sp.dma_start(xd[i], xv[bass.ds(n, 1)].rearrange("q h s w -> (q h) s w")))
                if first:
                    sp.wait_ge(scattered.sem, 16 * T * TOPK * B)
                    sp.wait_ge(rows_done.sem, B)
                    for i in range(WB):
                        xd_loaded[i].inc(sp.dma_start(xd[i], xv[bass.ds(i, 1)].rearrange("q h s w -> (q h) s w")))
            rounds(sp, fetch)
            for g in range(B):
                load_sums(sp, g, 0)
            for g in range(B):
                sp.wait_ge(final_sum.sem, g + 1)
                out_stored.inc(sp.dma_start(a["out"][g].rearrange("(t p) d -> p t d", p=P),
                                            part_sum[g][0].rearrange("p (t d) -> p t d", t=T)))
            sp.wait_ge(out_stored.sem, 16 * B)

        @block.scalar
        def _(act):
            sa = nc.scalar
            act.wait_ge(w_small_loaded.sem, 32)
            pro_act.inc(sa.activation(expA[:, :], expA[:, :], ACT.Exp))
            act.wait_ge(w_ffn_loaded.sem, 16 * len(ffn_loads))
            for i in range(3):
                last = sa.activation(pool_b[:, i * 1536:(i + 1) * 1536], wf[i], ACT.Abs, accum_out=absum[:, i:i + 1])
            pro_act.inc(last)

            b = None

            def at(s, k):
                act.wait_ge(s.sem, s.upto(k, b))

            def warm(func):
                warmed.append(func)
                sa.activation(warm_out[0:1, len(warmed) - 1:len(warmed)], eps[0:1, 0:1], func)
            warmed = []

            def norm_T(n):
                for i in range(2):
                    at(ln_T, pair_count(n, i))
                    ln_done.inc(sa.activation(xnT[:, :, i * 2 * P:(i + 1) * 2 * P], pb[i][:, :].rearrange("p (k n) -> p k n", k=KD), ACT.Copy))

            norm_T(0)
            for s in signals.values():
                s.new_trip()

            with act.Fori(0, B) as b:
                warmed.clear()
                warm(ACT.Exp)
                at(dt_abs, 1)
                dt_log.inc(sa.activation(l_dt[:, :, :], u_dt[:, :, :], ACT.Exp, scale=-1.0))
                at(dt_log, 1)
                dt_log.inc(sa.activation(l_dt[:, :, :], l_dt[:, :, :], ACT.Ln, bias=1.0))
                def decay_terms(u):
                    c, g = u // G, u % G
                    if u >= 2:
                        at(seg_mm, 2 * (u - 1))
                    for h in range(GH):
                        hh_ = g * GH + h
                        last = sa.activation(rA[u % 2][:, h, :], upto_[:, :], ACT.Copy, scale=a_[:, c, hh_:hh_ + 1])
                    rA_ready.inc(last)

                for j in range(CT + 2):
                    if j < CT:
                        ci = (CT - 2 + j) if j < 2 else j - 2
                        at(proj_mm, j + 1)
                        if j >= 2:
                            at(silu_done, j - 1)
                        tap3.inc(sa.activation(conv[j % 2], pb[j % 2][:, :], ACT.Identity,
                                               scale=convw[:, ci, 3:4], bias=convb[:, ci:ci + 1]))
                    if 1 <= j <= CT:
                        i = j - 1
                        at(conv_done, i + 1)
                        if i >= 4:
                            at(xT_mm, i - 2)
                        dst = (BT[:, :], CTm[:, :])[i] if i < 2 else xsf[i % 2]
                        silu_done.inc(sa.activation(dst, conv[i % 2], ACT.Silu))
                    if 2 <= j < CT:
                        m = j - 2
                        at(gate_mm, m + 1)
                        gate_done.inc(sa.activation(sz[:, m // G, (m % G) * GF:(m % G + 1) * GF], pb[2 + m % 2][:, :], ACT.Silu))
                    if j in (10, 12):
                        if j == 10:
                            at(a_ready, 1)
                            act.wait_ge(pro_pool.sem, 6)
                        decay_terms((j - 10) // 2)
                    if j == 2:
                        at(xT_mm, 1)
                        xtok_done.inc(sa.activation(btok[:, :, :], pb[4][:, :].rearrange("p (t n) -> p t n", t=T), ACT.Copy))
                    if j >= 4:
                        m = j - 4
                        at(xT_mm, m + 2)
                        xtok_done.inc(sa.activation(xtok[:, :, m * P:(m + 1) * P],
                                                    pb[4 + (m + 1) % 2][:, :].rearrange("p (t n) -> p t n", t=T), ACT.Copy))
                at(dec_mm, 1)
                dec_ready.inc(sa.activation(dec[:, :, :].rearrange("p s n -> p (s n)"), pb[6][:, 0:3 * T * H], ACT.Exp))

                def decays(u):
                    if u >= 2:
                        at(yd_mm, u - 1)
                    for half in range(2):
                        at(seg_mm, 2 * u + half + 1)
                        L_ready.inc(sa.activation(Lx[u % 2][:, half * 4:half * 4 + 4, :],
                                                  pb[half][:, :].rearrange("p (h i) -> p h i", h=4), ACT.Exp))

                at(silu_done, CT)
                decays(0)
                for u in range(UNITS + 1):
                    if u + 1 < UNITS:
                        decays(u + 1)
                    if u + 2 < UNITS:
                        decay_terms(u + 2)
                    if u >= 1:
                        w = u - 1
                        at(g_ready, w + 1)
                        if w >= 1:
                            at(g_sq, w)
                        g_sq.inc(sa.activation(junk[:, :], gb[w % 2][:, :], ACT.Square, accum_out=ssq[:, w // G, w % G:w % G + 1]))
                        at(gT_mm, w + 1)
                        if w >= 2:
                            at(out_mm, w - 1)
                        gTs_ready.inc(sa.activation(gTs[w % 2][:, :, :].rearrange("p k n -> p (k n)"), pb[5][:, :], ACT.Copy))

                warm(ACT.Sigmoid)
                for i in range(2):
                    at(ln_T, pair_count(1, i))
                    ln_done.inc(sa.activation(h_hi[:, :, i * 2 * P:(i + 1) * 2 * P], pb[i][:, :].rearrange("p (k n) -> p k n", k=KD), ACT.Copy))
                for f in range(FT):
                    at(up_mm, 2 * f + 1)
                    if f >= 2:
                        at(hid_done, f - 1)
                    sig_done.inc(sa.activation(sg[f % 2], pb[2 + f % 2][:, :], ACT.Sigmoid))
                    at(hid_done, f + 1)
                    hh_done.inc(sa.activation(hh[:, f, :], hid[f % 2], ACT.Copy))

                norm_T(2)
                for m in range(5):
                    if m < 4:
                        at(qk_mm, m + 1)
                        part1.inc(sa.activation(parts[m // 2][:, m % 2 * 3, :], pb[2 + m][:, :], ACT.Copy, scale=1.0 if m % 2 else AD ** -0.5))
                    if m >= 1:
                        at(qk_rest, m)
                        part2.inc(sa.activation(parts[(m - 1) // 2][:, (m - 1) % 2 * 3 + 1, :], rest[(m - 1) % 2], ACT.Copy))
                for q in range(2):
                    at(v_mm, 2 * q + 2)
                    v_done.inc(sa.activation(vt[:, 2 * q:2 * q + 2, :, 0:AD],
                                             pb[6 + q][:, :].rearrange("p (t h n) -> p t h n", t=2, h=AH), ACT.Copy))
                warm(ACT.Exp)
                for step, n in attention_steps:
                    if step == "turn":
                        at(pv_mm, of_group[n][-1] + 1)
                        if n >= 2:
                            at(o_mm, n - 1)
                        oT_done.inc(sa.activation(oT[n % 2], pb[4 + n % 2][:, 0:P], ACT.Copy))
                    elif step == "rows":
                        t, q = AGROUPS[n]
                        at(mT_mm, n + 1)
                        mrow_done.inc(sa.activation(qs[0:MROWS, q * AQ:(q + 1) * AQ, t * P:(t + 1) * P],
                                                    pb[7][0:MROWS, :].rearrange("p (h k) -> p h k", h=AQ), ACT.Copy))
                    elif step == "turn outputs":
                        at(yT_mm, n + 1)
                        yT_done.inc(sa.activation(yT[:, :, n * 2 * P:(n + 1) * 2 * P], pb[7][:, :].rearrange("p (k n) -> p k n", k=KD), ACT.Copy))
                    elif step == "exp":
                        _, t, _, nh = AUNITS[n]
                        at(sT_mm, n + 1)
                        if n >= 3:
                            at(pv_mm, n - 2)
                        exp_done.inc(sa.activation(pT[n % 3][:, 0:nh * (t + 1) * P], pb[(2, 3, 6)[n % 3]][:, 0:nh * (t + 1) * P], ACT.Exp))
                norm_T(3)
                warm(ACT.Sigmoid)
                at(lg_mm, 1)
                sc_ready.inc(sa.activation(sc.rearrange("p t e -> p (t e)"), pb[2][:, 0:T * E], ACT.Sigmoid))
                for f in range(ST):
                    at(su_mm, f + 1)
                    if f >= 2:
                        at(hs_ready, f - 1)
                    sr_ready.inc(sa.activation(sr[f % 2], pb[4 + f % 2][:, :], ACT.Relu))
                    at(sr_ready, f + 1)
                    hs_ready.inc(sa.activation(hs[:, f, :], sr[f % 2], ACT.Square))
                norm_T(NEXT)
                at(out_ready, 1)
                stored.inc(act.dma_start(acc[0:NTOK, :].rearrange("(b t p) w -> b p t w", p=P, t=T)[bass.ds(b, 1)]
                                         .rearrange("b p t w -> p (b t) w"), xb[:, :, :]))
                stage_end("act", act, b)

            def relu(r, i):
                act.wait_ge(h_mm.sem, r * WB + (i + 1))
                if not earliest(r, i):
                    act.wait_ge(hq_ready.sem, r * WB + (i - 1))
                hr_ready.inc(sa.activation(hr[i % 2], pb[2 + i % 2][:, 0:P], ACT.Relu))

            def gated(r, first, last):
                for i in range(WB):
                    n = r * WB + i
                    if not last or i + 1 < WB:
                        relu(r, i + 1)
                    act.wait_ge(y_mm.sem, n + 1)
                    if not first:
                        act.wait_ge(added[i % 2].sem, r * (WB * 8) + (i // 2 - 1) * 16)
                    for h in range(2):
                        gate = xd[i][h * CAP:(h + 1) * CAP, bass.ds(n + (D + h * PAIRS), 1)]
                        ins = sa.activation(ys[i][h * CAP:(h + 1) * CAP, :], pb[4 + i % 2][h * CAP:(h + 1) * CAP, 0:D],
                                            ACT.Copy, scale=gate)
                    ys_ready.inc(ins)
            relu(0, 0)
            rounds(act, gated)
            for g in range(B):
                load_sums(act, g, 1)

        @block.tensor
        def _(pe):
            mm = nc.tensor.matmul

            def transpose(out, in_, size=P):
                return nc.tensor.transpose(out, in_, ident[0:size, 0:size])

            pe.wait_ge(w_small_loaded.sem, 32)
            pe.wait_ge(pro_act.sem, 2)
            pro_pe.inc(mm(pb[7][:, 0:3], ones[:, :], absum, start=True, stop=True))
            pe.wait_ge(pro_dve.sem, 1)

            b = None

            def at(s, k):
                pe.wait_ge(s.sem, s.upto(k, b))

            def norm_T(n):
                for t in range(T):
                    at(ln_xn, tile_count(n, t))
                    for k in range(KD):
                        last = transpose(pb[t // 2][:, (2 * k + t % 2) * P:(2 * k + t % 2 + 1) * P], norm_out(n)[:, t, k * P:(k + 1) * P])
                    if t % 2:
                        ln_T.inc(last)
                at(ln_done, pair_count(n, 1))

            norm_T(0)
            for s in signals.values():
                s.new_trip()
            pe.wait_ge(w_in_loaded[0].sem, 16)

            with pe.Fori(0, B) as b:
                for t in range(T):
                    for k in range(KD):
                        last = mm(pb[7][:, t * H:(t + 1) * H], xnT[:, k, t * P:(t + 1) * P], win[:, k, DTC:DTC + H],
                                  start=(k == 0), stop=(k == KD - 1))
                dt_mm.inc(last)
                for j in range(CT + 1):
                    if j < CT:
                        if j >= 2:
                            at(conv_done, j - 1)
                        col = (BC, CC)[j] if j < 2 else XS + (j - 2) * P
                        for k in range(KD):
                            last = mm(pb[j % 2][:, :], win[:, k, col:col + P], xnT[:, k, :], start=(k == 0), stop=(k == KD - 1))
                        proj_mm.inc(last)
                    if 2 <= j < CT:
                        m = j - 2
                        if m == 0:
                            pe.wait_ge(w_in_loaded[1].sem, 16)
                        if m >= 2:
                            at(gate_done, m - 1)
                        c, g = m // G, m % G
                        for k in range(KD):
                            last = mm(pb[2 + m % 2][:, :], xnT[:, k, c * P:(c + 1) * P], win[:, k, g * GF:(g + 1) * GF],
                                      start=(k == 0), stop=(k == KD - 1))
                        gate_mm.inc(last)
                    i = j - 1
                    if i == 0 or i >= 2:
                        q = 0 if i == 0 else i - 1
                        at(silu_done, i + 1)
                        if q >= 2:
                            at(xtok_done, q - 1)
                        src = BT[:, :] if i == 0 else xsf[i % 2]
                        for t in range(T):
                            last = transpose(pb[4 + q % 2][:, t * P:(t + 1) * P], src[:, t * P:(t + 1) * P])
                        xT_mm.inc(last)
                    if j == 3:
                        at(a_ready, 1)
                        for s, m in enumerate((upto_, after, ones)):
                            last = mm(pb[6][:, s * T * H:(s + 1) * T * H], m[:, :], a_[:, :, :].rearrange("p t h -> p (t h)"),
                                      start=True, stop=True)
                        dec_mm.inc(last)

                def segment_sums(u):
                    at(rA_ready, u + 1)
                    for half in range(2):
                        if u >= 1:
                            at(L_ready, 2 * (u - 1) + half + 1)
                        seg_mm.inc(mm(pb[half][:, :], after[:, :], rA[u % 2][:, half * 4:half * 4 + 4, :].rearrange("p h i -> p (h i)"),
                                      start=True, stop=True))

                def products_bc(c):
                    if c >= 1:
                        at(cbm_ready, c)
                    cb_mm.inc(mm(pb[7][:, 0:P], BT[:, c * P:(c + 1) * P], CTm[:, c * P:(c + 1) * P], start=True, stop=True))

                def out_part(w):
                    c, g = w // G, w % G
                    at(gTs_ready, w + 1)
                    if g == 0 and c >= 1:
                        at(po_read, c)
                    for k in range(GK):
                        last = mm(pb[6][:, 0:D], gTs[w % 2][:, k, :], wout[:, g * GK + k, :],
                                  start=(g == 0 and k == 0), stop=(g == G - 1 and k == GK - 1))
                    out_mm.inc(last)

                products_bc(0)
                at(conv_done, CT)
                segment_sums(0)
                at(gate_done, T * G)
                at(xtok_done, CT - 1)
                at(dec_ready, 1)
                for u in range(UNITS + 2):
                    c, g = u // G, u % G
                    if u < UNITS:
                        if g == 3 and c + 1 < T:
                            products_bc(c + 1)
                        if u + 1 < UNITS:
                            segment_sums(u + 1)
                        if c > 0:
                            at(S_ready, u - G + 1)
                            if u > G:
                                at(yo_read, u - G)
                            yo_mm.inc(mm(pb[3][:, :], CTm[:, c * P:(c + 1) * P], S[:, g * GF:(g + 1) * GF], start=True, stop=True))
                        at(M_ready, u + 1)
                        at(xdt_ready, u + 1)
                        if u >= 1:
                            at(yd_read, u)
                        for h in range(GH):
                            last = mm(pb[2][:, h * HP:(h + 1) * HP], Lx[u % 2][:, h, :], xdt[u % 2][:, h * HP:(h + 1) * HP],
                                      start=True, stop=True)
                        yd_mm.inc(last)
                        if c < T - 1:
                            at(xde_ready, u + 1)
                            if u >= 1:
                                at(S_ready, u)
                            ds_mm.inc(mm(pb[4][:, :], btok[:, c, :], xde[u % 2], start=True, stop=True))
                    if 1 <= u <= UNITS:
                        w = u - 1
                        at(g_ready, w + 1)
                        if w >= 1:
                            at(gTs_ready, w)
                        for k in range(GK):
                            last = transpose(pb[5][:, k * P:(k + 1) * P], gb[w % 2][:, k * P:(k + 1) * P])
                        gT_mm.inc(last)
                    if u >= 2:
                        out_part(u - 2)

                norm_T(1)
                at(h_lo_done, 2)
                for f in range(FT + 2):
                    if f < FT:
                        for side, w in enumerate((w1q, w2q)):
                            if f >= 2:
                                at(hid_done, f - 1)
                            for k in range(KD):
                                for part in (h_hi, h_lo):
                                    last = mm(pb[2 + 2 * side + f % 2][:, :], w[:, k, f * P:(f + 1) * P], part[:, k, :],
                                              start=(k == 0 and part is h_hi), stop=(k == KD - 1 and part is h_lo))
                            up_mm.inc(last)
                    if f >= 2:
                        at(hh_done, f - 1)
                        at(hl_done, f - 1)
                        for t in range(T):
                            for part in (hh, hl):
                                last = mm(pb[down_bank[t]][:, 0:D], part[:, f - 2, t * P:(t + 1) * P], w3q[:, f - 2, :],
                                          start=(f == 2 and part is hh), stop=(f == FT + 1 and part is hl))
                            if f == FT + 1:
                                down_mm.inc(last)

                norm_T(2)
                at(late_loaded, len(row_loads))
                for m in range(4):
                    half, w = m // 2, (wq, wk)[m % 2]
                    for k in range(KD):
                        last = mm(pb[2 + m][:, :], w[:, k, half * P:(half + 1) * P], xnT[:, k, :], start=(k == 0), stop=(k == KD - 1))
                    qk_mm.inc(last)
                for t in range(T):
                    for k in range(KD):
                        last = mm(pb[6 + t // 2][:, (t % 2) * D:(t % 2 + 1) * D], xnT[:, k, t * P:(t + 1) * P], wv[:, k, :],
                                  start=(k == 0), stop=(k == KD - 1))
                    v_mm.inc(last)

                def scores(n):
                    g, t, h0, nh = AUNITS[n]
                    w = (t + 1) * P
                    if n == 0:
                        at(stacked[0], len(QPARTS))
                    if g == 2 * T:
                        at(stacked[1], len(QPARTS))
                    if n >= 2:
                        at(max_done, n - 1)
                    for i in range(nh):
                        out = pb[n % 2][:, i * w:(i + 1) * w]
                        mm(out, qs[0:ROWS, h0 + i, t * P:(t + 1) * P], ks[0:ROWS, h0 + i, 0:w], start=True, stop=False)
                        last = mm(out[:, t * P:w], identb[:, :], maskb[:, :], start=False, stop=True)
                    s_mm.inc(last)

                def maxima_rows(g):
                    at(mp_done, g + 1)
                    if g == 0:
                        at(v_done, 2)
                    else:
                        at(mrow_done, g)
                    for i in range(AQ):
                        last = mm(pb[7][0:MROWS, i * P:(i + 1) * P], mparts[g % 2][:, i, :], identb[:, :], start=True, stop=True)
                    mT_mm.inc(last)

                def transposed_scores(n):
                    g, t, h0, nh = AUNITS[n]
                    w = (t + 1) * P
                    bank = pb[(2, 3, 6)[n % 3]]
                    at(mrow_done, g + 1)
                    if n >= 3:
                        at(exp_done, n - 2)
                    for i in range(nh):
                        for kb in range(t + 1):
                            out = bank[:, i * w + kb * P:i * w + (kb + 1) * P]
                            last = mm(out, ks[0:ROWS, h0 + i, kb * P:(kb + 1) * P], qs[0:ROWS, h0 + i, t * P:(t + 1) * P],
                                      start=True, stop=(kb < t))
                        last = mm(out, identb[:, :], maskTb[:, :], start=False, stop=True)
                    sT_mm.inc(last)

                def weighted_values(n):
                    g, t, h0, nh = AUNITS[n]
                    at(exp_done, n + 1)
                    if g >= 2:
                        at(o_done, g - 1)
                    for i in range(nh):
                        r0 = (h0 + i) % AQ * AV
                        for kb in range(t + 1):
                            last = mm(pb[4 + g % 2][r0:r0 + AV, 0:P], vt[:, kb, h0 + i, :],
                                      pT[n % 3][:, (i * (t + 1) + kb) * P:(i * (t + 1) + kb + 1) * P], start=(kb == 0), stop=(kb == t))
                    pv_mm.inc(last)

                def turn_outputs(p):
                    at(o_done, of_pair_done[p])
                    at(mrow_done, len(AGROUPS))
                    for k in range(KD):
                        for i in range(2):
                            last = transpose(pb[7][:, (2 * k + i) * P:(2 * k + i + 1) * P], yat[:, 2 * p + i, k * P:(k + 1) * P])
                    yT_mm.inc(last)

                def project(p):
                    at(yT_done, p + 1)
                    for i in range(2):
                        t = 2 * p + i
                        for k in range(KD):
                            last = mm(pb[t][:, 0:D], yT[:, k, t * P:(t + 1) * P], wo[:, k, :], start=(k == 0), stop=(k == KD - 1))
                    wo_mm.inc(last)

                def turn(g):
                    at(oT_done, g + 1)
                    o_mm.inc(transpose(pb[4 + g % 2][:, P:2 * P], oT[g % 2]))

                at(part3, 4)
                at(v_ones, 1)
                for step, n in attention_steps:
                    if step == "max":
                        scores(n)
                    elif step == "rows":
                        maxima_rows(n)
                    elif step == "exp":
                        transposed_scores(n)
                    elif step == "values":
                        weighted_values(n)
                    elif step == "turn":
                        turn(n)
                    elif step == "turn outputs":
                        turn_outputs(n)
                    else:
                        project(n)
                norm_T(3)
                for t in range(T):
                    for k in range(KD):
                        last = mm(pb[2][:, t * E:(t + 1) * E], xnT[:, k, t * P:(t + 1) * P], gw[:, k, :],
                                  start=(k == 0), stop=(k == KD - 1))
                lg_mm.inc(last)
                at(late_loaded, len(row_loads))
                for f in range(ST):
                    if f >= 2:
                        at(sr_ready, f - 1)
                    for k in range(KD):
                        last = mm(pb[4 + f % 2][:, :], su[:, k, f * P:(f + 1) * P], xnT[:, k, :], start=(k == 0), stop=(k == KD - 1))
                    su_mm.inc(last)
                at(hs_ready, ST)
                for t in range(T):
                    if t == T // 2:
                        at(cum_ready, 1)
                        for i in range(T):
                            mm(pb[3][:, i * E:(i + 1) * E], before[:, :], sel[:, i, :], start=True, stop=False)
                            last = mm(pb[3][:, i * E:(i + 1) * E], ones[:, :], cum[:, i, :], start=False, stop=True)
                        pos_mm.inc(last)
                    for f in range(ST):
                        last = mm(pb[6 + t // 2][:, (t % 2) * D:(t % 2 + 1) * D], hs[:, f, t * P:(t + 1) * P], sd[:, f, :],
                                  start=(f == 0), stop=(f == ST - 1))
                sd_mm.inc(last)
                norm_T(NEXT)
                stage_end("pe", pe, b)

            def turn_tokens(r, i):
                pe.wait_ge(xd_loaded[i % WB].sem, (r + i // WB) * 16 + 16)
                if not earliest(r, i):
                    pe.wait_ge(xdT_ready.sem, r * WB + (i - 1))
                for k in range(KD):
                    last = transpose(pb[i % 2][:, k * P:(k + 1) * P], xd[i % WB][:, k * P:(k + 1) * P])
                xdT_mm.inc(last)

            def hidden(r, i):
                pe.wait_ge(wm_loaded[i % WB].sem, (r + i // WB) * 32 + 32)
                pe.wait_ge(xdT_ready.sem, r * WB + (i + 1))
                if not earliest(r, i):
                    pe.wait_ge(hq_ready.sem, r * WB + (i - 1))
                for e in range(2):
                    for k in range(KD):
                        last = mm(pb[2 + i % 2][:, e * CAP:(e + 1) * CAP], w1m[i % WB][:, e, k, :], xdT[i % 2][:, k, e * CAP:(e + 1) * CAP],
                                  start=(k == 0), stop=(k == KD - 1))
                h_mm.inc(last)

            def products(r, first, last_):
                for i in range(WB):
                    if not last_ or i + 2 < WB:
                        turn_tokens(r, i + 2)
                    if not last_ or i + 1 < WB:
                        hidden(r, i + 1)
                    pe.wait_ge(hq_ready.sem, r * WB + (i + 1))
                    if i >= 2 or not first:
                        pe.wait_ge(ys_ready.sem, r * WB + (i - 1))
                    for e in range(2):
                        last = mm(pb[4 + i % 2][e * CAP:(e + 1) * CAP, 0:D], hq[i % 2][:, e * CAP:(e + 1) * CAP], w2m[i][:, e, :],
                                  start=True, stop=True)
                    y_mm.inc(last)
            turn_tokens(0, 0)
            turn_tokens(0, 1)
            hidden(0, 0)
            rounds(pe, products)

        @block.vector
        def _(dve):
            v = nc.vector
            dve.wait_ge(w_ffn_loaded.sem, 16 * len(ffn_loads))
            dve.wait_ge(w_small_loaded.sem, 32)
            v.memset(cum[:, 0, :], 0.0)
            v.memset(xrow[:, 0, 0:XW - 1], 0.0)
            v.tensor_copy(identb[:, :], ident[:, :])
            v.tensor_copy(maskb[:, :], masks[:, 0:P])
            v.tensor_copy(maskTb[:, :], masks[:, P:2 * P])
            v.tensor_copy(xrow[:, 0, XW - 1:XW], small["empty"])
            dve.wait_ge(pro_pe.sem, 1)
            pro_dve.inc(v.tensor_scalar(thr, pb[7][:, 0:3], 1.0 / (FF * D), 1e-8, ALU.mult, ALU.add))
            dve.wait_ge(pro_dve.sem, 1)
            pro_dve.inc(v.tensor_scalar(nthr, thr, -0.5, None, ALU.mult))
            dve.wait_ge(pro_dve.sem, 2)
            pro_dve.inc(v.tensor_scalar(thr, thr, 0.5, None, ALU.mult))
            b = None

            def at(s, k):
                dve.wait_ge(s.sem, s.upto(k, b))

            def link(ins):
                dstep.inc(ins)
                at(dstep, dstep.count - (dstep.start if b is None else 0))

            def norm(n, make=None):
                for t in range(T + 1):
                    if t < T:
                        if make is not None:
                            make(t)
                        norm_stats(n, t)
                    if t >= 1:
                        norm_apply(n, t - 1)

            def norm_stats(n, t):
                link(v.bn_stats(stats[:, t, :], norm_in(n)[:, t, :]))
                settle(dve)
                ln_stats.inc(v.bn_aggr(mv[:, t, :], stats[:, t, :]))

            def norm_apply(n, t):
                at(ln_rstd, tile_count(n, t))
                ln_xn.inc(v.tensor_scalar(norm_out(n)[:, t, 0:D], norm_in(n)[:, t, :], mv[:, t, 0:1], rstd[:, t:t + 1], ALU.subtract, ALU.mult))

            at(xnext_loaded, 0)
            norm(0)
            for s in signals.values():
                s.new_trip()

            with dve.Fori(0, B) as b:

                def heads(x, c, n=GH, width=HP):
                    return x.unsqueeze(2).to_broadcast([P, n, width])

                at(dt_mm, 1)
                link(v.tensor_tensor(v_dt[:, :, :], pb[7][:, 0:T * H].rearrange("p (t h) -> p t h", t=T),
                                     dtb[:, :].unsqueeze(1).to_broadcast([P, T, H]), ALU.add))
                dt_abs.inc(v.scalar_tensor_tensor(out=u_dt[:, :, :], in0=v_dt[:, :, :], scalar=-1.0, in1=v_dt[:, :, :],
                                                  op0=ALU.mult, op1=ALU.max))
                at(dt_log, 2)
                link(v.scalar_tensor_tensor(out=dt_[:, :, :], in0=v_dt[:, :, :], scalar=0.0, in1=l_dt[:, :, :], op0=ALU.max, op1=ALU.add))
                a_ready.inc(v.scalar_tensor_tensor(out=a_[:, :, :], in0=dt_[:, :, :], scalar=-1.0,
                                                   in1=expA[:, :].unsqueeze(1).to_broadcast([P, T, H]), op0=ALU.mult, op1=ALU.mult))
                for j in range(CT):
                    ci = (CT - 2 + j) if j < 2 else j - 2
                    at(tap3, j + 1)
                    cv, bank = conv[j % 2], pb[j % 2]
                    for s in (1, 2, 3):
                        ins = v.scalar_tensor_tensor(out=cv[:, s:L], in0=bank[:, 0:L - s], scalar=convw[:, ci, TAPS - 1 - s:TAPS - s],
                                                     in1=cv[:, s:L], op0=ALU.mult, op1=ALU.add)
                        if s < 3:
                            link(ins)
                        else:
                            conv_done.inc(ins)

                at(gate_done, T * G)
                at(x_loaded, 1)

                def decay_products(u):
                    c, g = u // G, u % G
                    if g == 0:
                        at(cb_mm, c + 1)
                        if u >= 1:
                            at(M_ready, u)
                        cbm_ready.inc(v.tensor_tensor(cbm[:, :], pb[7][:, 0:P], upto_[:, :], ALU.mult))
                        at(cbm_ready, c + 1)
                    at(L_ready, 2 * u + 2)
                    M_ready.inc(v.tensor_tensor(Lx[u % 2], Lx[u % 2], cbm[:, :].unsqueeze(1).to_broadcast([P, GH, P]), ALU.mult))

                decay_products(0)
                for u in range(UNITS + 3):
                    c, g = u // G, u % G
                    w = u - 2
                    if w >= 0 and w % G == G - 1:
                        at(g_sq, w + 1)
                        ms_ready.inc(v.tensor_reduce(ms[:, w // G:w // G + 1], ssq[:, w // G, :], AX.X, ALU.add))
                    if u + 1 < UNITS:
                        decay_products(u + 1)
                    if u < UNITS:
                        hs_ = slice(c * H + g * GH, c * H + (g + 1) * GH)
                        at(yd_mm, u + 1)
                        at(xD_ready, u + 1)
                        if u >= 1:
                            at(g_ready, u)
                        yd_read.inc(v.tensor_tensor(yb, pb[2][:, :], xD[u % 2], ALU.add))
                        if c > 0:
                            at(yo_mm, u - G + 1)
                            yo_read.inc(v.tensor_tensor(yo[:, :].rearrange("p (h w) -> p h w", h=GH), pb[3][:, :].rearrange("p (h w) -> p h w", h=GH),
                                                        heads(dec[:, 0, hs_], c), ALU.mult))
                        if c < T - 1:
                            at(ds_mm, u + 1)
                            if c == 0:
                                S_ready.inc(v.tensor_copy(S[:, g * GF:(g + 1) * GF], pb[4][:, :]))
                            else:
                                at(sx_ready, u - G + 1)
                                S_ready.inc(v.tensor_tensor(S[:, g * GF:(g + 1) * GF], pb[4][:, :], sx[u % 2], ALU.add))
                        at(yd_read, u + 1)
                        if c > 0:
                            at(yo_read, u - G + 1)
                            link(v.tensor_tensor(yb[:, :], yb[:, :], yo[:, :], ALU.add))
                        if u >= 2:
                            at(gT_mm, u - 1)
                            at(g_sq, u - 1)
                        g_ready.inc(v.tensor_tensor(gb[u % 2][:, :], yb[:, :], sz[:, c, g * GF:(g + 1) * GF], ALU.mult))
                    if w >= 0 and w % G == G - 1:
                        t = w // G
                        at(out_mm, w + 1)
                        at(rms_rstd, t + 1)
                        po_read.inc(v.scalar_tensor_tensor(out=xb[:, t, :], in0=pb[6][:, 0:D], scalar=rms[:, t:t + 1], in1=xb[:, t, :],
                                                           op0=ALU.mult, op1=ALU.add))
                        at(po_read, t + 1)
                        norm_stats(1, t)
                    if w >= 1 and w % G == 0:
                        norm_apply(1, w // G - 1)

                for i in range(2):
                    at(ln_done, pair_count(1, i))
                    cols = slice(i * 2 * P, (i + 1) * 2 * P)
                    h_lo_done.inc(v.tensor_tensor(h_lo[:, :, cols], pb[i][:, :].rearrange("p (k n) -> p k n", k=KD), h_hi[:, :, cols], ALU.subtract))
                for f in range(FT):
                    at(up_mm, 2 * f + 2)
                    at(sig_done, f + 1)
                    if f >= 2:
                        at(hh_done, f - 1)
                        at(hl_done, f - 1)
                    hid_done.inc(v.tensor_tensor(hid[f % 2], pb[4 + f % 2][:, :], sg[f % 2], ALU.mult))
                    at(hh_done, f + 1)
                    hl_done.inc(v.tensor_tensor(hl[:, f, :], hid[f % 2], hh[:, f, :], ALU.subtract))
                def add_ffn(t):
                    at(down_mm, t + 1)
                    link(v.tensor_tensor(xb[:, t, :], pb[down_bank[t]][:, 0:D], xb[:, t, :], ALU.add))

                norm(2, add_ffn)
                at(late_loaded, len(row_loads))
                for m in range(5):
                    if m < 4:
                        at(part1, m + 1)
                        if m >= 2:
                            at(part3, m - 1)
                        qk_rest.inc(v.scalar_tensor_tensor(out=rest[m % 2], in0=pb[2 + m][:, :], scalar=1.0 if m % 2 else AD ** -0.5,
                                                           in1=parts[m // 2][:, m % 2 * 3, :], op0=ALU.mult, op1=ALU.subtract))
                    if m >= 1:
                        at(part2, m)
                        i = (m - 1) % 2 * 3
                        part3.inc(v.tensor_tensor(parts[(m - 1) // 2][:, i + 2, :], rest[(m - 1) % 2], parts[(m - 1) // 2][:, i + 1, :],
                                                  ALU.subtract))

                def values_norm(g):
                    t, q = AGROUPS[g]
                    at(o_mm, g + 1)
                    sums = pb[4 + g % 2][:, P:2 * P].rearrange("p (h w) -> p h w", h=AQ)
                    if g >= 1:
                        at(o_done, g)
                    link(v.reciprocal(rsums[:, :], sums[:, :, AD]))
                    o_done.inc(v.tensor_tensor(yat[:, t, q * AQ * AD:(q + 1) * AQ * AD].rearrange("p (h w) -> p h w", h=AQ),
                                               sums[:, :, 0:AD], heads(rsums[:, :], t, AQ, AD), ALU.mult))

                for step, n in attention_steps:
                    if step == "max":
                        _, t, h0, nh = AUNITS[n]
                        w = (t + 1) * P
                        at(s_mm, n + 1)
                        src = pb[n % 2][:, 0:nh * w].rearrange("p (h k) -> p h k", h=nh)
                        max_done.inc(v.tensor_reduce(nmax[:, t * AH + h0:t * AH + h0 + nh], src, AX.X, ALU.max, negate=True))
                    elif step == "turn":
                        values_norm(n)
                def add_attention(t):
                    at(wo_mm, t // 2 + 1)
                    link(v.tensor_tensor(xb[:, t, :], pb[t][:, 0:D], xb[:, t, :], ALU.add))

                dve.wait_ge(scattered.sem, scattered.upto(0, b))
                dve.wait_ge(empty_stored.sem, 32)
                norm(3, add_attention)
                at(xnext_loaded, 1)
                norm(NEXT)
                at(sc_ready, 1)
                link(v.tensor_tensor(sbi, sc, ebias[:, :].unsqueeze(1).to_broadcast([P, T, E]), ALU.add))
                settle(dve)
                for t in range(T):
                    for g in range(NG):
                        last = v.max(m8[:, t, g, :], sbi[:, t, g * EG:(g + 1) * EG])
                link(last)
                link(v.tensor_tensor(grp, m8[:, :, :, 0], m8[:, :, :, 1], ALU.add))
                settle(dve)
                for t in range(T):
                    last = v.max(gm8[:, t, :], grp[:, t, :])
                link(last)
                settle(dve)
                for t in range(T):
                    last = v.max_index(gi[:, t, :], gm8[:, t, :], grp[:, t, :])
                link(last)
                link(v.tensor_copy(gif, gi))
                link(v.tensor_tensor(goh, iota8[:, :].unsqueeze(1).unsqueeze(3).to_broadcast([P, T, NG, TKG]),
                                     gif[:, :, 0:TKG].unsqueeze(2).to_broadcast([P, T, NG, TKG]), ALU.is_equal))
                link(v.tensor_reduce(gmask.rearrange("p (t g) -> p t g", t=T), goh, AX.X, ALU.add))
                link(v.tensor_scalar(gmask, gmask, BIG, -BIG, ALU.mult, ALU.add))
                link(v.tensor_tensor(masked.rearrange("p (n e) -> p n e", e=EG), sbi.rearrange("p t (g e) -> p (t g) e", e=EG),
                                     gmask.unsqueeze(2).to_broadcast([P, T * NG, EG]), ALU.add))
                mk = masked.rearrange("p (t e) -> p t e", t=T)
                settle(dve)
                for t in range(T):
                    last = v.max(em8[:, t, :], mk[:, t, :])
                link(last)
                settle(dve)
                for t in range(T):
                    last = v.max_index(ei[:, t, :], em8[:, t, :], mk[:, t, :])
                link(last)
                link(v.tensor_copy(eif, ei))
                link(v.tensor_tensor(eoh, iota64[:, :].unsqueeze(1).unsqueeze(3).to_broadcast([P, T, E, TOPK]),
                                     eif[:, :, 0:TOPK].unsqueeze(2).to_broadcast([P, T, E, TOPK]), ALU.is_equal))
                sel_ready.inc(v.tensor_reduce(sel, eoh, AX.X, ALU.add))
                at(sel_ready, 1)
                for t in range(T):
                    ins = v.tensor_tensor(cum[:, t + 1, :], cum[:, t, :], sel[:, t, :], ALU.add)
                    if t < T - 1:
                        link(ins)
                    else:
                        cum_ready.inc(ins)
                link(v.tensor_tensor(wsel, sc, sel, ALU.mult))
                link(v.tensor_reduce(wsum, wsel, AX.X, ALU.add))
                link(v.tensor_scalar(wsum, wsum, 1e-20, None, ALU.add))
                link(v.reciprocal(wrec, wsum))
                v.tensor_copy(xrow[:, :, XW - 1], tokid[:, bass.ds(b * T, T)])
                for t in range(T):
                    last = v.tensor_scalar(wsel[:, t, :], wsel[:, t, :], wrec[:, t:t + 1], SCALE, ALU.mult, ALU.mult)
                w_ready.inc(last)
                at(pos_mm, 1)
                ppos = pb[3][:, 0:T * E]
                link(v.scalar_tensor_tensor(out=kept, in0=ppos, scalar=float(CAP), in1=sel.rearrange("p t e -> p (t e)"),
                                            op0=ALU.is_lt, op1=ALU.mult))
                link(v.tensor_tensor(sid.rearrange("p (t e) -> p t e", t=T), ppos.rearrange("p (t e) -> p t e", t=T),
                                     slot0[:, :].unsqueeze(1).to_broadcast([P, T, E]), ALU.add))
                link(v.tensor_tensor(sid, sid, kept, ALU.mult))
                settle(dve)
                for t in range(T):
                    last = v.max(s8[:, t, :], sid[:, t * E:(t + 1) * E])
                link(last)
                s8_ = s8.rearrange("p t k -> p (t k)")
                link(v.scalar_tensor_tensor(out=nos, in0=s8_, scalar=0.0, in1=noslot[:, :], op0=ALU.is_equal, op1=ALU.mult))
                slots_ready.inc(v.tensor_tensor(slots[:, :, :].rearrange("p t k -> p (t k)"), s8_, nos, ALU.add))
                v.tensor_copy(cum[:, 0, :], cum[:, T, :])
                at(sd_mm, 1)
                for q in range(2):
                    last = v.tensor_tensor(xb[:, 2 * q:2 * q + 2, :], pb[6 + q][:, :].rearrange("p (t n) -> p t n", t=2),
                                           xb[:, 2 * q:2 * q + 2, :], ALU.add)
                out_ready.inc(last)
                stage_end("dve", dve, b)
                settle(dve)
                rows_done.inc(dve.drain())

            def take_tokens(r, i):
                dve.wait_ge(xdT_mm.sem, r * WB + (i + 1))
                if not earliest(r, i):
                    dve.wait_ge(h_mm.sem, r * WB + (i - 1))
                xdT_ready.inc(v.tensor_copy(xdT[i % 2].rearrange("p k s -> p (k s)"), pb[i % 2][:, 0:KD * P]))

            def square(r, i):
                dve.wait_ge(hr_ready.sem, r * WB + (i + 1))
                if not earliest(r, i):
                    dve.wait_ge(y_mm.sem, r * WB + (i - 1))
                hq_ready.inc(v.tensor_tensor(hq[i % 2], hr[i % 2], hr[i % 2], ALU.mult))

            def ahead(r, first, last_):
                for i in range(WB):
                    if not last_ or i + 2 < WB:
                        take_tokens(r, i + 2)
                    if not last_ or i + 1 < WB:
                        square(r, i + 1)
                    dve.wait_ge(xd_loaded[i].sem, r * 16 + 16)
                    if not first:
                        dve.wait_ge(added[i % 2].sem, r * (WB * 8) + (i // 2 - 1) * 16)
                    target_ready.inc(v.tensor_tensor(target[i][:, :], xd[i][:, XW - 1:XW], sum0[:, i % 2:i % 2 + 1], ALU.add))
            take_tokens(0, 0)
            take_tokens(0, 1)
            square(0, 0)
            rounds(dve, ahead)
            for g in range(B):
                s0, s1, s2, _ = part_sum[g]
                dve.wait_ge(sums_loaded[g].sem, 16 * SUMS)
                pair_sum_dve.inc(v.tensor_tensor(s0, s0, s1, ALU.add))
                dve.wait_ge(pair_sum_dve.sem, g + 1)
                dve.wait_ge(pair_sum.sem, g + 1)
                final_sum.inc(v.tensor_tensor(s0, s0, s2, ALU.add))

        @block.gpsimd
        def _(pool):
            p = nc.gpsimd
            pool.wait_ge(pro_dve.sem, 3)
            b = None

            def at(s, k):
                pool.wait_ge(s.sem, s.upto(k, b))

            def power_half(out, in_, scale, t, done):
                settle(pool)
                pstep.inc(p.tensor_scalar(vare[:, t:t + 1], in_, scale, EPS, ALU.mult, ALU.add))
                at(pstep, pstep.count - (pstep.start if b is None else 0))
                settle(pool)
                done.inc(p.tensor_tensor(out, vare[:, t:t + 1], power[:, 0:1], ALU.pow))
                at(done, done.count - (done.start if b is None else 0))

            def norm_rstd(n, tiles=range(T)):
                for t in tiles:
                    at(ln_stats, tile_count(n, t))
                    power_half(rstd[:, t:t + 1], mv[:, t, 1:2], 1.0, t, ln_rstd)

            p.memset(power[:, :], -0.5)
            norm_rstd(0)
            k = 0
            for i in range(3):
                p.tensor_scalar(low, wf[i], nthr[:, i:i + 1], None, ALU.is_lt)
                pro_pool.inc(p.tensor_scalar(wf[i], wf[i], thr[:, i:i + 1], None, ALU.is_gt))
                k += 1
                pool.wait_ge(pro_pool.sem, k)
                pro_pool.inc(p.tensor_tensor(wt[i], wf[i], low, ALU.subtract))
                k += 1
                pool.wait_ge(pro_pool.sem, k)
            rows = SUMS * (NTOK + CAP) - NTOK
            pool.wait_ge(x_loaded.sem, 16)
            empty_stored.inc(pool.dma_start(xslot[1:1 + E * CAP, :].rearrange("(k p) w -> p k w", p=P),
                                            xrow[:, 0:1, :].to_broadcast([P, E * CAP // P, XW])))
            empty_stored.inc(pool.dma_start(acc[NTOK:NTOK + rows, :].rearrange("(k p) w -> p k w", p=P),
                                            xrow[:, 0:1, 0:D].to_broadcast([P, rows // P, D])))
            pool.wait_ge(w_out_loaded.sem, 16)
            for kk in range(INTER // P):
                p.tensor_scalar(wout[:, kk, :], wout[:, kk, :], normw[:, kk:kk + 1], None, ALU.mult)

            for s in signals.values():
                s.new_trip()

            with pool.Fori(0, B) as b:
                def heads(x):
                    return x.unsqueeze(2).to_broadcast([P, GH, HP])

                def by_head(x):
                    return x.rearrange("p (h w) -> p h w", h=GH)

                at(xtok_done, CT - 1)
                at(a_ready, 1)
                at(dec_ready, 1)
                for u in range(UNITS + 3):
                    w = u - 2
                    if w >= 0 and w % G == 0 and w >= G:
                        norm_rstd(1, [w // G - 1])
                    if u >= UNITS:
                        if w % G == G - 1:
                            at(ms_ready, w // G + 1)
                            power_half(rms[:, w // G:w // G + 1], ms[:, w // G:w // G + 1], 1.0 / INTER, w // G, rms_rstd)
                        continue
                    c, g = u // G, u % G
                    hs_ = slice(g * GH, (g + 1) * GH)
                    dh = slice(c * H + g * GH, c * H + (g + 1) * GH)
                    xs = by_head(xtok[:, c, g * GF:(g + 1) * GF])
                    if u >= 2:
                        at(yd_mm, u - 1)
                        at(xde_ready, min(u - 1, (T - 1) * G))
                    xdt_ready.inc(p.tensor_tensor(by_head(xdt[u % 2]), xs, heads(dt_[:, c, hs_]), ALU.mult))
                    if c < T - 1:
                        at(xdt_ready, u + 1)
                        if u >= 2:
                            at(ds_mm, u - 1)
                        xde_ready.inc(p.tensor_tensor(by_head(xde[u % 2]), by_head(xdt[u % 2]), heads(dec[:, 1, dh]), ALU.mult))
                    if u >= 2:
                        at(yd_read, u - 1)
                    xD_ready.inc(p.tensor_tensor(by_head(xD[u % 2]), xs, heads(dpar[:, hs_]), ALU.mult))
                    if 0 < c < T - 1:
                        at(S_ready, max(u - 4, u - 2) + 1)
                        sx_ready.inc(p.tensor_tensor(by_head(sx[u % 2]), by_head(S[:, g * GF:(g + 1) * GF]), heads(dec[:, 2, dh]), ALU.mult))
                    if w >= 0 and w % G == G - 1:
                        at(ms_ready, w // G + 1)
                        power_half(rms[:, w // G:w // G + 1], ms[:, w // G:w // G + 1], 1.0 / INTER, w // G, rms_rstd)
                norm_rstd(2)
                settle(pool)
                v_ones.inc(p.memset(vt[:, :, :, AD:AV], 1.0))
                for g, (t, q) in enumerate(AGROUPS):
                    m = nmax[:, t * AH + q * AQ:t * AH + (q + 1) * AQ]
                    mp = mparts[g % 2]
                    at(max_done, of_group[g][-1] + 1)
                    if g >= 2:
                        at(mT_mm, g - 1)
                    for part, src in enumerate((m, mrest[:, :])):
                        settle(pool)
                        pstep.inc(p.tensor_copy(mp[:, :, part], src))
                        at(pstep, pstep.count)
                        ins = p.tensor_tensor(mrest[:, :] if part == 0 else mp[:, :, 2], src, mp[:, :, part], ALU.subtract)
                        if part == 0:
                            pstep.inc(ins)
                            at(pstep, pstep.count)
                        else:
                            mp_done.inc(ins)
                            at(mp_done, g + 1)
                norm_rstd(3)
                norm_rstd(NEXT)
                n_stage["pool"] += 1
                settle(pool)
                stage["pool"].inc(pool.drain())
                at(slots_ready, 1)
                at(w_ready, 1)
                pool.wait_ge(empty_stored.sem, 32)
                settle(pool)
                for t in range(T):
                    for k in range(TOPK):
                        scattered.inc(p.indirect_dma_start(xslot, bass.IndirectOffsetOnAxis(ap=slots[:, t, k:k + 1], axis=0),
                                                           xrow[:, t, :], None))
                for other in stage:
                    if other != "pool":
                        pool.wait_ge(stage[other].sem, stage[other].upto(1, b))

            def add_outputs(r, first, last):
                for i in range(WB):
                    n = r * WB + i
                    pool.wait_ge(target_ready.sem, n + 1)
                    pool.wait_ge(ys_ready.sem, n + 1)
                    if i >= 2 or not first:
                        pool.wait_ge(added[i % 2].sem, r * (WB * 8) + i // 2 * 16)
                    settle(pool)
                    added[i % 2].inc(p.indirect_dma_start(acc, bass.IndirectOffsetOnAxis(ap=target[i][:, :], axis=0), ys[i], None,
                                                          compute_op=ALU.add))
            pool.wait_ge(stored.sem, 16 * B)
            rounds(pool, add_outputs)
            for g in range(B):
                pool.wait_ge(sums_loaded[g].sem, 16 * SUMS)
                pair_sum.inc(p.tensor_tensor(part_sum[g][2], part_sum[g][2], part_sum[g][3], ALU.add))
        return {n: s.most for n, s in signals.items()}


def constants():
    r = np.arange(P)
    upto = (r[:, None] <= r[None, :]).astype(np.float32)
    q, k = np.arange(L, dtype=np.float32), np.arange(L, dtype=np.float32)
    slopes = (2.0 ** (-8.0 / np.arange(1, AH + 1, dtype=np.float32))).astype(np.float32)
    def parts(v):
        out = []
        for _ in range(3):
            bits = np.ascontiguousarray(v).view(np.uint32)
            out.append(((bits + 0x7FFF + (bits >> 16 & 1)) & 0xFFFF0000).astype(np.uint32).view(np.float32))
            v = v - out[-1]
        return out

    qrows, krows = np.zeros((BROWS, AH, L), np.float32), np.ones((BROWS, AH, L), np.float32)
    for i, (at_q, slope) in enumerate(zip(parts(-slopes[:, None] * q[None, :]), parts(slopes))):
        qrows[MROWS + i] = at_q
        qrows[MROWS + 3 + i] = qrows[MROWS + 6 + i] = slope[:, None]
    krows[MROWS + 3:MROWS + 6] = k - k % 256
    krows[MROWS + 6:MROWS + 9] = k % 256
    rows = (np.stack([qrows, krows], 2).reshape(BROWS, -1).view(np.uint32) >> 16).astype(np.uint16)
    mask = np.where(r[None, :] > r[:, None], -BIG, 0.0).astype(np.float32)
    rep = lambda v: np.ascontiguousarray(np.broadcast_to(np.asarray(v, np.float32), (P, len(v))))
    c = dict(ident=np.eye(P, dtype=np.float32), upto=upto, after=np.ascontiguousarray(1 - upto),
                before=(upto - np.eye(P, dtype=np.float32)), ones=np.ones((P, P), np.float32),
                rows=rows.view(np.float32),
                iota8=rep(np.arange(NG)), iota64=rep(np.arange(E)), slot0=rep(1 + CAP * np.arange(E)),
                eps=np.full((P, 1), EPS, np.float32),
                tokid=np.arange(NTOK, dtype=np.float32).reshape(-1, P).T.copy(),
                noslot=(1 + E * CAP + (r[:, None, None] + P * (TOPK * np.arange(T)[None, :, None] + np.arange(8)[None, None, :]))
                        ).reshape(P, -1).astype(np.float32),
                empty=(NTOK + r[:, None] % CAP).astype(np.float32),
                sum0=((r[:, None] // CAP + 2 * np.arange(2)[None, :]) * (NTOK + CAP)).astype(np.float32))
    return dict(rows=c["rows"], masks=np.concatenate([mask, mask.T], 1), consts=np.concatenate([c[n] for n in CONSTS], 1))


def layouts(i):
    def tiles(w):
        return np.ascontiguousarray(w.reshape(-1, P, w.shape[1]).transpose(1, 0, 2))

    def by_place(w):
        return np.ascontiguousarray(w.reshape(D, 2, AH // 2, AD).transpose(0, 1, 3, 2)).reshape(D, D)

    def padded(w, rows, cols):
        out = np.zeros((rows, cols), np.float32)
        out[:w.shape[0], :w.shape[1]] = w
        return out

    def rep(v):
        return np.ascontiguousarray(np.broadcast_to(v, (P, len(v))))

    flat = lambda w: np.ascontiguousarray(w.reshape(P, -1))
    wqkv = i["L1_attn_W_qkv"]
    out = dict(
        x=np.ascontiguousarray(i["L0_attn_hidden_states"]), win=tiles(i["L0_attn_W_in"].T),
        convw=np.ascontiguousarray(i["L0_attn_conv_w"].reshape(CT, P, TAPS).transpose(1, 0, 2)),
        convb=np.ascontiguousarray(i["L0_attn_conv_b"].reshape(CT, P).T),
        dtb=rep(i["L0_attn_dt_bias"]), alog=rep(i["L0_attn_A_log"]), dpar=rep(i["L0_attn_D_param"]),
        normw=np.ascontiguousarray(i["L0_attn_norm_w"].reshape(-1, P).T), wout=tiles(i["L0_attn_W_out"].T),
        w1=flat(tiles(padded(i["L0_ffn_w1"].T, D, FT * P))), w2=flat(tiles(padded(i["L0_ffn_w2"].T, D, FT * P))),
        w3=flat(tiles(padded(i["L0_ffn_w3"].T, FT * P, D))),
        wq=tiles(by_place(wqkv[:, 0:D])), wk=tiles(by_place(wqkv[:, D:2 * D])), wv=tiles(wqkv[:, 2 * D:]), wo=tiles(i["L1_attn_W_o"]),
        gw=tiles(i["L1_ffn_gate_w"].T), ebias=rep(i["L1_ffn_e_bias"]),
        su=tiles(i["L1_ffn_shared_up_w"].T), sd=tiles(i["L1_ffn_shared_down_w"].T),
        w1m=np.ascontiguousarray(i["L1_ffn_w1"].reshape(E, P, KD, P).transpose(0, 3, 2, 1)),
        w2m=np.ascontiguousarray(i["L1_ffn_w2"].transpose(0, 2, 1)))
    out["params"] = np.concatenate([out.pop(n).reshape(P, -1) for n in PARAMS], 1)
    return out


def kernel(**inputs):
    from concourse import bacc
    from concourse.bass_utils import run_bass_kernel_spmd

    arrays = {**layouts({k: np.asarray(v) for k, v in inputs.items()}), **constants()}

    def program(per_trip):
        nc = bacc.Bacc("TRN2", target_bir_lowering=False, num_devices=1)
        aps = {n: nc.dram_tensor(f"in_{n}", x.shape, F32, kind="ExternalInput").ap() for n, x in arrays.items()}
        aps["out"] = nc.dram_tensor("out", (B, L, D), F32, kind="ExternalOutput").ap()
        return nc, build(nc, aps, per_trip)

    _, counts = program({})
    nc, again = program(counts)
    assert counts == again
    r = run_bass_kernel_spmd(nc, [{f"in_{n}": x for n, x in arrays.items()}], core_ids=[0])
    return r.results[0]["out"]
```

```python
from contextlib import ExitStack

import numpy as np
import concourse.bass as bass
from concourse import mybir

ALU = mybir.AluOpType
ACT = mybir.ActivationFunctionType
AX = mybir.AxisListType
F32 = mybir.dt.float32
F16 = mybir.dt.float16
BF16 = mybir.dt.bfloat16
U32 = mybir.dt.uint32

P = 128
B, L, D = 4, 512, 256
T = L // P
KD = D // P
NTOK = B * L
H, HP, N = 32, 64, 128
INTER = H * HP
TAPS = 4
XS, BC, CC, DTC = INTER, 2 * INTER, 2 * INTER + N, 2 * INTER + 2 * N
PROJ = DTC + H
CT = (INTER + 2 * N) // P
G = 4
GH = H // G
GF = INTER // G
GK = GF // P
UNITS = T * G
FF = 704
FT = (FF + P - 1) // P
AH, AD = 16, 16
MROWS, BROWS = 3, 12
QPARTS, KPARTS = (0, 0, 1, 1, 0, 2), (0, 1, 0, 1, 2, 0)
ROWS = BROWS + len(QPARTS) * AD
AV = 2 * AD
AQ = 4
AGROUPS = [(t, q) for half in range(2) for t in range(T) for q in range(half * 2, half * 2 + 2)]
AUNITS = [(g, t, q * AQ + h, T // (t + 1) or 1) for g, (t, q) in enumerate(AGROUPS)
          for h in range(0, AQ, T // (t + 1) or 1)]
E, TOPK, NG, TKG, CAP = 64, 6, 8, 4, 64
EG = E // NG
SCALE = 2.5
SH = 512
ST = SH // P
XW = D + E + 1
PAIRS = E // 2
SUMS = 4
BLOCKS = 2 * B
BLOCK_T = NTOK // P // BLOCKS
CONSTS = dict(ident=P, upto=P, after=P, before=P, ones=P, iota8=NG, iota64=E, slot0=E, noslot=T * 8, sum0=2,
              tokid=NTOK // P, empty=1, eps=1)
PARAMS = dict(convw=CT * TAPS, convb=CT, dtb=H, alog=H, dpar=H, normw=INTER // P, gw=KD * E, ebias=E)
EPS = 1e-5
BIG = 1e30


class Signal:

    def __init__(self, sem, step, per_trip, start):
        self.sem, self.step, self.per_trip, self.start = sem, step, per_trip, start
        self.count = self.most = 0

    def inc(self, instruction):
        self.count += 1
        self.most = max(self.most, self.count)
        instruction.then_inc(self.sem, self.step)

    def new_trip(self):
        self.count = 0

    def free_at_first(self, engine):
        for _ in range(self.start):
            engine.drain().then_inc(self.sem, self.step)

    def upto(self, k, b=None):
        value = (self.start + k) * self.step
        assert value > 0
        return value if b is None else b * (self.per_trip * self.step) + value


def build(nc, a, per_trip):
    with ExitStack() as ctx:
        signals = {}

        def sb(name, shape, dt=F32):
            return ctx.enter_context(nc.sbuf_tensor(name, shape, dt))

        def signal(name, step=1, start=0):
            s = Signal(ctx.enter_context(nc.semaphore(name)), step, per_trip.get(name, 0), start)
            signals[name] = s
            return s

        pb = [ctx.enter_context(nc.psum_tensor(f"bank{i}", [P, 512], F32)) for i in range(8)]

        xslot = nc.dram_tensor("xslot", (1 + E * CAP + T * TOPK * P, XW), F32).ap()
        acc = nc.dram_tensor("acc", (SUMS * (NTOK + CAP), D), F32).ap()

        joint = sb("joint", [P, KD * PROJ + T * INTER])
        win = joint[:, 0:KD * PROJ].rearrange("p (k n) -> p k n", k=KD)
        wout = sb("wout", [P, INTER // P, D])
        small = {}
        for group, fields in (("consts", CONSTS), ("params", PARAMS)):
            whole = small[group] = sb(group, [P, sum(fields.values())])
            first = 0
            for name, width in fields.items():
                small[name] = whole[:, first:first + width]
                first += width
        convw = small["convw"].rearrange("p (c t) -> p c t", c=CT)
        convb, dtb, expA, dpar, normw = (small[n] for n in ("convb", "dtb", "alog", "dpar", "normw"))
        gw = small["gw"].rearrange("p (k e) -> p k e", k=KD)
        ebias, ident, ones, iota8, iota64 = (small[n] for n in ("ebias", "ident", "ones", "iota8", "iota64"))
        upto_ = small["upto"]
        after = small["after"]
        before = small["before"]
        slot0 = small["slot0"]
        noslot = small["noslot"]
        sum0 = small["sum0"]
        tokid, eps = small["tokid"], small["eps"]
        w1q = sb("w1q", [P, KD, FT * P], F16)
        w2q = sb("w2q", [P, KD, FT * P], F16)
        w3q = sb("w3q", [P, FT, D], F16)
        identb = sb("identb", [P, P], BF16)
        maskb = sb("maskb", [P, P], BF16)
        maskTb = sb("maskTb", [P, P], BF16)
        cum = sb("cum", [P, T + 1, E])

        xrow = sb("xrow", [P, T, XW])
        xb = sb("xb", [P, T, D])
        xn = sb("xn", [P, T, D])
        xnT = sb("xnT", [P, KD, L])
        stats = sb("stats", [P, T, 6])
        mv = sb("mv", [P, T, 2])
        vare = sb("vare", [P, T])
        power = sb("power", [P, T])
        rms = sb("rms", [P, T])
        warm_out = sb("warm_out", [1, 16])
        rstd = sb("rstd", [P, T])

        pool_a = joint[:, KD * PROJ:KD * PROJ + T * INTER]
        pool_b = sb("pool_b", [P, T * INTER])
        pool_c = sb("pool_c", [P, 8192])
        xtok = pool_a[:, :].rearrange("p (t f) -> p t f", t=T)
        sz = pool_b[:, :].rearrange("p (t f) -> p t f", t=T)

        def carve(buf, at, n, dt=F32):
            ap = buf[:, at:at + n]
            return ap if dt == F32 else ap.bitcast(dt)

        conv = [carve(pool_c, i * 512, 512) for i in range(2)]
        xsf = [carve(pool_c, 1024 + i * 512, 512) for i in range(2)]
        rA = [carve(pool_c, 2048 + i * 1024, 1024).rearrange("p (h i) -> p h i", h=GH) for i in range(2)]
        Lx = [carve(pool_c, i * 1024, 1024).rearrange("p (h i) -> p h i", h=GH) for i in range(2)]
        xdt = [carve(pool_c, 4096 + i * 512, 512) for i in range(2)]
        xde = [carve(pool_c, 5120 + i * 512, 512) for i in range(2)]
        xD = [carve(pool_c, 6144 + i * 512, 512) for i in range(2)]
        sx = [carve(pool_c, 7168 + i * 512, 512) for i in range(2)]
        BT = sb("BT", [P, L])
        CTm = sb("CTm", [P, L])
        btok = sb("btok", [P, T, N])
        v_dt = sb("v_dt", [P, T, H])
        u_dt = sb("u_dt", [P, T, H])
        l_dt = sb("l_dt", [P, T, H])
        dt_ = sb("dt_", [P, T, H])
        a_ = sb("a_", [P, T, H])
        dec = sb("dec", [P, 3, T * H])
        cbm = sb("cbm", [P, P])
        S = sb("S", [P, INTER])
        yb, yo = xn[:, 0:2, :].rearrange("p t n -> p (t n)"), xn[:, 2:4, :].rearrange("p t n -> p (t n)")
        gb = [xnT[:, i, :] for i in range(2)]
        gTs = [sb(f"gTs{i}", [P, GK, P]) for i in range(2)]
        ssq = sb("ssq", [P, T, G])
        ms = sb("ms", [P, T])
        pob = sb("pob", [P, T, D])
        junk = sb("junk", [P, 512], BF16)

        h_hi = carve(pool_c, 0, 512, F16).rearrange("p (k n) -> p k n", k=KD)
        h_lo = carve(pool_c, 512, 512, F16).rearrange("p (k n) -> p k n", k=KD)
        sg = [carve(pool_c, 1024 + i * 512, 512) for i in range(2)]
        hid = [carve(pool_c, 2048 + i * 512, 512) for i in range(2)]
        hh = carve(pool_c, 3072, FT * 256, F16).rearrange("p (f n) -> p f n", f=FT)
        hl = carve(pool_c, 3072 + FT * 256, FT * 256, F16).rearrange("p (f n) -> p f n", f=FT)

        qks = carve(pool_a, 0, AH * L, BF16).rearrange("p (h s n) -> p h s n", s=2, h=AH)
        qs, ks = qks[:, :, 0], qks[:, :, 1]
        parts = [carve(pool_b, i * 1536, 1536, BF16).rearrange("p (s n) -> p s n", s=6) for i in range(2)]
        rest = [carve(pool_b, 3072 + i * L, L) for i in range(2)]
        vt = carve(pool_b, 4096, T * AH * AV).rearrange("p (t h n) -> p t h n", t=T, h=AH)
        pT = [carve(pool_c, i * 512, 512) for i in range(3)]
        oT = [carve(pool_c, 3584 + i * P, P) for i in range(2)]
        yat = carve(pool_c, 1536, T * D).rearrange("p (t n) -> p t n", t=T)
        yT = carve(pool_c, 2560, KD * L).rearrange("p (k n) -> p k n", k=KD)
        wq = carve(pool_c, 6144, KD * D).rearrange("p (k n) -> p k n", k=KD)
        wk = carve(pool_c, 6656, KD * D).rearrange("p (k n) -> p k n", k=KD)
        wv = carve(pool_c, 7168, KD * D).rearrange("p (k n) -> p k n", k=KD)
        wo = carve(pool_c, 7680, KD * D).rearrange("p (k n) -> p k n", k=KD)
        nmax = sb("nmax", [P, T * AH])
        mrest = sb("mrest", [P, AQ])
        mparts = [sb(f"mparts{i}", [P, AQ, MROWS], BF16) for i in range(2)]
        rsums = sb("rsums", [P, AQ])

        sc = carve(pool_c, 0, 256).rearrange("p (t e) -> p t e", t=T)
        sbi = carve(pool_c, 256, 256).rearrange("p (t e) -> p t e", t=T)
        m8 = carve(pool_c, 512, 256).rearrange("p (t g m) -> p t g m", t=T, g=NG)
        grp = carve(pool_c, 768, 32).rearrange("p (t g) -> p t g", t=T)
        gm8 = carve(pool_c, 800, 32).rearrange("p (t g) -> p t g", t=T)
        gi = carve(pool_c, 832, 32, U32).rearrange("p (t g) -> p t g", t=T)
        gif = carve(pool_c, 864, 32).rearrange("p (t g) -> p t g", t=T)
        goh = carve(pool_c, 896, 128).rearrange("p (t g k) -> p t g k", t=T, g=NG)
        gmask = carve(pool_c, 1024, 32)
        em8 = carve(pool_c, 1056, 32).rearrange("p (t g) -> p t g", t=T)
        ei = carve(pool_c, 1088, 32, U32).rearrange("p (t g) -> p t g", t=T)
        eif = carve(pool_c, 1120, 32).rearrange("p (t g) -> p t g", t=T)
        wsum = carve(pool_c, 1152, 4)
        wrec = carve(pool_c, 1156, 4)
        s8 = carve(pool_c, 1160, 32).rearrange("p (t g) -> p t g", t=T)
        masked = carve(pool_c, 1280, 256)
        sel = carve(pool_c, 1536, 256).rearrange("p (t e) -> p t e", t=T)
        wsel = xrow[:, :, D:D + E]
        kept = carve(pool_c, 2048, 256)
        sid = carve(pool_c, 2304, 256)
        eoh = carve(pool_c, 2560, T * E * TOPK).rearrange("p (t e k) -> p t e k", t=T, e=E)
        sr = [carve(pool_b, i * 512, 512) for i in range(2)]
        su = carve(pool_b, 6144, KD * SH).rearrange("p (k n) -> p k n", k=KD)
        sd = carve(pool_b, 7168, ST * D).rearrange("p (k n) -> p k n", k=ST)
        xnext = carve(pool_b, 5120, T * D).rearrange("p (t n) -> p t n", t=T)
        hs = carve(pool_b, 1024, ST * L).rearrange("p (f n) -> p f n", f=ST)
        nos = carve(pool_c, 5760, 32)
        slots = sb("slots", [P, T, 8], U32)

        TRIP = 16
        WB = 8
        W1, W2 = 2 * KD * P, 2 * D

        def weights_at(r, i):
            return (r % 2) * (KD * PROJ) + i * (W1 + W2)

        w1m = [joint[:, c:c + W1].rearrange("p (e k i) -> p e k i", e=2, k=KD) for c in (weights_at(i // WB, i % WB) for i in range(TRIP))]
        w2m = [joint[:, c + W1:c + W1 + W2].rearrange("p (e n) -> p e n", e=2) for c in (weights_at(i // WB, i % WB) for i in range(TRIP))]
        xd = [carve(pool_b, i * XW, XW) for i in range(WB)]
        xdT = [carve(pool_b, 2592 + i * 256, 256).rearrange("p (k s) -> p k s", k=KD) for i in range(2)]
        hr = [carve(pool_b, 3104 + i * P, P) for i in range(2)]
        hq = [carve(pool_b, 3360 + i * P, P) for i in range(2)]
        ys = [carve(pool_b, 3616 + i * D, D) for i in range(WB)]
        target = [sb(f"target{i}", [P, 1], U32) for i in range(WB)]
        part_sum = [[carve((pool_c, pool_a)[i // (BLOCKS // 2)], (i % (BLOCKS // 2) * SUMS + s) * BLOCK_T * D, BLOCK_T * D)
                     for s in range(SUMS)] for i in range(BLOCKS)]

        w_in_loaded = [signal(f"w_in_loaded{i}", 16) for i in range(2)]
        w_small_loaded = signal("w_small_loaded", 16)
        w_out_loaded = signal("w_out_loaded", 16)
        w_ffn_loaded = signal("w_ffn_loaded", 16)
        pro_act = signal("pro_act")
        pro_pe = signal("pro_pe")
        pro_dve = signal("pro_dve")
        pro_pool = signal("pro_pool")
        x_loaded = signal("x_loaded", 16)
        late_loaded = signal("late_loaded", 16)
        xnext_loaded = signal("xnext_loaded", 16, start=1)
        rows_done = signal("rows_done")
        stored = signal("stored", 16, start=1)
        stage = {n: signal(f"stage_{n}") for n in ("pe", "act", "dve", "pool")}
        dstep = signal("dstep", start=T)
        settled = signal("settled")
        pstep = signal("pstep", start=T)
        ln_stats, ln_rstd, ln_xn = (signal(n, start=T) for n in ("ln_stats", "ln_rstd", "ln_xn"))
        ln_T, ln_done = signal("ln_T", start=2), signal("ln_done", start=2)
        h_lo_done = signal("h_lo_done")
        dt_mm, dt_abs, dt_log, a_ready, dec_mm, dec_ready = (signal(n) for n in ("dt_mm", "dt_abs", "dt_log", "a_ready", "dec_mm", "dec_ready"))
        proj_mm, tap3, conv_done, silu_done, gate_mm, gate_done, xT_mm, xtok_done = (
            signal(n) for n in ("proj_mm", "tap3", "conv_done", "silu_done", "gate_mm", "gate_done", "xT_mm", "xtok_done"))
        rA_ready, seg_mm, L_ready, M_ready, cb_mm, cbm_ready = (signal(n) for n in ("rA_ready", "seg_mm", "L_ready", "M_ready", "cb_mm", "cbm_ready"))
        xdt_ready, xde_ready, xD_ready, sx_ready = (signal(n) for n in ("xdt_ready", "xde_ready", "xD_ready", "sx_ready"))
        yd_mm, yo_mm, ds_mm, yd_read, yo_read, S_ready = (signal(n) for n in ("yd_mm", "yo_mm", "ds_mm", "yd_read", "yo_read", "S_ready"))
        g_ready, g_sq, gT_mm, gTs_ready, out_mm, po_read = (signal(n) for n in ("g_ready", "g_sq", "gT_mm", "gTs_ready", "out_mm", "po_read"))
        ms_ready, rms_rstd = signal("ms_ready"), signal("rms_rstd")
        up_mm, sig_done, hid_done, hh_done, hl_done, down_mm = (signal(n) for n in ("up_mm", "sig_done", "hid_done", "hh_done", "hl_done", "down_mm"))
        qk_mm, part1, part2, part3, qk_rest, v_mm, v_done, v_ones = (
            signal(n) for n in ("qk_mm", "part1", "part2", "part3", "qk_rest", "v_mm", "v_done", "v_ones"))
        stacked = [signal(f"stacked{i}", 16) for i in range(2)]
        s_mm, max_done, mp_done, mT_mm, mrow_done, sT_mm, exp_done, pv_mm, oT_done, o_mm, o_done = (
            signal(n) for n in ("s_mm", "max_done", "mp_done", "mT_mm", "mrow_done", "sT_mm", "exp_done", "pv_mm", "oT_done", "o_mm", "o_done"))
        yT_mm, yT_done, wo_mm = (signal(n) for n in ("yT_mm", "yT_done", "wo_mm"))
        lg_mm, sc_ready, su_mm, sr_ready, hs_ready, sd_mm = (signal(n) for n in ("lg_mm", "sc_ready", "su_mm", "sr_ready", "hs_ready", "sd_mm"))
        sel_ready, w_ready, pos_mm, slots_ready, out_ready, cum_ready = (
            signal(n) for n in ("sel_ready", "w_ready", "pos_mm", "slots_ready", "out_ready", "cum_ready"))
        scattered = signal("scattered", 16, start=1)
        wm_loaded = [signal(f"wm_loaded{i}", 16) for i in range(WB)]
        xd_loaded = [signal(f"xd_loaded{i}", 16) for i in range(WB)]
        xdT_mm, xdT_ready, h_mm, hr_ready, hq_ready, y_mm, ys_ready, target_ready = (
            signal(n, start=1) for n in ("xdT_mm", "xdT_ready", "h_mm", "hr_ready", "hq_ready", "y_mm", "ys_ready", "target_ready"))
        added = [signal(f"added{i}", 16, start=1) for i in range(2)]
        sums_loaded = [[signal(f"sums_loaded{i}_{j}", 16) for j in range(2)] for i in range(BLOCKS)]
        pair_sum, final_sum = signal("pair_sum"), signal("final_sum")
        out_stored = signal("out_stored", 16)

        block = ctx.enter_context(nc.Block())
        n_stage = {n: 0 for n in stage}

        def settle(eng):
            eng.sem_inc(settled.sem, 1)

        def stage_end(name, eng, b):
            n_stage[name] += 1
            settle(eng)
            stage[name].inc(eng.drain())
            for other in stage:
                if other != name:
                    eng.wait_ge(stage[other].sem, stage[other].upto(n_stage[name], b))

        attention_steps = []
        of_group = [[n for n, u in enumerate(AUNITS) if u[0] == g] for g in range(len(AGROUPS))]
        for g in range(len(AGROUPS) + 2):
            ahead = of_group[g] if g < len(AGROUPS) else []
            behind = of_group[g - 2] if g >= 2 else []
            turns = max(len(ahead), len(behind))
            for i in range(turns):
                if i < len(ahead):
                    attention_steps.append(("max", ahead[i]))
                if i == min(1, turns - 1) and 1 <= g <= len(AGROUPS):
                    attention_steps.append(("rows", g - 1))
                if i < len(behind):
                    attention_steps.append(("exp", behind[i]))
                    if behind[i] >= 2:
                        attention_steps.append(("values", behind[i] - 2))
        attention_steps += [("values", len(AUNITS) - 2), ("values", len(AUNITS) - 1)]
        for g in range(len(AGROUPS)):
            i = attention_steps.index(("values", of_group[g][-1]))
            attention_steps.insert(min(i + 7, len(attention_steps)), ("turn", g))
        i = attention_steps.index(("rows", len(AGROUPS) - 1))
        attention_steps.insert(i + 5, ("turn outputs", 0))
        attention_steps.insert(i + 8, ("project", 0))
        attention_steps += [("turn outputs", 1), ("project", 1)]
        of_pair_done = [max(g for g, (t, _) in enumerate(AGROUPS) if t // 2 == p) + 1 for p in range(2)]

        down_bank = (0, 6, 7, 1)
        NEXT = 4

        def tile_count(n, t):
            return T * (n - 1) + t + 1

        def pair_count(n, p):
            return 2 * (n - 1) + p + 1

        def norm_out(n):
            return {1: pob, 3: xrow}.get(n, xn)

        def norm_in(n):
            return xnext if n in (0, NEXT) else xb

        def trips(eng, body):
            with eng.Fori(0, PAIRS // TRIP) as q:
                body(q)

        def pair_count_of(q, i, ago=0):
            return q * TRIP + max(i - ago + 1, 0) + 1

        def added_count(q, i, ago):
            return (q * (TRIP // 2) + max((i - ago) // 2 + 1, 0) + 1) * 16

        def load_sums(eng, g, j):
            eng.wait_ge(added[j].sem, added[j].upto(PAIRS // 2))
            for q in range(2 * j, 2 * j + 2):
                r0 = q * (NTOK + CAP) + g * BLOCK_T * P
                sums_loaded[g][j].inc(eng.dma_start(part_sum[g][q].rearrange("p (t d) -> p t d", t=BLOCK_T),
                                                    acc[r0:r0 + BLOCK_T * P, :].rearrange("(t p) d -> p t d", p=P)))

        row_loads = [(wq, a["wq"]), (wk, a["wk"]), (wv, a["wv"]), (wo, a["wo"]), (pool_a[0:BROWS, :], a["rows"]),
                     (su, a["su"]), (sd, a["sd"])]
        wf = [carve(pool_c, 2048, KD * FT * P), carve(pool_c, 2048 + 1536, KD * FT * P), carve(pool_c, 2048 + 3072, FT * D)]
        masks = carve(pool_c, 2048 + 4608, 2 * P)
        wt = [w.rearrange("p k n -> p (k n)") for w in (w1q[:, :, :], w2q[:, :, :], w3q[:, :, :])]
        low = S[:, 0:KD * FT * P]
        absum, thr, nthr = S[:, 2040:2043], S[:, 2030:2033], S[:, 2034:2037]
        ffn_loads = [(wf[0], a["w1"]), (wf[1], a["w2"]), (wf[2], a["w3"]), (masks, a["masks"])]

        @block.sync
        def _(sp):
            def rows_of(x, b):
                return x.rearrange("b (t p) d -> b p t d", p=P)[bass.ds(b, 1)].rearrange("b p t d -> p (b t) d")

            xnext_loaded.inc(sp.dma_start(xnext, rows_of(a["x"], 0)))
            for name in ("consts", "params"):
                w_small_loaded.inc(sp.dma_start(small[name][:, :], a[name]))
            for dst, src in ffn_loads:
                w_ffn_loaded.inc(sp.dma_start(dst, src))
            for lo, hi in ((INTER, PROJ), (0, INTER)):
                w_in_loaded[lo == 0].inc(sp.dma_start(win[:, :, lo:hi], a["win"][:, :, lo:hi]))
            w_out_loaded.inc(sp.dma_start(wout[:, :, :], a["wout"]))
            w1v = a["w1m"].rearrange("(h q) p k i -> q p h (k i)", h=2)
            w2v = a["w2m"].rearrange("(h q) i n -> q i h n", h=2)
            xv = xslot[1:1 + E * CAP, :].rearrange("(h q s) w -> q h s w", h=2, s=CAP)

            def load_weights(r, i):
                n, at_w = r * WB + i, weights_at(r, i)
                wm_loaded[i].inc(sp.dma_start(joint[:, bass.ds(at_w, W1)].rearrange("p (e w) -> p e w", e=2),
                                              w1v[bass.ds(n, 1)].rearrange("q p h w -> p (q h) w")))
                wm_loaded[i].inc(sp.dma_start(joint[:, bass.ds(at_w + W1, W2)].rearrange("p (e w) -> p e w", e=2),
                                              w2v[bass.ds(n, 1)].rearrange("q i h n -> i (q h) n")))

            def load_tokens(r, i):
                xd_loaded[i].inc(sp.dma_start(xd[i], xv[bass.ds(r * WB + i, 1)].rearrange("q h s w -> (q h) s w")))

            def row(b, following, last=False):
                sp.wait_ge(stored.sem, stored.upto(0, b))
                x_loaded.inc(sp.dma_start(xb[:, :, :], rows_of(a["x"], b)))
                sp.wait_ge(ln_xn.sem, ln_xn.upto(tile_count(1, T - 1), b))
                for dst, src in row_loads:
                    late_loaded.inc(sp.dma_start(dst, src))
                if last:
                    for i in range(WB):
                        load_weights(0, i)
                for half in range(2):
                    sp.wait_ge(part3.sem, part3.upto(2 * half + 2, b))
                    for i, (qp, kp) in enumerate(zip(QPARTS, KPARTS)):
                        r0, kp = BROWS + i * AD, kp + 3
                        stacked[half].inc(sp.dma_start(qks[r0:r0 + AD, half * 8:half * 8 + 8],
                                                       parts[half][:, qp:kp + 1:kp - qp, :]))
                sp.wait_ge(wo_mm.sem, wo_mm.upto(2, b))
                xnext_loaded.inc(sp.dma_start(xnext, rows_of(a["x"], following)))

            for s in signals.values():
                s.new_trip()
            with sp.Fori(0, B - 1) as b:
                row(b, b + 1)
            for s in signals.values():
                s.new_trip()
            row(B - 1, 0, True)
            for i in range(WB):
                sp.wait_ge(wm_loaded[i].sem, 32)
                load_weights(1, i)
            sp.wait_ge(scattered.sem, scattered.upto(T * TOPK * B))
            sp.wait_ge(rows_done.sem, B)
            for i in range(WB):
                load_tokens(0, i)

            def fetch(r, last):
                for i in range(WB):
                    n = r * WB + i
                    sp.wait_ge(ys_ready.sem, n - WB + 2)
                    sp.wait_ge(target_ready.sem, n - WB + 2)
                    load_tokens(r, i)
                    if not last:
                        sp.wait_ge(wm_loaded[i].sem, r * 32 + 32)
                        load_weights(r + 1, i)
            with sp.Fori(1, PAIRS // WB - 1) as r:
                fetch(r, False)
            fetch(PAIRS // WB - 1, True)
            for g in range(BLOCKS):
                load_sums(sp, g, 0)
            out = a["out"].rearrange("b l d -> (b l) d").rearrange("(g t p) d -> g p t d", p=P, t=BLOCK_T)
            for g in range(BLOCKS):
                sp.wait_ge(final_sum.sem, g + 1)
                out_stored.inc(sp.dma_start(out[g], part_sum[g][0].rearrange("p (t d) -> p t d", t=BLOCK_T)))
            sp.wait_ge(out_stored.sem, 16 * BLOCKS)

        @block.scalar
        def _(act):
            sa = nc.scalar
            for s in (stored, hr_ready, ys_ready):
                s.free_at_first(act)
            act.wait_ge(w_small_loaded.sem, 32)
            pro_act.inc(sa.activation(expA[:, :], expA[:, :], ACT.Exp))
            act.wait_ge(w_ffn_loaded.sem, 16 * len(ffn_loads))
            for i in range(3):
                last = sa.activation(pool_b[:, i * 1536:(i + 1) * 1536], wf[i], ACT.Abs, accum_out=absum[:, i:i + 1])
            pro_act.inc(last)

            b = None

            def at(s, k):
                act.wait_ge(s.sem, s.upto(k, b))

            def warm(func):
                warmed.append(func)
                sa.activation(warm_out[0:1, len(warmed) - 1:len(warmed)], eps[0:1, 0:1], func)
            warmed = []

            def norm_T(n):
                for i in range(2):
                    at(ln_T, pair_count(n, i))
                    ln_done.inc(sa.activation(xnT[:, :, i * 2 * P:(i + 1) * 2 * P], pb[i][:, :].rearrange("p (k n) -> p k n", k=KD), ACT.Copy))

            norm_T(0)
            for s in signals.values():
                s.new_trip()

            with act.Fori(0, B) as b:
                warmed.clear()
                warm(ACT.Exp)
                at(dt_abs, 1)
                dt_log.inc(sa.activation(l_dt[:, :, :], u_dt[:, :, :], ACT.Exp, scale=-1.0))
                at(dt_log, 1)
                dt_log.inc(sa.activation(l_dt[:, :, :], l_dt[:, :, :], ACT.Ln, bias=1.0))

                def decay_terms(u):
                    c, g = u // G, u % G
                    if u >= 2:
                        at(seg_mm, 2 * (u - 1))
                    for h in range(GH):
                        hh_ = g * GH + h
                        last = sa.activation(rA[u % 2][:, h, :], upto_[:, :], ACT.Copy, scale=a_[:, c, hh_:hh_ + 1])
                    rA_ready.inc(last)

                for j in range(CT + 2):
                    if j < CT:
                        ci = (CT - 2 + j) if j < 2 else j - 2
                        at(proj_mm, j + 1)
                        if j >= 2:
                            at(silu_done, j - 1)
                        tap3.inc(sa.activation(conv[j % 2], pb[j % 2][:, :], ACT.Identity,
                                               scale=convw[:, ci, 3:4], bias=convb[:, ci:ci + 1]))
                    if 1 <= j <= CT:
                        i = j - 1
                        at(conv_done, i + 1)
                        if i >= 4:
                            at(xT_mm, i - 2)
                        dst = (BT[:, :], CTm[:, :])[i] if i < 2 else xsf[i % 2]
                        silu_done.inc(sa.activation(dst, conv[i % 2], ACT.Silu))
                    if 2 <= j < CT:
                        m = j - 2
                        at(gate_mm, m + 1)
                        gate_done.inc(sa.activation(sz[:, m // G, (m % G) * GF:(m % G + 1) * GF], pb[2 + m % 2][:, :], ACT.Silu))
                    if j in (10, 12):
                        if j == 10:
                            at(a_ready, 1)
                            act.wait_ge(pro_pool.sem, 6)
                        decay_terms((j - 10) // 2)
                    if j == 2:
                        at(xT_mm, 1)
                        xtok_done.inc(sa.activation(btok[:, :, :], pb[4][:, :].rearrange("p (t n) -> p t n", t=T), ACT.Copy))
                    if j >= 4:
                        m = j - 4
                        at(xT_mm, m + 2)
                        xtok_done.inc(sa.activation(xtok[:, :, m * P:(m + 1) * P],
                                                    pb[4 + (m + 1) % 2][:, :].rearrange("p (t n) -> p t n", t=T), ACT.Copy))
                at(dec_mm, 1)
                dec_ready.inc(sa.activation(dec[:, :, :].rearrange("p s n -> p (s n)"), pb[6][:, 0:3 * T * H], ACT.Exp))

                def decays(u):
                    if u >= 2:
                        at(yd_mm, u - 1)
                    for half in range(2):
                        at(seg_mm, 2 * u + half + 1)
                        L_ready.inc(sa.activation(Lx[u % 2][:, half * 4:half * 4 + 4, :],
                                                  pb[half][:, :].rearrange("p (h i) -> p h i", h=4), ACT.Exp))

                at(silu_done, CT)
                decays(0)
                for u in range(UNITS + 1):
                    if u + 1 < UNITS:
                        decays(u + 1)
                    if u + 2 < UNITS:
                        decay_terms(u + 2)
                    if u >= 1:
                        w = u - 1
                        at(g_ready, w + 1)
                        if w >= 1:
                            at(g_sq, w)
                        g_sq.inc(sa.activation(junk[:, :], gb[w % 2][:, :], ACT.Square, accum_out=ssq[:, w // G, w % G:w % G + 1]))
                        at(gT_mm, w + 1)
                        if w >= 2:
                            at(out_mm, w - 1)
                        gTs_ready.inc(sa.activation(gTs[w % 2][:, :, :].rearrange("p k n -> p (k n)"), pb[5][:, :], ACT.Copy))

                warm(ACT.Sigmoid)
                for i in range(2):
                    at(ln_T, pair_count(1, i))
                    ln_done.inc(sa.activation(h_hi[:, :, i * 2 * P:(i + 1) * 2 * P], pb[i][:, :].rearrange("p (k n) -> p k n", k=KD), ACT.Copy))
                for f in range(FT):
                    at(up_mm, 2 * f + 1)
                    if f >= 2:
                        at(hid_done, f - 1)
                    sig_done.inc(sa.activation(sg[f % 2], pb[2 + f % 2][:, :], ACT.Sigmoid))
                    at(hid_done, f + 1)
                    hh_done.inc(sa.activation(hh[:, f, :], hid[f % 2], ACT.Copy))

                norm_T(2)
                for m in range(5):
                    if m < 4:
                        at(qk_mm, m + 1)
                        part1.inc(sa.activation(parts[m // 2][:, m % 2 * 3, :], pb[2 + m][:, :], ACT.Copy, scale=1.0 if m % 2 else AD ** -0.5))
                    if m >= 1:
                        at(qk_rest, m)
                        part2.inc(sa.activation(parts[(m - 1) // 2][:, (m - 1) % 2 * 3 + 1, :], rest[(m - 1) % 2], ACT.Copy))
                for q in range(2):
                    at(v_mm, 2 * q + 2)
                    v_done.inc(sa.activation(vt[:, 2 * q:2 * q + 2, :, 0:AD],
                                             pb[6 + q][:, :].rearrange("p (t h n) -> p t h n", t=2, h=AH), ACT.Copy))
                warm(ACT.Exp)
                for step, n in attention_steps:
                    if step == "turn":
                        at(pv_mm, of_group[n][-1] + 1)
                        if n >= 2:
                            at(o_mm, n - 1)
                        oT_done.inc(sa.activation(oT[n % 2], pb[4 + n % 2][:, 0:P], ACT.Copy))
                    elif step == "rows":
                        t, q = AGROUPS[n]
                        at(mT_mm, n + 1)
                        mrow_done.inc(sa.activation(qs[0:MROWS, q * AQ:(q + 1) * AQ, t * P:(t + 1) * P],
                                                    pb[7][0:MROWS, :].rearrange("p (h k) -> p h k", h=AQ), ACT.Copy))
                    elif step == "turn outputs":
                        at(yT_mm, n + 1)
                        yT_done.inc(sa.activation(yT[:, :, n * 2 * P:(n + 1) * 2 * P], pb[7][:, :].rearrange("p (k n) -> p k n", k=KD), ACT.Copy))
                    elif step == "exp":
                        _, t, _, nh = AUNITS[n]
                        at(sT_mm, n + 1)
                        if n >= 3:
                            at(pv_mm, n - 2)
                        exp_done.inc(sa.activation(pT[n % 3][:, 0:nh * (t + 1) * P], pb[(2, 3, 6)[n % 3]][:, 0:nh * (t + 1) * P], ACT.Exp))
                norm_T(3)
                warm(ACT.Sigmoid)
                at(lg_mm, 1)
                sc_ready.inc(sa.activation(sc.rearrange("p t e -> p (t e)"), pb[2][:, 0:T * E], ACT.Sigmoid))
                for f in range(ST):
                    at(su_mm, f + 1)
                    if f >= 2:
                        at(hs_ready, f - 1)
                    sr_ready.inc(sa.activation(sr[f % 2], pb[4 + f % 2][:, :], ACT.Relu))
                    at(sr_ready, f + 1)
                    hs_ready.inc(sa.activation(hs[:, f, :], sr[f % 2], ACT.Square))
                norm_T(NEXT)
                at(out_ready, 1)
                stored.inc(act.dma_start(acc[0:NTOK, :].rearrange("(b t p) w -> b p t w", p=P, t=T)[bass.ds(b, 1)]
                                         .rearrange("b p t w -> p (b t) w"), xb[:, :, :]))
                stage_end("act", act, b)

            def relu(q, i):
                act.wait_ge(h_mm.sem, pair_count_of(q, i))
                act.wait_ge(hq_ready.sem, pair_count_of(q, i, 2))
                hr_ready.inc(sa.activation(hr[i % 2], pb[2 + i % 2][:, 0:P], ACT.Relu))

            def gated(q):
                for i in range(-1, TRIP):
                    if i + 1 < TRIP:
                        relu(q, i + 1)
                    if i >= 0:
                        act.wait_ge(y_mm.sem, pair_count_of(q, i))
                        act.wait_ge(added[i % 2].sem, added_count(q, i, WB))
                        y = ys[i % WB]
                        for h in range(2):
                            rows = slice(h * CAP, (h + 1) * CAP)
                            gate = xd[i % WB][rows, bass.ds(q * TRIP + (D + h * PAIRS + i), 1)]
                            ins = sa.activation(y[rows, :], pb[4 + i % 2][rows, 0:D], ACT.Copy, scale=gate)
                        ys_ready.inc(ins)
            trips(act, gated)
            for g in range(BLOCKS):
                load_sums(act, g, 1)

        @block.tensor
        def _(pe):
            mm = nc.tensor.matmul

            def transpose(out, in_, size=P):
                return nc.tensor.transpose(out, in_, ident[0:size, 0:size])

            for s in (xdT_mm, h_mm, y_mm):
                s.free_at_first(pe)
            pe.wait_ge(w_small_loaded.sem, 32)
            pe.wait_ge(pro_act.sem, 2)
            pro_pe.inc(mm(pb[7][:, 0:3], ones[:, :], absum, start=True, stop=True))
            pe.wait_ge(pro_dve.sem, 1)

            b = None

            def at(s, k):
                pe.wait_ge(s.sem, s.upto(k, b))

            def norm_T(n):
                for t in range(T):
                    at(ln_xn, tile_count(n, t))
                    for k in range(KD):
                        last = transpose(pb[t // 2][:, (2 * k + t % 2) * P:(2 * k + t % 2 + 1) * P], norm_out(n)[:, t, k * P:(k + 1) * P])
                    if t % 2:
                        ln_T.inc(last)
                at(ln_done, pair_count(n, 1))

            norm_T(0)
            for s in signals.values():
                s.new_trip()
            pe.wait_ge(w_in_loaded[0].sem, 16)

            with pe.Fori(0, B) as b:
                for t in range(T):
                    for k in range(KD):
                        last = mm(pb[7][:, t * H:(t + 1) * H], xnT[:, k, t * P:(t + 1) * P], win[:, k, DTC:DTC + H],
                                  start=(k == 0), stop=(k == KD - 1))
                dt_mm.inc(last)
                for j in range(CT + 1):
                    if j < CT:
                        if j >= 2:
                            at(conv_done, j - 1)
                        col = (BC, CC)[j] if j < 2 else XS + (j - 2) * P
                        for k in range(KD):
                            last = mm(pb[j % 2][:, :], win[:, k, col:col + P], xnT[:, k, :], start=(k == 0), stop=(k == KD - 1))
                        proj_mm.inc(last)
                    if 2 <= j < CT:
                        m = j - 2
                        if m == 0:
                            pe.wait_ge(w_in_loaded[1].sem, 16)
                        if m >= 2:
                            at(gate_done, m - 1)
                        c, g = m // G, m % G
                        for k in range(KD):
                            last = mm(pb[2 + m % 2][:, :], xnT[:, k, c * P:(c + 1) * P], win[:, k, g * GF:(g + 1) * GF],
                                      start=(k == 0), stop=(k == KD - 1))
                        gate_mm.inc(last)
                    i = j - 1
                    if i == 0 or i >= 2:
                        q = 0 if i == 0 else i - 1
                        at(silu_done, i + 1)
                        if q >= 2:
                            at(xtok_done, q - 1)
                        src = BT[:, :] if i == 0 else xsf[i % 2]
                        for t in range(T):
                            last = transpose(pb[4 + q % 2][:, t * P:(t + 1) * P], src[:, t * P:(t + 1) * P])
                        xT_mm.inc(last)
                    if j == 3:
                        at(a_ready, 1)
                        for s, m in enumerate((upto_, after, ones)):
                            last = mm(pb[6][:, s * T * H:(s + 1) * T * H], m[:, :], a_[:, :, :].rearrange("p t h -> p (t h)"),
                                      start=True, stop=True)
                        dec_mm.inc(last)

                def segment_sums(u):
                    at(rA_ready, u + 1)
                    for half in range(2):
                        if u >= 1:
                            at(L_ready, 2 * (u - 1) + half + 1)
                        seg_mm.inc(mm(pb[half][:, :], after[:, :], rA[u % 2][:, half * 4:half * 4 + 4, :].rearrange("p h i -> p (h i)"),
                                      start=True, stop=True))

                def products_bc(c):
                    if c >= 1:
                        at(cbm_ready, c)
                    cb_mm.inc(mm(pb[7][:, 0:P], BT[:, c * P:(c + 1) * P], CTm[:, c * P:(c + 1) * P], start=True, stop=True))

                def out_part(w):
                    c, g = w // G, w % G
                    at(gTs_ready, w + 1)
                    if g == 0 and c >= 1:
                        at(po_read, c)
                    for k in range(GK):
                        last = mm(pb[6][:, 0:D], gTs[w % 2][:, k, :], wout[:, g * GK + k, :],
                                  start=(g == 0 and k == 0), stop=(g == G - 1 and k == GK - 1))
                    out_mm.inc(last)

                products_bc(0)
                at(conv_done, CT)
                segment_sums(0)
                at(gate_done, T * G)
                at(xtok_done, CT - 1)
                at(dec_ready, 1)
                for u in range(UNITS + 2):
                    c, g = u // G, u % G
                    if u < UNITS:
                        if g == 3 and c + 1 < T:
                            products_bc(c + 1)
                        if u + 1 < UNITS:
                            segment_sums(u + 1)
                        if c > 0:
                            at(S_ready, u - G + 1)
                            if u > G:
                                at(yo_read, u - G)
                            yo_mm.inc(mm(pb[3][:, :], CTm[:, c * P:(c + 1) * P], S[:, g * GF:(g + 1) * GF], start=True, stop=True))
                        at(M_ready, u + 1)
                        at(xdt_ready, u + 1)
                        if u >= 1:
                            at(yd_read, u)
                        for h in range(GH):
                            last = mm(pb[2][:, h * HP:(h + 1) * HP], Lx[u % 2][:, h, :], xdt[u % 2][:, h * HP:(h + 1) * HP],
                                      start=True, stop=True)
                        yd_mm.inc(last)
                        if c < T - 1:
                            at(xde_ready, u + 1)
                            if u >= 1:
                                at(S_ready, u)
                            ds_mm.inc(mm(pb[4][:, :], btok[:, c, :], xde[u % 2], start=True, stop=True))
                    if 1 <= u <= UNITS:
                        w = u - 1
                        at(g_ready, w + 1)
                        if w >= 1:
                            at(gTs_ready, w)
                        for k in range(GK):
                            last = transpose(pb[5][:, k * P:(k + 1) * P], gb[w % 2][:, k * P:(k + 1) * P])
                        gT_mm.inc(last)
                    if u >= 2:
                        out_part(u - 2)

                norm_T(1)
                at(h_lo_done, 2)
                for f in range(FT + 2):
                    if f < FT:
                        for side, w in enumerate((w1q, w2q)):
                            if f >= 2:
                                at(hid_done, f - 1)
                            for k in range(KD):
                                for part in (h_hi, h_lo):
                                    last = mm(pb[2 + 2 * side + f % 2][:, :], w[:, k, f * P:(f + 1) * P], part[:, k, :],
                                              start=(k == 0 and part is h_hi), stop=(k == KD - 1 and part is h_lo))
                            up_mm.inc(last)
                    if f >= 2:
                        at(hh_done, f - 1)
                        at(hl_done, f - 1)
                        for t in range(T):
                            for part in (hh, hl):
                                last = mm(pb[down_bank[t]][:, 0:D], part[:, f - 2, t * P:(t + 1) * P], w3q[:, f - 2, :],
                                          start=(f == 2 and part is hh), stop=(f == FT + 1 and part is hl))
                            if f == FT + 1:
                                down_mm.inc(last)

                norm_T(2)
                at(late_loaded, len(row_loads))
                for m in range(4):
                    half, w = m // 2, (wq, wk)[m % 2]
                    for k in range(KD):
                        last = mm(pb[2 + m][:, :], w[:, k, half * P:(half + 1) * P], xnT[:, k, :], start=(k == 0), stop=(k == KD - 1))
                    qk_mm.inc(last)
                for t in range(T):
                    for k in range(KD):
                        last = mm(pb[6 + t // 2][:, (t % 2) * D:(t % 2 + 1) * D], xnT[:, k, t * P:(t + 1) * P], wv[:, k, :],
                                  start=(k == 0), stop=(k == KD - 1))
                    v_mm.inc(last)

                def scores(n):
                    g, t, h0, nh = AUNITS[n]
                    w = (t + 1) * P
                    if n == 0:
                        at(stacked[0], len(QPARTS))
                    if g == 2 * T:
                        at(stacked[1], len(QPARTS))
                    if n >= 2:
                        at(max_done, n - 1)
                    for i in range(nh):
                        out = pb[n % 2][:, i * w:(i + 1) * w]
                        mm(out, qs[0:ROWS, h0 + i, t * P:(t + 1) * P], ks[0:ROWS, h0 + i, 0:w], start=True, stop=False)
                        last = mm(out[:, t * P:w], identb[:, :], maskb[:, :], start=False, stop=True)
                    s_mm.inc(last)

                def maxima_rows(g):
                    at(mp_done, g + 1)
                    if g == 0:
                        at(v_done, 2)
                    else:
                        at(mrow_done, g)
                    for i in range(AQ):
                        last = mm(pb[7][0:MROWS, i * P:(i + 1) * P], mparts[g % 2][:, i, :], identb[:, :], start=True, stop=True)
                    mT_mm.inc(last)

                def transposed_scores(n):
                    g, t, h0, nh = AUNITS[n]
                    w = (t + 1) * P
                    bank = pb[(2, 3, 6)[n % 3]]
                    at(mrow_done, g + 1)
                    if n >= 3:
                        at(exp_done, n - 2)
                    for i in range(nh):
                        for kb in range(t + 1):
                            out = bank[:, i * w + kb * P:i * w + (kb + 1) * P]
                            last = mm(out, ks[0:ROWS, h0 + i, kb * P:(kb + 1) * P], qs[0:ROWS, h0 + i, t * P:(t + 1) * P],
                                      start=True, stop=(kb < t))
                        last = mm(out, identb[:, :], maskTb[:, :], start=False, stop=True)
                    sT_mm.inc(last)

                def weighted_values(n):
                    g, t, h0, nh = AUNITS[n]
                    at(exp_done, n + 1)
                    if g >= 2:
                        at(o_done, g - 1)
                    for i in range(nh):
                        r0 = (h0 + i) % AQ * AV
                        for kb in range(t + 1):
                            last = mm(pb[4 + g % 2][r0:r0 + AV, 0:P], vt[:, kb, h0 + i, :],
                                      pT[n % 3][:, (i * (t + 1) + kb) * P:(i * (t + 1) + kb + 1) * P], start=(kb == 0), stop=(kb == t))
                    pv_mm.inc(last)

                def turn_outputs(p):
                    at(o_done, of_pair_done[p])
                    at(mrow_done, len(AGROUPS))
                    for k in range(KD):
                        for i in range(2):
                            last = transpose(pb[7][:, (2 * k + i) * P:(2 * k + i + 1) * P], yat[:, 2 * p + i, k * P:(k + 1) * P])
                    yT_mm.inc(last)

                def project(p):
                    at(yT_done, p + 1)
                    for i in range(2):
                        t = 2 * p + i
                        for k in range(KD):
                            last = mm(pb[t][:, 0:D], yT[:, k, t * P:(t + 1) * P], wo[:, k, :], start=(k == 0), stop=(k == KD - 1))
                    wo_mm.inc(last)

                def turn(g):
                    at(oT_done, g + 1)
                    o_mm.inc(transpose(pb[4 + g % 2][:, P:2 * P], oT[g % 2]))

                at(part3, 4)
                at(v_ones, 1)
                for step, n in attention_steps:
                    if step == "max":
                        scores(n)
                    elif step == "rows":
                        maxima_rows(n)
                    elif step == "exp":
                        transposed_scores(n)
                    elif step == "values":
                        weighted_values(n)
                    elif step == "turn":
                        turn(n)
                    elif step == "turn outputs":
                        turn_outputs(n)
                    else:
                        project(n)
                norm_T(3)
                for t in range(T):
                    for k in range(KD):
                        last = mm(pb[2][:, t * E:(t + 1) * E], xnT[:, k, t * P:(t + 1) * P], gw[:, k, :],
                                  start=(k == 0), stop=(k == KD - 1))
                lg_mm.inc(last)
                at(late_loaded, len(row_loads))
                for f in range(ST):
                    if f >= 2:
                        at(sr_ready, f - 1)
                    for k in range(KD):
                        last = mm(pb[4 + f % 2][:, :], su[:, k, f * P:(f + 1) * P], xnT[:, k, :], start=(k == 0), stop=(k == KD - 1))
                    su_mm.inc(last)
                at(hs_ready, ST)
                for t in range(T):
                    if t == T // 2:
                        at(cum_ready, 1)
                        for i in range(T):
                            mm(pb[3][:, i * E:(i + 1) * E], before[:, :], sel[:, i, :], start=True, stop=False)
                            last = mm(pb[3][:, i * E:(i + 1) * E], ones[:, :], cum[:, i, :], start=False, stop=True)
                        pos_mm.inc(last)
                    for f in range(ST):
                        last = mm(pb[6 + t // 2][:, (t % 2) * D:(t % 2 + 1) * D], hs[:, f, t * P:(t + 1) * P], sd[:, f, :],
                                  start=(f == 0), stop=(f == ST - 1))
                sd_mm.inc(last)
                norm_T(NEXT)
                stage_end("pe", pe, b)

            def turn_tokens(q, i):
                pe.wait_ge(xd_loaded[i % WB].sem, q * (TRIP // WB * 16) + (i // WB + 1) * 16)
                pe.wait_ge(xdT_ready.sem, pair_count_of(q, i, 2))
                for k in range(KD):
                    last = transpose(pb[i % 2][:, k * P:(k + 1) * P], xd[i % WB][:, k * P:(k + 1) * P])
                xdT_mm.inc(last)

            def hidden(q, i):
                pe.wait_ge(wm_loaded[i % WB].sem, q * (TRIP // WB * 32) + (i // WB + 1) * 32)
                pe.wait_ge(xdT_ready.sem, pair_count_of(q, i))
                pe.wait_ge(hr_ready.sem, pair_count_of(q, i, 2))
                for e in range(2):
                    for k in range(KD):
                        last = mm(pb[2 + i % 2][:, e * CAP:(e + 1) * CAP], w1m[i][:, e, k, :], xdT[i % 2][:, k, e * CAP:(e + 1) * CAP],
                                  start=(k == 0), stop=(k == KD - 1))
                h_mm.inc(last)

            def products(q):
                for i in range(-2, TRIP):
                    if i + 2 < TRIP:
                        turn_tokens(q, i + 2)
                    if 0 <= i + 1 < TRIP:
                        hidden(q, i + 1)
                    if i >= 0:
                        pe.wait_ge(hq_ready.sem, pair_count_of(q, i))
                        pe.wait_ge(ys_ready.sem, pair_count_of(q, i, 2))
                        for e in range(2):
                            last = mm(pb[4 + i % 2][e * CAP:(e + 1) * CAP, 0:D], hq[i % 2][:, e * CAP:(e + 1) * CAP], w2m[i][:, e, :],
                                      start=True, stop=True)
                        y_mm.inc(last)
            trips(pe, products)

        @block.vector
        def _(dve):
            v = nc.vector
            for s in (xdT_ready, hq_ready, target_ready):
                s.free_at_first(dve)
            dve.wait_ge(w_ffn_loaded.sem, 16 * len(ffn_loads))
            dve.wait_ge(w_small_loaded.sem, 32)
            v.memset(cum[:, 0, :], 0.0)
            v.memset(xrow[:, 0, 0:XW - 1], 0.0)
            v.tensor_copy(identb[:, :], ident[:, :])
            v.tensor_copy(maskb[:, :], masks[:, 0:P])
            v.tensor_copy(maskTb[:, :], masks[:, P:2 * P])
            v.tensor_copy(xrow[:, 0, XW - 1:XW], small["empty"])
            dve.wait_ge(pro_pe.sem, 1)
            pro_dve.inc(v.tensor_scalar(thr, pb[7][:, 0:3], 1.0 / (FF * D), 1e-8, ALU.mult, ALU.add))
            dve.wait_ge(pro_dve.sem, 1)
            pro_dve.inc(v.tensor_scalar(nthr, thr, -0.5, None, ALU.mult))
            dve.wait_ge(pro_dve.sem, 2)
            pro_dve.inc(v.tensor_scalar(thr, thr, 0.5, None, ALU.mult))
            b = None

            def at(s, k):
                dve.wait_ge(s.sem, s.upto(k, b))

            def link(ins):
                dstep.inc(ins)
                at(dstep, dstep.count - (dstep.start if b is None else 0))

            def norm(n, make=None):
                for t in range(T + 1):
                    if t < T:
                        if make is not None:
                            make(t)
                        norm_stats(n, t)
                    if t >= 1:
                        norm_apply(n, t - 1)

            def norm_stats(n, t):
                link(v.bn_stats(stats[:, t, :], norm_in(n)[:, t, :]))
                settle(dve)
                ln_stats.inc(v.bn_aggr(mv[:, t, :], stats[:, t, :]))

            def norm_apply(n, t):
                at(ln_rstd, tile_count(n, t))
                ln_xn.inc(v.tensor_scalar(norm_out(n)[:, t, 0:D], norm_in(n)[:, t, :], mv[:, t, 0:1], rstd[:, t:t + 1], ALU.subtract, ALU.mult))

            at(xnext_loaded, 0)
            norm(0)
            for s in signals.values():
                s.new_trip()

            with dve.Fori(0, B) as b:

                def heads(x, c, n=GH, width=HP):
                    return x.unsqueeze(2).to_broadcast([P, n, width])

                at(dt_mm, 1)
                link(v.tensor_tensor(v_dt[:, :, :], pb[7][:, 0:T * H].rearrange("p (t h) -> p t h", t=T),
                                     dtb[:, :].unsqueeze(1).to_broadcast([P, T, H]), ALU.add))
                dt_abs.inc(v.scalar_tensor_tensor(out=u_dt[:, :, :], in0=v_dt[:, :, :], scalar=-1.0, in1=v_dt[:, :, :],
                                                  op0=ALU.mult, op1=ALU.max))
                at(dt_log, 2)
                link(v.scalar_tensor_tensor(out=dt_[:, :, :], in0=v_dt[:, :, :], scalar=0.0, in1=l_dt[:, :, :], op0=ALU.max, op1=ALU.add))
                a_ready.inc(v.scalar_tensor_tensor(out=a_[:, :, :], in0=dt_[:, :, :], scalar=-1.0,
                                                   in1=expA[:, :].unsqueeze(1).to_broadcast([P, T, H]), op0=ALU.mult, op1=ALU.mult))
                for j in range(CT):
                    ci = (CT - 2 + j) if j < 2 else j - 2
                    at(tap3, j + 1)
                    cv, bank = conv[j % 2], pb[j % 2]
                    for s in (1, 2, 3):
                        ins = v.scalar_tensor_tensor(out=cv[:, s:L], in0=bank[:, 0:L - s], scalar=convw[:, ci, TAPS - 1 - s:TAPS - s],
                                                     in1=cv[:, s:L], op0=ALU.mult, op1=ALU.add)
                        if s < 3:
                            link(ins)
                        else:
                            conv_done.inc(ins)

                at(gate_done, T * G)
                at(x_loaded, 1)

                def decay_products(u):
                    c, g = u // G, u % G
                    if g == 0:
                        at(cb_mm, c + 1)
                        if u >= 1:
                            at(M_ready, u)
                        cbm_ready.inc(v.tensor_tensor(cbm[:, :], pb[7][:, 0:P], upto_[:, :], ALU.mult))
                        at(cbm_ready, c + 1)
                    at(L_ready, 2 * u + 2)
                    M_ready.inc(v.tensor_tensor(Lx[u % 2], Lx[u % 2], cbm[:, :].unsqueeze(1).to_broadcast([P, GH, P]), ALU.mult))

                decay_products(0)
                for u in range(UNITS + 3):
                    c, g = u // G, u % G
                    w = u - 2
                    if w >= 0 and w % G == G - 1:
                        at(g_sq, w + 1)
                        ms_ready.inc(v.tensor_reduce(ms[:, w // G:w // G + 1], ssq[:, w // G, :], AX.X, ALU.add))
                    if u + 1 < UNITS:
                        decay_products(u + 1)
                    if u < UNITS:
                        hs_ = slice(c * H + g * GH, c * H + (g + 1) * GH)
                        at(yd_mm, u + 1)
                        at(xD_ready, u + 1)
                        if u >= 1:
                            at(g_ready, u)
                        yd_read.inc(v.tensor_tensor(yb, pb[2][:, :], xD[u % 2], ALU.add))
                        if c > 0:
                            at(yo_mm, u - G + 1)
                            yo_read.inc(v.tensor_tensor(yo[:, :].rearrange("p (h w) -> p h w", h=GH), pb[3][:, :].rearrange("p (h w) -> p h w", h=GH),
                                                        heads(dec[:, 0, hs_], c), ALU.mult))
                        if c < T - 1:
                            at(ds_mm, u + 1)
                            if c == 0:
                                S_ready.inc(v.tensor_copy(S[:, g * GF:(g + 1) * GF], pb[4][:, :]))
                            else:
                                at(sx_ready, u - G + 1)
                                S_ready.inc(v.tensor_tensor(S[:, g * GF:(g + 1) * GF], pb[4][:, :], sx[u % 2], ALU.add))
                        at(yd_read, u + 1)
                        if c > 0:
                            at(yo_read, u - G + 1)
                            link(v.tensor_tensor(yb[:, :], yb[:, :], yo[:, :], ALU.add))
                        if u >= 2:
                            at(gT_mm, u - 1)
                            at(g_sq, u - 1)
                        g_ready.inc(v.tensor_tensor(gb[u % 2][:, :], yb[:, :], sz[:, c, g * GF:(g + 1) * GF], ALU.mult))
                    if w >= 0 and w % G == G - 1:
                        t = w // G
                        at(out_mm, w + 1)
                        at(rms_rstd, t + 1)
                        po_read.inc(v.scalar_tensor_tensor(out=xb[:, t, :], in0=pb[6][:, 0:D], scalar=rms[:, t:t + 1], in1=xb[:, t, :],
                                                           op0=ALU.mult, op1=ALU.add))
                        at(po_read, t + 1)
                        norm_stats(1, t)
                    if w >= 1 and w % G == 0:
                        norm_apply(1, w // G - 1)

                for i in range(2):
                    at(ln_done, pair_count(1, i))
                    cols = slice(i * 2 * P, (i + 1) * 2 * P)
                    h_lo_done.inc(v.tensor_tensor(h_lo[:, :, cols], pb[i][:, :].rearrange("p (k n) -> p k n", k=KD), h_hi[:, :, cols], ALU.subtract))
                for f in range(FT):
                    at(up_mm, 2 * f + 2)
                    at(sig_done, f + 1)
                    if f >= 2:
                        at(hh_done, f - 1)
                        at(hl_done, f - 1)
                    hid_done.inc(v.tensor_tensor(hid[f % 2], pb[4 + f % 2][:, :], sg[f % 2], ALU.mult))
                    at(hh_done, f + 1)
                    hl_done.inc(v.tensor_tensor(hl[:, f, :], hid[f % 2], hh[:, f, :], ALU.subtract))

                def add_ffn(t):
                    at(down_mm, t + 1)
                    link(v.tensor_tensor(xb[:, t, :], pb[down_bank[t]][:, 0:D], xb[:, t, :], ALU.add))

                norm(2, add_ffn)
                at(late_loaded, len(row_loads))
                for m in range(5):
                    if m < 4:
                        at(part1, m + 1)
                        if m >= 2:
                            at(part3, m - 1)
                        qk_rest.inc(v.scalar_tensor_tensor(out=rest[m % 2], in0=pb[2 + m][:, :], scalar=1.0 if m % 2 else AD ** -0.5,
                                                           in1=parts[m // 2][:, m % 2 * 3, :], op0=ALU.mult, op1=ALU.subtract))
                    if m >= 1:
                        at(part2, m)
                        i = (m - 1) % 2 * 3
                        part3.inc(v.tensor_tensor(parts[(m - 1) // 2][:, i + 2, :], rest[(m - 1) % 2], parts[(m - 1) // 2][:, i + 1, :],
                                                  ALU.subtract))

                def values_norm(g):
                    t, q = AGROUPS[g]
                    at(o_mm, g + 1)
                    sums = pb[4 + g % 2][:, P:2 * P].rearrange("p (h w) -> p h w", h=AQ)
                    if g >= 1:
                        at(o_done, g)
                    link(v.reciprocal(rsums[:, :], sums[:, :, AD]))
                    o_done.inc(v.tensor_tensor(yat[:, t, q * AQ * AD:(q + 1) * AQ * AD].rearrange("p (h w) -> p h w", h=AQ),
                                               sums[:, :, 0:AD], heads(rsums[:, :], t, AQ, AD), ALU.mult))

                for step, n in attention_steps:
                    if step == "max":
                        _, t, h0, nh = AUNITS[n]
                        w = (t + 1) * P
                        at(s_mm, n + 1)
                        src = pb[n % 2][:, 0:nh * w].rearrange("p (h k) -> p h k", h=nh)
                        max_done.inc(v.tensor_reduce(nmax[:, t * AH + h0:t * AH + h0 + nh], src, AX.X, ALU.max, negate=True))
                    elif step == "turn":
                        values_norm(n)
                def add_attention(t):
                    at(wo_mm, t // 2 + 1)
                    link(v.tensor_tensor(xb[:, t, :], pb[t][:, 0:D], xb[:, t, :], ALU.add))

                dve.wait_ge(scattered.sem, scattered.upto(0, b))
                for half in added:
                    dve.wait_ge(half.sem, 16)
                norm(3, add_attention)
                at(xnext_loaded, 1)
                norm(NEXT)
                at(sc_ready, 1)
                link(v.tensor_tensor(sbi, sc, ebias[:, :].unsqueeze(1).to_broadcast([P, T, E]), ALU.add))
                settle(dve)
                for t in range(T):
                    for g in range(NG):
                        last = v.max(m8[:, t, g, :], sbi[:, t, g * EG:(g + 1) * EG])
                link(last)
                link(v.tensor_tensor(grp, m8[:, :, :, 0], m8[:, :, :, 1], ALU.add))
                settle(dve)
                for t in range(T):
                    last = v.max(gm8[:, t, :], grp[:, t, :])
                link(last)
                settle(dve)
                for t in range(T):
                    last = v.max_index(gi[:, t, :], gm8[:, t, :], grp[:, t, :])
                link(last)
                link(v.tensor_copy(gif, gi))
                link(v.tensor_tensor(goh, iota8[:, :].unsqueeze(1).unsqueeze(3).to_broadcast([P, T, NG, TKG]),
                                     gif[:, :, 0:TKG].unsqueeze(2).to_broadcast([P, T, NG, TKG]), ALU.is_equal))
                link(v.tensor_reduce(gmask.rearrange("p (t g) -> p t g", t=T), goh, AX.X, ALU.add))
                link(v.tensor_scalar(gmask, gmask, BIG, -BIG, ALU.mult, ALU.add))
                link(v.tensor_tensor(masked.rearrange("p (n e) -> p n e", e=EG), sbi.rearrange("p t (g e) -> p (t g) e", e=EG),
                                     gmask.unsqueeze(2).to_broadcast([P, T * NG, EG]), ALU.add))
                mk = masked.rearrange("p (t e) -> p t e", t=T)
                settle(dve)
                for t in range(T):
                    last = v.max(em8[:, t, :], mk[:, t, :])
                link(last)
                settle(dve)
                for t in range(T):
                    last = v.max_index(ei[:, t, :], em8[:, t, :], mk[:, t, :])
                link(last)
                link(v.tensor_copy(eif, ei))
                link(v.tensor_tensor(eoh, iota64[:, :].unsqueeze(1).unsqueeze(3).to_broadcast([P, T, E, TOPK]),
                                     eif[:, :, 0:TOPK].unsqueeze(2).to_broadcast([P, T, E, TOPK]), ALU.is_equal))
                sel_ready.inc(v.tensor_reduce(sel, eoh, AX.X, ALU.add))
                at(sel_ready, 1)
                for t in range(T):
                    ins = v.tensor_tensor(cum[:, t + 1, :], cum[:, t, :], sel[:, t, :], ALU.add)
                    if t < T - 1:
                        link(ins)
                    else:
                        cum_ready.inc(ins)
                link(v.tensor_tensor(wsel, sc, sel, ALU.mult))
                link(v.tensor_reduce(wsum, wsel, AX.X, ALU.add))
                link(v.tensor_scalar(wsum, wsum, 1e-20, None, ALU.add))
                link(v.reciprocal(wrec, wsum))
                v.tensor_copy(xrow[:, :, XW - 1], tokid[:, bass.ds(b * T, T)])
                for t in range(T):
                    last = v.tensor_scalar(wsel[:, t, :], wsel[:, t, :], wrec[:, t:t + 1], SCALE, ALU.mult, ALU.mult)
                w_ready.inc(last)
                at(pos_mm, 1)
                ppos = pb[3][:, 0:T * E]
                link(v.scalar_tensor_tensor(out=kept, in0=ppos, scalar=float(CAP), in1=sel.rearrange("p t e -> p (t e)"),
                                            op0=ALU.is_lt, op1=ALU.mult))
                link(v.tensor_tensor(sid.rearrange("p (t e) -> p t e", t=T), ppos.rearrange("p (t e) -> p t e", t=T),
                                     slot0[:, :].unsqueeze(1).to_broadcast([P, T, E]), ALU.add))
                link(v.tensor_tensor(sid, sid, kept, ALU.mult))
                settle(dve)
                for t in range(T):
                    last = v.max(s8[:, t, :], sid[:, t * E:(t + 1) * E])
                link(last)
                s8_ = s8.rearrange("p t k -> p (t k)")
                link(v.scalar_tensor_tensor(out=nos, in0=s8_, scalar=0.0, in1=noslot[:, :], op0=ALU.is_equal, op1=ALU.mult))
                slots_ready.inc(v.tensor_tensor(slots[:, :, :].rearrange("p t k -> p (t k)"), s8_, nos, ALU.add))
                v.tensor_copy(cum[:, 0, :], cum[:, T, :])
                at(sd_mm, 1)
                for q in range(2):
                    last = v.tensor_tensor(xb[:, 2 * q:2 * q + 2, :], pb[6 + q][:, :].rearrange("p (t n) -> p t n", t=2),
                                           xb[:, 2 * q:2 * q + 2, :], ALU.add)
                out_ready.inc(last)
                stage_end("dve", dve, b)
                settle(dve)
                rows_done.inc(dve.drain())

            def take_tokens(q, i):
                dve.wait_ge(xdT_mm.sem, pair_count_of(q, i))
                dve.wait_ge(h_mm.sem, pair_count_of(q, i, 2))
                xdT_ready.inc(v.tensor_copy(xdT[i % 2].rearrange("p k s -> p (k s)"), pb[i % 2][:, 0:KD * P]))

            def square(q, i):
                dve.wait_ge(hr_ready.sem, pair_count_of(q, i))
                dve.wait_ge(y_mm.sem, pair_count_of(q, i, 2))
                hq_ready.inc(v.tensor_tensor(hq[i % 2], hr[i % 2], hr[i % 2], ALU.mult))

            def targets(q, i):
                dve.wait_ge(xd_loaded[i % WB].sem, q * (TRIP // WB * 16) + (i // WB + 1) * 16)
                dve.wait_ge(added[i % 2].sem, added_count(q, i, WB))
                target_ready.inc(v.tensor_tensor(target[i % WB][:, :], xd[i % WB][:, XW - 1:XW], sum0[:, i % 2:i % 2 + 1], ALU.add))

            def ahead(q):
                for i in range(-2, TRIP):
                    if i + 2 < TRIP:
                        take_tokens(q, i + 2)
                    if 0 <= i + 1 < TRIP:
                        square(q, i + 1)
                    if i >= 0:
                        targets(q, i)
            trips(dve, ahead)
            for g in range(BLOCKS):
                s0, s1, s2, s3 = part_sum[g]
                dve.wait_ge(sums_loaded[g][0].sem, 32)
                pair_sum.inc(v.tensor_tensor(s0, s0, s1, ALU.add))
                dve.wait_ge(sums_loaded[g][1].sem, 32)
                pair_sum.inc(v.tensor_tensor(s2, s2, s3, ALU.add))
                dve.wait_ge(pair_sum.sem, 2 * g + 2)
                final_sum.inc(v.tensor_tensor(s0, s0, s2, ALU.add))

        @block.gpsimd
        def _(pool):
            p = nc.gpsimd
            pool.wait_ge(pro_dve.sem, 3)
            b = None

            def at(s, k):
                pool.wait_ge(s.sem, s.upto(k, b))

            def power_half(out, in_, scale, t, done):
                settle(pool)
                pstep.inc(p.tensor_scalar(vare[:, t:t + 1], in_, scale, EPS, ALU.mult, ALU.add))
                at(pstep, pstep.count - (pstep.start if b is None else 0))
                settle(pool)
                done.inc(p.tensor_tensor(out, vare[:, t:t + 1], power[:, 0:1], ALU.pow))
                at(done, done.count - (done.start if b is None else 0))

            def norm_rstd(n, tiles=range(T)):
                for t in tiles:
                    at(ln_stats, tile_count(n, t))
                    power_half(rstd[:, t:t + 1], mv[:, t, 1:2], 1.0, t, ln_rstd)

            p.memset(power[:, :], -0.5)
            norm_rstd(0)
            k = 0
            for i in range(3):
                p.tensor_scalar(low, wf[i], nthr[:, i:i + 1], None, ALU.is_lt)
                pro_pool.inc(p.tensor_scalar(wf[i], wf[i], thr[:, i:i + 1], None, ALU.is_gt))
                k += 1
                pool.wait_ge(pro_pool.sem, k)
                pro_pool.inc(p.tensor_tensor(wt[i], wf[i], low, ALU.subtract))
                k += 1
                pool.wait_ge(pro_pool.sem, k)
            rows = SUMS * (NTOK + CAP) - NTOK
            pool.wait_ge(x_loaded.sem, 16)
            scattered.inc(pool.dma_start(xslot[1:1 + E * CAP, :].rearrange("(k p) w -> p k w", p=P),
                                         xrow[:, 0:1, :].to_broadcast([P, E * CAP // P, XW])))
            for half in range(2):
                r0 = NTOK + half * rows // 2
                added[half].inc(pool.dma_start(acc[r0:r0 + rows // 2, :].rearrange("(k p) w -> p k w", p=P),
                                               xrow[:, 0:1, 0:D].to_broadcast([P, rows // 2 // P, D])))
            pool.wait_ge(w_out_loaded.sem, 16)
            for kk in range(INTER // P):
                p.tensor_scalar(wout[:, kk, :], wout[:, kk, :], normw[:, kk:kk + 1], None, ALU.mult)

            for s in signals.values():
                s.new_trip()

            with pool.Fori(0, B) as b:
                def heads(x):
                    return x.unsqueeze(2).to_broadcast([P, GH, HP])

                def by_head(x):
                    return x.rearrange("p (h w) -> p h w", h=GH)

                at(xtok_done, CT - 1)
                at(a_ready, 1)
                at(dec_ready, 1)
                for u in range(UNITS + 3):
                    w = u - 2
                    if w >= 0 and w % G == 0 and w >= G:
                        norm_rstd(1, [w // G - 1])
                    if u >= UNITS:
                        if w % G == G - 1:
                            at(ms_ready, w // G + 1)
                            power_half(rms[:, w // G:w // G + 1], ms[:, w // G:w // G + 1], 1.0 / INTER, w // G, rms_rstd)
                        continue
                    c, g = u // G, u % G
                    hs_ = slice(g * GH, (g + 1) * GH)
                    dh = slice(c * H + g * GH, c * H + (g + 1) * GH)
                    xs = by_head(xtok[:, c, g * GF:(g + 1) * GF])
                    if u >= 2:
                        at(yd_mm, u - 1)
                        at(xde_ready, min(u - 1, (T - 1) * G))
                    xdt_ready.inc(p.tensor_tensor(by_head(xdt[u % 2]), xs, heads(dt_[:, c, hs_]), ALU.mult))
                    if c < T - 1:
                        at(xdt_ready, u + 1)
                        if u >= 2:
                            at(ds_mm, u - 1)
                        xde_ready.inc(p.tensor_tensor(by_head(xde[u % 2]), by_head(xdt[u % 2]), heads(dec[:, 1, dh]), ALU.mult))
                    if u >= 2:
                        at(yd_read, u - 1)
                    xD_ready.inc(p.tensor_tensor(by_head(xD[u % 2]), xs, heads(dpar[:, hs_]), ALU.mult))
                    if 0 < c < T - 1:
                        at(S_ready, max(u - 4, u - 2) + 1)
                        sx_ready.inc(p.tensor_tensor(by_head(sx[u % 2]), by_head(S[:, g * GF:(g + 1) * GF]), heads(dec[:, 2, dh]), ALU.mult))
                    if w >= 0 and w % G == G - 1:
                        at(ms_ready, w // G + 1)
                        power_half(rms[:, w // G:w // G + 1], ms[:, w // G:w // G + 1], 1.0 / INTER, w // G, rms_rstd)
                norm_rstd(2)
                settle(pool)
                v_ones.inc(p.memset(vt[:, :, :, AD:AV], 1.0))
                for g, (t, q) in enumerate(AGROUPS):
                    m = nmax[:, t * AH + q * AQ:t * AH + (q + 1) * AQ]
                    mp = mparts[g % 2]
                    at(max_done, of_group[g][-1] + 1)
                    if g >= 2:
                        at(mT_mm, g - 1)
                    for part, src in enumerate((m, mrest[:, :])):
                        settle(pool)
                        pstep.inc(p.tensor_copy(mp[:, :, part], src))
                        at(pstep, pstep.count)
                        ins = p.tensor_tensor(mrest[:, :] if part == 0 else mp[:, :, 2], src, mp[:, :, part], ALU.subtract)
                        if part == 0:
                            pstep.inc(ins)
                            at(pstep, pstep.count)
                        else:
                            mp_done.inc(ins)
                            at(mp_done, g + 1)
                norm_rstd(3)
                norm_rstd(NEXT)
                n_stage["pool"] += 1
                settle(pool)
                stage["pool"].inc(pool.drain())
                at(slots_ready, 1)
                at(w_ready, 1)
                at(scattered, 0)
                settle(pool)
                for t in range(T):
                    for k in range(TOPK):
                        scattered.inc(p.indirect_dma_start(xslot, bass.IndirectOffsetOnAxis(ap=slots[:, t, k:k + 1], axis=0),
                                                           xrow[:, t, :], None))
                for other in stage:
                    if other != "pool":
                        pool.wait_ge(stage[other].sem, stage[other].upto(1, b))

            def add_outputs(q):
                for i in range(TRIP):
                    pool.wait_ge(target_ready.sem, pair_count_of(q, i))
                    pool.wait_ge(ys_ready.sem, pair_count_of(q, i))
                    pool.wait_ge(added[i % 2].sem, added_count(q, i, 2))
                    settle(pool)
                    added[i % 2].inc(p.indirect_dma_start(acc, bass.IndirectOffsetOnAxis(ap=target[i % WB][:, :], axis=0), ys[i % WB], None,
                                                          compute_op=ALU.add))
            pool.wait_ge(stored.sem, stored.upto(B))
            for half in added:
                pool.wait_ge(half.sem, 16)
            trips(pool, add_outputs)
        return {n: s.most for n, s in signals.items()}


def constants():
    r = np.arange(P)
    upto = (r[:, None] <= r[None, :]).astype(np.float32)
    q, k = np.arange(L, dtype=np.float32), np.arange(L, dtype=np.float32)
    slopes = (2.0 ** (-8.0 / np.arange(1, AH + 1, dtype=np.float32))).astype(np.float32)

    def parts(v):
        out = []
        for _ in range(3):
            bits = np.ascontiguousarray(v).view(np.uint32)
            out.append(((bits + 0x7FFF + (bits >> 16 & 1)) & 0xFFFF0000).astype(np.uint32).view(np.float32))
            v = v - out[-1]
        return out

    qrows, krows = np.zeros((BROWS, AH, L), np.float32), np.ones((BROWS, AH, L), np.float32)
    for i, (at_q, slope) in enumerate(zip(parts(-slopes[:, None] * q[None, :]), parts(slopes))):
        qrows[MROWS + i] = at_q
        qrows[MROWS + 3 + i] = qrows[MROWS + 6 + i] = slope[:, None]
    krows[MROWS + 3:MROWS + 6] = k - k % 256
    krows[MROWS + 6:MROWS + 9] = k % 256
    rows = (np.stack([qrows, krows], 2).reshape(BROWS, -1).view(np.uint32) >> 16).astype(np.uint16)
    mask = np.where(r[None, :] > r[:, None], -BIG, 0.0).astype(np.float32)
    rep = lambda v: np.ascontiguousarray(np.broadcast_to(np.asarray(v, np.float32), (P, len(v))))
    c = dict(ident=np.eye(P, dtype=np.float32), upto=upto, after=np.ascontiguousarray(1 - upto),
             before=(upto - np.eye(P, dtype=np.float32)), ones=np.ones((P, P), np.float32),
             rows=rows.view(np.float32),
             iota8=rep(np.arange(NG)), iota64=rep(np.arange(E)), slot0=rep(1 + CAP * np.arange(E)),
             eps=np.full((P, 1), EPS, np.float32),
             tokid=np.arange(NTOK, dtype=np.float32).reshape(-1, P).T.copy(),
             noslot=(1 + E * CAP + (r[:, None, None] + P * (TOPK * np.arange(T)[None, :, None] + np.arange(8)[None, None, :]))
                        ).reshape(P, -1).astype(np.float32),
             empty=(NTOK + r[:, None] % CAP).astype(np.float32),
             sum0=((r[:, None] // CAP + 2 * np.arange(2)[None, :]) * (NTOK + CAP)).astype(np.float32))
    return dict(rows=c["rows"], masks=np.concatenate([mask, mask.T], 1), consts=np.concatenate([c[n] for n in CONSTS], 1))


def layouts(i):
    def tiles(w):
        return np.ascontiguousarray(w.reshape(-1, P, w.shape[1]).transpose(1, 0, 2))

    def by_place(w):
        return np.ascontiguousarray(w.reshape(D, 2, AH // 2, AD).transpose(0, 1, 3, 2)).reshape(D, D)

    def padded(w, rows, cols):
        out = np.zeros((rows, cols), np.float32)
        out[:w.shape[0], :w.shape[1]] = w
        return out

    def rep(v):
        return np.ascontiguousarray(np.broadcast_to(v, (P, len(v))))

    flat = lambda w: np.ascontiguousarray(w.reshape(P, -1))
    wqkv = i["L1_attn_W_qkv"]
    out = dict(
        x=np.ascontiguousarray(i["L0_attn_hidden_states"]), win=tiles(i["L0_attn_W_in"].T),
        convw=np.ascontiguousarray(i["L0_attn_conv_w"].reshape(CT, P, TAPS).transpose(1, 0, 2)),
        convb=np.ascontiguousarray(i["L0_attn_conv_b"].reshape(CT, P).T),
        dtb=rep(i["L0_attn_dt_bias"]), alog=rep(i["L0_attn_A_log"]), dpar=rep(i["L0_attn_D_param"]),
        normw=np.ascontiguousarray(i["L0_attn_norm_w"].reshape(-1, P).T), wout=tiles(i["L0_attn_W_out"].T),
        w1=flat(tiles(padded(i["L0_ffn_w1"].T, D, FT * P))), w2=flat(tiles(padded(i["L0_ffn_w2"].T, D, FT * P))),
        w3=flat(tiles(padded(i["L0_ffn_w3"].T, FT * P, D))),
        wq=tiles(by_place(wqkv[:, 0:D])), wk=tiles(by_place(wqkv[:, D:2 * D])), wv=tiles(wqkv[:, 2 * D:]), wo=tiles(i["L1_attn_W_o"]),
        gw=tiles(i["L1_ffn_gate_w"].T), ebias=rep(i["L1_ffn_e_bias"]),
        su=tiles(i["L1_ffn_shared_up_w"].T), sd=tiles(i["L1_ffn_shared_down_w"].T),
        w1m=np.ascontiguousarray(i["L1_ffn_w1"].reshape(E, P, KD, P).transpose(0, 3, 2, 1)),
        w2m=np.ascontiguousarray(i["L1_ffn_w2"].transpose(0, 2, 1)))
    out["params"] = np.concatenate([out.pop(n).reshape(P, -1) for n in PARAMS], 1)
    return out


def kernel(**inputs):
    from concourse import bacc
    from concourse.bass_utils import run_bass_kernel_spmd

    arrays = {**layouts({k: np.asarray(v) for k, v in inputs.items()}), **constants()}

    def program(per_trip):
        nc = bacc.Bacc("TRN2", target_bir_lowering=False, num_devices=1)
        aps = {n: nc.dram_tensor(f"in_{n}", x.shape, F32, kind="ExternalInput").ap() for n, x in arrays.items()}
        aps["out"] = nc.dram_tensor("out", (B, L, D), F32, kind="ExternalOutput").ap()
        return nc, build(nc, aps, per_trip)

    _, counts = program({})
    nc, again = program(counts)
    assert counts == again
    r = run_bass_kernel_spmd(nc, [{f"in_{n}": x for n, x in arrays.items()}], core_ids=[0])
    return r.results[0]["out"]
```
